# Optimizing a Trainium2 kernel written in Bass

```python
import numpy as np
import jax
import jax.numpy as jnp

def _softmax(x, axis=-1):
    return jax.nn.softmax(x, axis=axis)

def _gelu(x):
    return jax.nn.gelu(x, approximate=True)

def _silu(x):
    return jax.nn.silu(x)

def _sigmoid(x):
    return jax.nn.sigmoid(x)

def _layernorm(x, axis=-1, eps=1e-05):
    m = jnp.mean(x, axis=axis, keepdims=True)
    v = jnp.var(x, axis=axis, keepdims=True)
    return (x - m) / jnp.sqrt(v + eps)

def _scatter_add(tgt, idx, src, axis=0):
    return tgt.at[idx].add(src)

def _segment_sum(src, seg, n):
    return jax.ops.segment_sum(src, seg, n)
kernel_name = 'mk_decoder_preln_d2_seqx_r8_004d6b'

def setup_inputs(seed: int=0):
    np.random.seed(seed)
    _w = jnp.asarray

    def _rec_inputs():
        import jax
        import jax.numpy as jnp
        _rk = jax.random.key(seed)
        x = -0.0002928 + 1 * jax.random.normal(jax.random.fold_in(_rk, 1), (8, 128, 512), jnp.float32)
        _lenS = 128 - jax.random.randint(jax.random.fold_in(_rk, 7), (8,), 0, max(1, 128 // 4) + 1, jnp.int32)
        _lenS2 = 128 - jax.random.randint(jax.random.fold_in(_rk, 8), (8,), 0, max(1, 128 // 4) + 1, jnp.int32)
        _ctx_4096P = jax.random.normal(jax.random.fold_in(_rk, 11), (8, 16, 512), jnp.float32)
        _ctx_4096c = jax.random.dirichlet(jax.random.fold_in(_rk, 511), 0.3 * jnp.ones((16,), jnp.float32), (8, 128))
        _ctx_4096t = jnp.einsum('bsk,bkd->bsd', _ctx_4096c, _ctx_4096P)
        _ctx_4096t = _ctx_4096t * jax.lax.rsqrt(jnp.mean(jnp.square(_ctx_4096t)) + 1e-12) * 0.953939
        ctx_4096 = -2.8382e-05 + 0.999851 * (_ctx_4096t + 0.3 * jax.random.normal(jax.random.fold_in(_rk, 611), (8, 128, 512), jnp.float32))
        _validS = jnp.arange(128)[None, :] < _lenS[:, None]
        _validS2 = jnp.arange(128)[None, :] < _lenS2[:, None]
        _causal = jnp.tril(jnp.ones((128, 128), dtype=bool))
        mask_1x1xSxS2_ff0 = jnp.where(jnp.ones((1, 1, 128, 128), dtype=bool), 0.0, -1000000000.0).astype(jnp.float32)
        return (x, ctx_4096, mask_1x1xSxS2_ff0)
    x, ctx_4096, mask_1x1xSxS2_ff0 = _rec_inputs()

    def _L0_attn_setup():
        import jax, jax.numpy as jnp
        import numpy as np
        D_MODEL = 512
        N_HEADS = 32
        HEAD_DIM = D_MODEL // N_HEADS
        CLIP_QKV = 8.0
        ALIBI_BIAS_MAX = 8.0
        LN_EPS = 1e-05

        def _alibi_slopes(n_heads: int, bias_max: float) -> jnp.ndarray:
            next_pow2 = 2 ** int(np.ceil(np.log2(n_heads)))
            m = np.arange(1, next_pow2 + 1, dtype=np.float32) * (bias_max / next_pow2)
            slopes = 1.0 / np.power(2.0, m)
            if next_pow2 != n_heads:
                slopes = np.concatenate([slopes[1::2], slopes[::2]])[:n_heads]
            return jnp.asarray(slopes)

        def _layer_norm(x, w, b):
            mu = jnp.mean(x, axis=-1, keepdims=True)
            var = jnp.mean(jnp.square(x - mu), axis=-1, keepdims=True)
            return (x - mu) * jax.lax.rsqrt(var + LN_EPS) * w + b
        key = jax.random.key(seed)
        ks = jax.random.split(key, 3)
        B, S = (1, 256)
        hidden_states = jax.random.normal(ks[0], (B, S, D_MODEL), dtype=jnp.float32)
        Wqkv = jax.random.normal(ks[1], (3 * D_MODEL, D_MODEL), dtype=jnp.float32) * 0.02
        Wout = jax.random.normal(ks[2], (D_MODEL, D_MODEL), dtype=jnp.float32) * 0.02
        return {'hidden_states': hidden_states, 'Wqkv': Wqkv, 'q_ln_w': jnp.ones((D_MODEL,), jnp.float32), 'q_ln_b': jnp.zeros((D_MODEL,), jnp.float32), 'k_ln_w': jnp.ones((D_MODEL,), jnp.float32), 'k_ln_b': jnp.zeros((D_MODEL,), jnp.float32), 'Wout': Wout}
    _L0_attn_all = _L0_attn_setup()
    _L0_attn_in = {k: v for k, v in _L0_attn_all.items() if k in ('Wqkv', 'q_ln_w', 'q_ln_b', 'k_ln_w', 'k_ln_b', 'Wout')}
    del _L0_attn_all

    def _L0_xattn_setup():
        import jax, jax.numpy as jnp
        import numpy as np
        NUM_HEADS = 32
        NUM_KV_HEADS = 8
        HEAD_DIM = 128
        HIDDEN = 512
        EPS = 1e-05

        def rmsnorm(x, w, eps=EPS):
            xf = x.astype(jnp.float32)
            var = jnp.mean(xf * xf, axis=-1, keepdims=True)
            return w * (xf * jax.lax.rsqrt(var + eps)).astype(x.dtype)
        key = jax.random.key(seed)
        ks = jax.random.split(key, 10)
        B, Q, KV = (1, 128, 6404)
        s = 1.0 / np.sqrt(HIDDEN)
        return {'hidden_states': jax.random.normal(ks[0], (B, Q, HIDDEN), jnp.float32), 'cross_attention_states': jax.random.normal(ks[1], (B, KV, HIDDEN), jnp.float32), 'attention_mask': jnp.zeros((B, 1, Q, KV), jnp.float32), 'q_proj_w': jax.random.normal(ks[2], (NUM_HEADS * HEAD_DIM, HIDDEN), jnp.float32) * s, 'k_proj_w': jax.random.normal(ks[3], (NUM_KV_HEADS * HEAD_DIM, HIDDEN), jnp.float32) * s, 'v_proj_w': jax.random.normal(ks[4], (NUM_KV_HEADS * HEAD_DIM, HIDDEN), jnp.float32) * s, 'o_proj_w': jax.random.normal(ks[5], (HIDDEN, NUM_HEADS * HEAD_DIM), jnp.float32) * s, 'q_norm_w': jnp.ones((HEAD_DIM,), jnp.float32), 'k_norm_w': jnp.ones((HEAD_DIM,), jnp.float32)}
    _L0_xattn_all = _L0_xattn_setup()
    _L0_xattn_in = {k: v for k, v in _L0_xattn_all.items() if k in ('q_proj_w', 'k_proj_w', 'v_proj_w', 'o_proj_w', 'q_norm_w', 'k_norm_w')}
    del _L0_xattn_all

    def _L0_ffn_setup():
        import jax, jax.numpy as jnp
        import numpy as np
        B, S, D, O, E, R = (4, 256, 512, 512, 8, 16)
        SCALING = 32.0 / 16.0
        MAX_THRESHOLD = 0.125
        key = jax.random.key(seed)
        ks = jax.random.split(key, 8)
        return {'x': jax.random.normal(ks[0], (B, S, D), jnp.float32), 'W_base': jax.random.normal(ks[1], (O, D), jnp.float32) * (1.0 / np.sqrt(D)), 'b_base': jax.random.normal(ks[2], (O,), jnp.float32) * 0.02, 'W_gate': jax.random.normal(ks[3], (E, D), jnp.float32) * (1.0 / np.sqrt(D)), 'W_thr': jax.random.normal(ks[4], (D,), jnp.float32) * (1.0 / np.sqrt(D)), 'b_thr': jax.random.normal(ks[5], (1,), jnp.float32) * 0.02, 'A_w': jax.random.normal(ks[6], (E, R, D), jnp.float32) * (1.0 / np.sqrt(D)), 'B_w': jax.random.normal(ks[7], (E, O, R), jnp.float32) * (1.0 / np.sqrt(R))}
    _L0_ffn_all = _L0_ffn_setup()
    _L0_ffn_in = {k: v for k, v in _L0_ffn_all.items() if k in ('W_base', 'b_base', 'W_gate', 'W_thr', 'b_thr', 'A_w', 'B_w')}
    del _L0_ffn_all

    def _L1_attn_setup():
        import jax, jax.numpy as jnp
        import numpy as np
        import math
        HIDDEN = 512
        N_HEADS = 32
        N_KV_HEADS = 8
        HEAD_DIM = HIDDEN // N_HEADS
        N_REP = N_HEADS // N_KV_HEADS
        B, S = (1, 256)
        key = jax.random.key(seed)
        k0, k1, k2, k3, k4 = jax.random.split(key, 5)
        scale = 0.02
        return {'hidden_states': jax.random.normal(k0, (B, S, HIDDEN), dtype=jnp.float32), 'Wq': jax.random.normal(k1, (N_HEADS * HEAD_DIM, HIDDEN), dtype=jnp.float32) * scale, 'Wk': jax.random.normal(k2, (N_KV_HEADS * HEAD_DIM, HIDDEN), dtype=jnp.float32) * scale, 'Wv': jax.random.normal(k3, (N_KV_HEADS * HEAD_DIM, HIDDEN), dtype=jnp.float32) * scale, 'Wo': jax.random.normal(k4, (HIDDEN, N_HEADS * HEAD_DIM), dtype=jnp.float32) * scale}
    _L1_attn_all = _L1_attn_setup()
    _L1_attn_in = {k: v for k, v in _L1_attn_all.items() if k in ('Wq', 'Wk', 'Wv', 'Wo')}
    del _L1_attn_all

    def _L1_xattn_setup():
        import jax, jax.numpy as jnp
        import numpy as np
        TEXT_DIM = 512
        FEATURE_DIM = 512

        def _xavier_uniform(key, shape):
            fan_in, fan_out = (shape[1], shape[0])
            limit = float(np.sqrt(6.0 / (fan_in + fan_out)))
            return jax.random.uniform(key, shape, jnp.float32, -limit, limit)
        key = jax.random.key(seed)
        k1, k2, k3, k4 = jax.random.split(key, 4)
        text = jax.random.normal(k1, (8, 256, TEXT_DIM), jnp.float32)
        features = jax.random.normal(k2, (8, 72, FEATURE_DIM), jnp.float32)
        Wq = _xavier_uniform(k3, (FEATURE_DIM, TEXT_DIM))
        bq = jnp.zeros((FEATURE_DIM,), jnp.float32)
        Wk = _xavier_uniform(k4, (FEATURE_DIM, FEATURE_DIM))
        bk = jnp.zeros((FEATURE_DIM,), jnp.float32)
        return {'text': text, 'features': features, 'Wq': Wq, 'bq': bq, 'Wk': Wk, 'bk': bk}
    _L1_xattn_all = _L1_xattn_setup()
    _L1_xattn_in = {k: v for k, v in _L1_xattn_all.items() if k in ('Wq', 'bq', 'Wk', 'bk')}
    del _L1_xattn_all

    def _L1_ffn_setup():
        import jax, jax.numpy as jnp
        import numpy as np
        D_IN, D_OUT = (512, 512)
        B, S = (2, 256)
        key = jax.random.key(seed)
        kx, kw = jax.random.split(key)
        x = jax.random.normal(kx, (B, S, D_IN), dtype=jnp.float32)
        w = jax.random.normal(kw, (D_IN, D_OUT), dtype=jnp.float32)
        sign = jnp.where(w >= 0, 1.0, -1.0).astype(jnp.float32)
        scale = jnp.abs(w).mean().astype(jnp.float32)
        return {'x': x, 'sign': sign, 'scale': scale}
    _L1_ffn_all = _L1_ffn_setup()
    _L1_ffn_in = {k: v for k, v in _L1_ffn_all.items() if k in ('sign', 'scale')}
    del _L1_ffn_all
    return {'x': x, 'ctx_4096': ctx_4096, 'mask_1x1xSxS2_ff0': mask_1x1xSxS2_ff0, 'L0_attn_Wqkv': _L0_attn_in['Wqkv'], 'L0_attn_q_ln_w': _L0_attn_in['q_ln_w'], 'L0_attn_q_ln_b': _L0_attn_in['q_ln_b'], 'L0_attn_k_ln_w': _L0_attn_in['k_ln_w'], 'L0_attn_k_ln_b': _L0_attn_in['k_ln_b'], 'L0_attn_Wout': _L0_attn_in['Wout'], 'L0_xattn_q_proj_w': _L0_xattn_in['q_proj_w'], 'L0_xattn_k_proj_w': _L0_xattn_in['k_proj_w'], 'L0_xattn_v_proj_w': _L0_xattn_in['v_proj_w'], 'L0_xattn_o_proj_w': _L0_xattn_in['o_proj_w'], 'L0_xattn_q_norm_w': _L0_xattn_in['q_norm_w'], 'L0_xattn_k_norm_w': _L0_xattn_in['k_norm_w'], 'L0_ffn_W_base': _L0_ffn_in['W_base'], 'L0_ffn_b_base': _L0_ffn_in['b_base'], 'L0_ffn_W_gate': _L0_ffn_in['W_gate'], 'L0_ffn_W_thr': _L0_ffn_in['W_thr'], 'L0_ffn_b_thr': _L0_ffn_in['b_thr'], 'L0_ffn_A_w': _L0_ffn_in['A_w'], 'L0_ffn_B_w': _L0_ffn_in['B_w'], 'L1_attn_Wq': _L1_attn_in['Wq'], 'L1_attn_Wk': _L1_attn_in['Wk'], 'L1_attn_Wv': _L1_attn_in['Wv'], 'L1_attn_Wo': _L1_attn_in['Wo'], 'L1_xattn_Wq': _L1_xattn_in['Wq'], 'L1_xattn_bq': _L1_xattn_in['bq'], 'L1_xattn_Wk': _L1_xattn_in['Wk'], 'L1_xattn_bk': _L1_xattn_in['bk'], 'L1_ffn_sign': _L1_ffn_in['sign'], 'L1_ffn_scale': _L1_ffn_in['scale']}

def reference(x, ctx_4096, mask_1x1xSxS2_ff0, L0_attn_Wqkv, L0_attn_q_ln_w, L0_attn_q_ln_b, L0_attn_k_ln_w, L0_attn_k_ln_b, L0_attn_Wout, L0_xattn_q_proj_w, L0_xattn_k_proj_w, L0_xattn_v_proj_w, L0_xattn_o_proj_w, L0_xattn_q_norm_w, L0_xattn_k_norm_w, L0_ffn_W_base, L0_ffn_b_base, L0_ffn_W_gate, L0_ffn_W_thr, L0_ffn_b_thr, L0_ffn_A_w, L0_ffn_B_w, L1_attn_Wq, L1_attn_Wk, L1_attn_Wv, L1_attn_Wo, L1_xattn_Wq, L1_xattn_bq, L1_xattn_Wk, L1_xattn_bk, L1_ffn_sign, L1_ffn_scale):
    import jax
    import jax.numpy as jnp

    def _L0_attn_ref(hidden_states, Wqkv, q_ln_w, q_ln_b, k_ln_w, k_ln_b, Wout):
        import jax, jax.numpy as jnp
        import numpy as np
        D_MODEL = 512
        N_HEADS = 32
        HEAD_DIM = D_MODEL // N_HEADS
        CLIP_QKV = 8.0
        ALIBI_BIAS_MAX = 8.0
        LN_EPS = 1e-05

        def _alibi_slopes(n_heads: int, bias_max: float) -> jnp.ndarray:
            next_pow2 = 2 ** int(np.ceil(np.log2(n_heads)))
            m = np.arange(1, next_pow2 + 1, dtype=np.float32) * (bias_max / next_pow2)
            slopes = 1.0 / np.power(2.0, m)
            if next_pow2 != n_heads:
                slopes = np.concatenate([slopes[1::2], slopes[::2]])[:n_heads]
            return jnp.asarray(slopes)

        def _layer_norm(x, w, b):
            mu = jnp.mean(x, axis=-1, keepdims=True)
            var = jnp.mean(jnp.square(x - mu), axis=-1, keepdims=True)
            return (x - mu) * jax.lax.rsqrt(var + LN_EPS) * w + b
        B, S, _ = hidden_states.shape
        qkv = jnp.einsum('bsd,ed->bse', hidden_states, Wqkv)
        qkv = jnp.clip(qkv, -CLIP_QKV, CLIP_QKV)
        q, k, v = jnp.split(qkv, [D_MODEL, 2 * D_MODEL], axis=-1)
        q = _layer_norm(q, q_ln_w, q_ln_b)
        k = _layer_norm(k, k_ln_w, k_ln_b)
        q = q.reshape(B, S, N_HEADS, HEAD_DIM)
        k = k.reshape(B, S, N_HEADS, HEAD_DIM)
        v = v.reshape(B, S, N_HEADS, HEAD_DIM)
        scale = HEAD_DIM ** (-0.5)
        scores = jnp.einsum('bqhd,bkhd->bhqk', q, k) * scale
        slopes = _alibi_slopes(N_HEADS, ALIBI_BIAS_MAX)
        pos = jnp.arange(S)
        rel = (pos[None, :] - pos[:, None]).astype(jnp.float32)
        scores = scores + slopes[None, :, None, None] * rel[None, None]
        causal = pos[None, :] <= pos[:, None]
        scores = jnp.where(causal[None, None], scores, jnp.float32(-1e+30))
        probs = jax.nn.softmax(scores, axis=-1)
        out = jnp.einsum('bhqk,bkhd->bqhd', probs, v).reshape(B, S, D_MODEL)
        return jnp.einsum('bsd,ed->bse', out, Wout)

    def _L0_xattn_ref(hidden_states, cross_attention_states, attention_mask, q_proj_w, k_proj_w, v_proj_w, o_proj_w, q_norm_w, k_norm_w):
        import jax, jax.numpy as jnp
        import numpy as np
        NUM_HEADS = 32
        NUM_KV_HEADS = 8
        HEAD_DIM = 128
        HIDDEN = 512
        EPS = 1e-05

        def rmsnorm(x, w, eps=EPS):
            xf = x.astype(jnp.float32)
            var = jnp.mean(xf * xf, axis=-1, keepdims=True)
            return w * (xf * jax.lax.rsqrt(var + eps)).astype(x.dtype)
        B, Q, _ = hidden_states.shape
        KV = cross_attention_states.shape[1]
        n_rep = NUM_HEADS // NUM_KV_HEADS
        q = (hidden_states @ q_proj_w.T).reshape(B, Q, NUM_HEADS, HEAD_DIM).transpose(0, 2, 1, 3)
        k = (cross_attention_states @ k_proj_w.T).reshape(B, KV, NUM_KV_HEADS, HEAD_DIM).transpose(0, 2, 1, 3)
        v = (cross_attention_states @ v_proj_w.T).reshape(B, KV, NUM_KV_HEADS, HEAD_DIM).transpose(0, 2, 1, 3)
        q = rmsnorm(q, q_norm_w)
        k = jnp.repeat(k, n_rep, axis=1)
        v = jnp.repeat(v, n_rep, axis=1)
        k = rmsnorm(k, k_norm_w)
        scale = 1.0 / np.sqrt(HEAD_DIM)
        scores = jnp.einsum('bhqd,bhkd->bhqk', q, k) * scale + attention_mask
        attn = jax.nn.softmax(scores.astype(jnp.float32), axis=-1).astype(q.dtype)
        out = jnp.einsum('bhqk,bhkd->bhqd', attn, v)
        out = out.transpose(0, 2, 1, 3).reshape(B, Q, NUM_HEADS * HEAD_DIM)
        return out @ o_proj_w.T

    def _L0_ffn_ref(x, W_base, b_base, W_gate, W_thr, b_thr, A_w, B_w):
        import jax, jax.numpy as jnp
        import numpy as np
        B, S, D, O, E, R = (4, 256, 512, 512, 8, 16)
        SCALING = 32.0 / 16.0
        MAX_THRESHOLD = 0.125
        base = jnp.einsum('bsd,od->bso', x, W_base) + b_base
        xf = x.reshape(-1, D)
        gate = jax.nn.softmax(xf @ W_gate.T, axis=-1)
        thr = jax.nn.sigmoid(xf @ W_thr + b_thr[0]) * MAX_THRESHOLD
        adapted = gate - thr[:, None]
        selected = (adapted >= 0).astype(x.dtype)
        w = adapted * selected
        wsum = jnp.sum(w, axis=-1, keepdims=True)
        wsum = jnp.where(wsum == 0, jnp.ones_like(wsum), wsum)
        w = w / wsum
        h = jnp.einsum('nd,erd->ner', xf, A_w)
        moe = jnp.einsum('ner,ne,eor->no', h, w, B_w) * SCALING
        return base + moe.reshape(base.shape)

    def _L1_attn_ref(hidden_states, Wq, Wk, Wv, Wo):
        import jax, jax.numpy as jnp
        import numpy as np
        import math
        HIDDEN = 512
        N_HEADS = 32
        N_KV_HEADS = 8
        HEAD_DIM = HIDDEN // N_HEADS
        N_REP = N_HEADS // N_KV_HEADS
        B, S = (1, 256)
        bsz, q_len, _ = hidden_states.shape
        q = hidden_states @ Wq.T
        k = hidden_states @ Wk.T
        v = hidden_states @ Wv.T
        q = q.reshape(bsz, q_len, N_HEADS, HEAD_DIM).transpose(0, 2, 1, 3)
        k = k.reshape(bsz, q_len, N_KV_HEADS, HEAD_DIM).transpose(0, 2, 1, 3)
        v = v.reshape(bsz, q_len, N_KV_HEADS, HEAD_DIM).transpose(0, 2, 1, 3)
        k = jnp.broadcast_to(k[:, :, None], (bsz, N_KV_HEADS, N_REP, q_len, HEAD_DIM)).reshape(bsz, N_HEADS, q_len, HEAD_DIM)
        v = jnp.broadcast_to(v[:, :, None], (bsz, N_KV_HEADS, N_REP, q_len, HEAD_DIM)).reshape(bsz, N_HEADS, q_len, HEAD_DIM)
        scores = jnp.einsum('bnsh,bnkh->bnsk', q, k) / math.sqrt(HEAD_DIM)
        attn = jax.nn.softmax(scores.astype(jnp.float32), axis=-1).astype(q.dtype)
        out = jnp.einsum('bnsk,bnkh->bnsh', attn, v)
        out = out.transpose(0, 2, 1, 3).reshape(bsz, q_len, HIDDEN)
        return out @ Wo.T

    def _L1_xattn_ref(text, features, Wq, bq, Wk, bk):
        import jax, jax.numpy as jnp
        import numpy as np
        TEXT_DIM = 512
        FEATURE_DIM = 512

        def _xavier_uniform(key, shape):
            fan_in, fan_out = (shape[1], shape[0])
            limit = float(np.sqrt(6.0 / (fan_in + fan_out)))
            return jax.random.uniform(key, shape, jnp.float32, -limit, limit)
        Q = jnp.einsum('btx,dx->btd', text, Wq) + bq
        K = jnp.einsum('bpx,dx->bpd', features, Wk) + bk
        scale = 1.0 / jnp.sqrt(jnp.asarray(K.shape[-1], K.dtype))
        scores = jnp.einsum('btd,bpd->btp', Q, K) * scale
        attn = jax.nn.softmax(scores, axis=-1)
        attended = jnp.einsum('btp,bpd->btd', attn, features)
        return attended

    def _L1_ffn_ref(x, sign, scale):
        import jax, jax.numpy as jnp
        import numpy as np
        D_IN, D_OUT = (512, 512)
        B, S = (2, 256)
        s = jax.nn.softplus(scale)
        return jnp.einsum('bsi,io->bso', x, sign) * s
    x = x + _L0_attn_ref(_layernorm(x, axis=-1), L0_attn_Wqkv, L0_attn_q_ln_w, L0_attn_q_ln_b, L0_attn_k_ln_w, L0_attn_k_ln_b, L0_attn_Wout)
    x = x + _L0_xattn_ref(_layernorm(x, axis=-1), ctx_4096, mask_1x1xSxS2_ff0, L0_xattn_q_proj_w, L0_xattn_k_proj_w, L0_xattn_v_proj_w, L0_xattn_o_proj_w, L0_xattn_q_norm_w, L0_xattn_k_norm_w)
    x = x + _L0_ffn_ref(_layernorm(x, axis=-1), L0_ffn_W_base, L0_ffn_b_base, L0_ffn_W_gate, L0_ffn_W_thr, L0_ffn_b_thr, L0_ffn_A_w, L0_ffn_B_w)
    x = x + _L1_attn_ref(_layernorm(x, axis=-1), L1_attn_Wq, L1_attn_Wk, L1_attn_Wv, L1_attn_Wo)
    x = x + _L1_xattn_ref(_layernorm(x, axis=-1), ctx_4096, L1_xattn_Wq, L1_xattn_bq, L1_xattn_Wk, L1_xattn_bk)
    x = x + _L1_ffn_ref(_layernorm(x, axis=-1), L1_ffn_sign, L1_ffn_scale)
    return x

_drawn_inputs = setup_inputs


def setup_inputs(seed=0):
    import zlib

    import numpy as np

    out = dict(_drawn_inputs(seed))
    spreads = {'L0_attn_q_ln_w': (1.0, 0.6),
     'L0_attn_q_ln_b': (0.0, 0.8),
     'L0_attn_k_ln_w': (1.0, 0.6),
     'L0_attn_k_ln_b': (0.0, 0.8),
     'L0_xattn_q_norm_w': (1.0, 0.2),
     'L0_xattn_k_norm_w': (1.0, 0.2),
     'L1_xattn_bq': (0.0, 0.8),
     'L1_xattn_bk': (0.0, 0.8)}
    factors = {'L0_ffn_b_base': 7.653, 'L1_attn_Wq': 8.0, 'L1_attn_Wk': 8.0}
    for name, (base, spread) in spreads.items():
        noise = np.random.default_rng([zlib.crc32(name.encode()), seed]).standard_normal(out[name].shape)
        drawn = base * np.exp(spread * noise) if base else spread * noise
        out[name] = jnp.asarray(drawn.astype(out[name].dtype))
    for name, factor in factors.items():
        out[name] = (out[name] * factor).astype(out[name].dtype)
    return out
```

```python
from contextlib import ExitStack

import numpy as np

import concourse.bass as bass
from concourse import mybir

F32 = mybir.dt.float32
F16 = mybir.dt.float16
BF16 = mybir.dt.bfloat16
ALU = mybir.AluOpType
ACT = mybir.ActivationFunctionType
AX = mybir.AxisListType.X

P = 128
NB = 8
D = 512
CH = D // P
MAT = CH * D
EPS = 1e-5
NH = 32
HD = 16
NKV = 8
GH = 4
NG = NH // GH
CLIP = 8.0
PSCALE = 1024.0
NE, RANK = 8, 16
SLOTS = 6

W_QKVO = 0
W_XK, W_XV = 4, 6
W_XQO = 8
W_L1Q, W_L1KV, W_BASE, W_AG, W_L1O, W_LXQ, W_LXK, W_SIGN = range(8 + 2 * NKV, 16 + 2 * NKV)
N_MATS = 16 + 2 * NKV

V_QW, V_QB, V_KW, V_KB, V_XQN, V_XKN, V_BASE, V_BTHR, V_SCALE = range(9)


class Use:

    def __init__(self, slot, tile, full, free, n):
        self.slot, self.tile, self.full, self.free, self.n, self.done = slot, tile, full, free, n, n + 1


class Ring:

    def __init__(self, name, tiles, sem):
        self.tiles = tiles
        self.full = [sem(f"{name}{i}_full") for i in range(len(tiles))]
        self.free = [sem(f"{name}{i}_free") for i in range(len(tiles))]

    def credit(self, eng):
        for s in self.free:
            eng.sem_inc(s, 1)

    def use(self, k, it=0, per=0):
        depth = len(self.tiles)
        assert per % depth == 0
        i = k % depth
        return Use(i, self.tiles[i], self.full[i], self.free[i], it * (per // depth) + (k // depth + 1))


class Chip:

    def __init__(self, nc, ctx, io):
        self.nc, self.io, self.phase = nc, io, 0

        def sb(name, shape, dt=F32):
            return ctx.enter_context(nc.sbuf_tensor(name, shape, dt))

        self.x = sb("x", [P, NB * D])
        self.hT = [sb("hT_hi", [P, NB * D], F16), sb("hT_lo", [P, NB * D], F16)]
        self.cT = [sb("cT_hi", [P, NB * D], F16), sb("cT_lo", [P, NB * D], F16)]
        self.w = [sb("w_hi", [P, SLOTS, MAT], F16), sb("w_lo", [P, SLOTS, MAT], BF16)]
        self.stage = sb("stage", [P, 2, MAT])
        self.ident = sb("ident", [P, P])
        self.half = sb("half", [P, 2])
        self.z = sb("z", [P, D])
        self.st = sb("st", [P, 6])
        self.mv = sb("mv", [P, 2])
        self.ve = sb("ve", [P, 1])
        self.rstd = sb("rstd", [P, 1])
        self.mhalf = sb("mhalf", [P, 8])
        self.big = sb("big", [P, 16384])
        self.small = sb("small", [P, 5632])
        self.psum = [ctx.enter_context(nc.psum_tensor(f"bank{i}", [P, 512], F32)) for i in range(8)]
        self.loaded = ctx.enter_context(nc.semaphore("loaded"))
        self.staged = [ctx.enter_context(nc.semaphore(f"staged{i}")) for i in range(2)]
        self.n_staged = [0, 0]

    def sem(self, name):
        return self.nc.alloc_semaphore(f"{name}_{self.phase}")

    def begin(self):
        self.phase += 1
        return self.nc.cleanup_on_exit()

    def load_weight(self, eng, mat, buf):
        self.n_staged[buf] += 16
        eng.dma_start(self.stage[:, buf, :], self.io["weights"][mat]).then_inc(self.staged[buf], 16)

    def weight(self, slot):
        return [self.w[0][:, slot, :], self.w[1][:, slot, :]]


def carve(region, shapes):
    at, out = 0, []
    for cols, dt in shapes:
        words = cols if dt == F32 else cols // 2
        v = region[:, at:at + words]
        out.append(v if dt == F32 else v.bitcast(dt))
        at += words
    assert at <= region.shape[1], (at, region.shape)
    return out


def product(nc, out, lhs, rhs, chunks, start=True, stop=True):
    n = 0
    for c in range(chunks):
        for a, b in ((0, 0), (0, 1), (1, 0)):
            last = nc.tensor.matmul(out, lhs(a, c), rhs(b, c), start=start and n == 0,
                                    stop=stop and n == 3 * chunks - 1)
            n += 1
    return last


def tokens(pair, b):
    return lambda half, c: pair[half][:, bass.ds(b * D + c * P, P)]


def columns(pair, first=0, n=D):
    return lambda half, c: pair[half][:, c * D + first:c * D + first + n]


def turn(chip, bank, src, n=4):
    for i in range(n):
        last = chip.nc.tensor.transpose(bank[:, i * P:(i + 1) * P], src[:, i * P:(i + 1) * P], chip.ident[:])
    return last


def heads(ap, n=GH):
    return ap.rearrange("p (h k) -> p h k", h=n)


def spread(ap, n, m):
    return ap.unsqueeze(2).to_broadcast([P, n, m])


class Norm:

    def __init__(self, chip, sem):
        self.chip = chip
        self.chain, self.var, self.rstd, self.z, self.hi, self.carrier = (
            sem(f"norm_{n}") for n in ("chain", "var", "rstd", "z", "hi", "carrier"))

    def stats(self, dve, b, k):
        nc, c = self.chip.nc, self.chip
        nc.vector.bn_stats(c.st[:], c.x[:, bass.ds(b * D, D)]).then_inc(self.chain, 1)
        dve.wait_ge(self.chain, k * 2 + 1)
        dve.sem_inc(self.carrier, 1)
        nc.vector.bn_aggr(c.mv[:], c.st[:]).then_inc(self.chain, 1)
        dve.wait_ge(self.chain, k * 2 + 2)
        nc.vector.tensor_scalar(c.ve[:], c.mv[:, 1:2], EPS, None, ALU.add).then_inc(self.var, 1)

    def root(self, pool, k):
        c = self.chip
        pool.wait_ge(self.var, k + 1)
        c.nc.gpsimd.tensor_tensor(c.rstd[:], c.ve[:], c.mhalf[:, 0:1], ALU.pow).then_inc(self.rstd, 1)

    def scale(self, dve, b, k):
        c = self.chip
        dve.wait_ge(self.rstd, k + 1)
        c.nc.vector.tensor_scalar(c.z[:], c.x[:, bass.ds(b * D, D)], c.mv[:, 0:1], c.rstd[:],
                                  ALU.subtract, ALU.mult).then_inc(self.z, 1)

    def turn(self, pe, k, bank):
        pe.wait_ge(self.z, k + 1)
        pe.wait_ge(bank.free, bank.n)
        turn(self.chip, bank.tile, self.chip.z[:]).then_inc(bank.full, 1)

    def split_hi(self, act, b, bank):
        c = self.chip
        act.wait_ge(bank.full, bank.n)
        c.nc.scalar.activation(c.hT[0][:, bass.ds(b * D, D)], bank.tile[:], ACT.Copy).then_inc(self.hi, 1)

    def split_lo(self, dve, b, k, bank):
        c = self.chip
        dve.wait_ge(self.hi, k + 1)
        at = bass.ds(b * D, D)
        c.nc.vector.tensor_tensor(c.hT[1][:, at], bank.tile[:], c.hT[0][:, at], ALU.subtract).then_inc(bank.free, 1)


def prepare(chip):
    nc, io = chip.nc, chip.io
    with chip.begin():
        split = chip.sem("ctx_hi")
        const = chip.sem("const")
        cstage = chip.big[:, 0:NB * D]
        with nc.Block() as block:

            @block.sync
            def _(sp):
                sp.dma_start(chip.x[:], io["x"]).then_inc(chip.loaded, 16)
                sp.dma_start(chip.ident[:], io["ident"]).then_inc(chip.loaded, 16)
                sp.dma_start(chip.half[:], io["half"]).then_inc(chip.loaded, 16)
                chip.load_weight(sp, W_QKVO, 0)
                chip.load_weight(sp, W_QKVO + 1, 1)
                sp.dma_start(cstage, io["ctxT"]).then_inc(chip.loaded, 16)

            @block.gpsimd
            def _(pool):
                nc.gpsimd.memset(chip.mhalf[:], -0.5).then_inc(const, 1)

            @block.scalar
            def _(act):
                act.wait_ge(chip.loaded, 64)
                nc.scalar.activation(chip.cT[0][:], cstage, ACT.Copy).then_inc(split, 1)

            @block.vector
            def _(dve):
                dve.wait_ge(chip.loaded, 64)
                dve.wait_ge(split, 1)
                nc.vector.tensor_tensor(chip.cT[1][:], cstage, chip.cT[0][:], ALU.subtract)


def split_weights(chip, plan, prefetch):
    nc = chip.nc
    with chip.begin():
        hi, lo_dve, lo_pool = chip.sem("weight_hi"), chip.sem("weight_lo_dve"), chip.sem("weight_lo_pool")
        at = list(chip.n_staged)
        due = []
        for i in range(len(plan)):
            if i >= 2:
                at[i % 2] += 16
            due.append(at[i % 2])
        cut = MAT // 2
        with nc.Block() as block:

            @block.sync
            def _(sp):
                for i, mat in enumerate([m for m, _ in plan[2:]] + prefetch):
                    sp.wait_ge(lo_dve, i + 1)
                    sp.wait_ge(lo_pool, i + 1)
                    chip.load_weight(sp, mat, i % 2)

            @block.scalar
            def _(act):
                for i, (_, slot) in enumerate(plan):
                    act.wait_ge(chip.staged[i % 2], due[i])
                    nc.scalar.activation(chip.w[0][:, slot, :], chip.stage[:, i % 2, :], ACT.Copy).then_inc(hi, 1)

            @block.vector
            def _(dve):
                for i, (_, slot) in enumerate(plan):
                    dve.wait_ge(hi, i + 1)
                    nc.vector.tensor_tensor(chip.w[1][:, slot, 0:cut], chip.stage[:, i % 2, 0:cut],
                                            chip.w[0][:, slot, 0:cut], ALU.subtract).then_inc(lo_dve, 1)

            @block.gpsimd
            def _(pool):
                for i, (_, slot) in enumerate(plan):
                    pool.wait_ge(hi, i + 1)
                    nc.gpsimd.tensor_tensor(chip.w[1][:, slot, cut:], chip.stage[:, i % 2, cut:],
                                            chip.w[0][:, slot, cut:], ALU.subtract).then_inc(lo_pool, 1)


FRONT_T = ["norm", "q0", "q1", "k0", "k1"]
FRONT_A = ["q", "k", "v"]
SELF_ORDER = [("next", "norm_stats"), ("scores", 0), ("scores", 1), ("next", "norm_turn"), ("probs", 0),
              ("scores", 2), ("next", "norm_split"), ("pv", 0), ("probs", 1), ("scores", 3), ("next", "q"),
              ("pv", 1), ("probs", 2), ("scores", 4), ("next", "k"), ("pv", 2), ("probs", 3), ("next", "q_norm"),
              ("scores", 5), ("pv", 3), ("probs", 4), ("next", "k_norm"), ("scores", 6), ("pv", 4), ("probs", 5),
              ("scores", 7), ("pv", 5), ("probs", 6), ("pv", 6), ("probs", 7), ("next", "q_turn"), ("pv", 7),
              ("next", "v"), ("out_turn", 0), ("next", "k_turn"), ("out", 0)]
SELF_FRONT = [("next", n) for n in ("norm_stats", "norm_turn", "norm_split", "q", "k", "q_norm", "k_norm", "q_turn",
                                    "v", "k_turn")]


def self_attention(chip, layer, slots):
    nc, io = chip.nc, chip.io
    first = layer == 0
    nkv = NH if first else NKV
    tiles_t = NH // GH
    bias, qd, kd, qc, kc, qw, kw, rows_, sB, prob, pT, hold, qS, kT_, kS_, vaug = carve(chip.big, [
        (NG * 512, F32), (1024, F32), (1024, F32), (512, F32), (512, F32), (512, F32), (512, F32), (2048, F32),
        (1024, F32), (1024, F32), (1024, F32), (1024, F16), (1024, F16), (1024, F16), (1024, F16), (NH * 17, F32)])
    o, oh, ol, nmax, rinv, qst, qmv, qve, qrs = carve(chip.small, [
        (512, F32), (512, F16), (512, F16), (8, F32), (32, F32), (12, F32), (4, F32), (2, F32), (2, F32)])
    group = [[((g // 4) * 4 + i, g % 4, ((g // 4) * 4 + i) * 4 + g % 4) for i in range(GH)] for g in range(NG)]
    raw = {"q": (qc, qw, qd, 0), "k": (kc, kw, kd, 1)}
    q_pair, stackT, stackS = qS, kT_, kS_

    body_T = ["norm", "p0", "p1", "p2", "p3", "p4", "p5", "p6", "p7", "q0", "q1", "out", "k0", "k1"]
    body_A = ["q", "k", "v", "out"]

    with chip.begin():
        sem = chip.sem
        A = Ring("A", chip.psum[0:2], sem)
        T = Ring("T", chip.psum[2:4], sem)
        S = Ring("S", chip.psum[4:6], sem)
        O = Ring("O", chip.psum[6:8], sem)
        norm = Norm(chip, sem)
        qk_chain, qk_var, qk_rstd, qk_z, qk_w, qk_ready = (
            sem(n) for n in ("qk_chain", "qk_var", "qk_rstd", "qk_z", "qk_w", "qk_ready"))
        stacked, v_ready, carrier = sem("stacked"), sem("v_ready"), sem("carrier")
        held, maxed, prob_ready, summed, o_hi, prepared = (
            sem(n) for n in ("held", "maxed", "prob_ready", "summed", "o_hi", "prepared"))

        def place(front, body, where, name):
            if where == "ahead":
                return front.index(name)
            if where == "body":
                return len(front) + body.index(name)
            kept = [n for n in body if n not in front]
            return len(front) + (NB - 1) * len(body) + kept.index(name)

        def t_use(where, name, it):
            return T.use(place(FRONT_T, body_T, where, name), it, len(body_T) if where == "body" else 0)

        def a_use(where, name, it):
            return A.use(place(FRONT_A, body_A, where, name), it, len(body_A) if where == "body" else 0)

        def schedule(eng, step):
            for _, what in SELF_FRONT:
                step("ahead", what, 0, 0, 0)
            with eng.Fori(0, NB - 1) as it:
                for kind, what in SELF_ORDER:
                    if kind == "next":
                        step("body", what, 0, it + 1, it)
                    else:
                        step("body", kind, what, it, it)
            for kind, what in SELF_ORDER:
                if kind != "next":
                    step("last", kind, what, NB - 1, 0)

        with nc.Block() as block:

            @block.sync
            def _(sp):
                if first:
                    for i, row in enumerate((V_QW, V_QB, V_KW, V_KB)):
                        sp.dma_start(rows_[:, i * D:(i + 1) * D],
                                     io["vectors"][row:row + 1, :].partition_broadcast(P)).then_inc(prepared, 16)
                    sp.dma_start(bias, io["alibi"]).then_inc(prepared, 16)

            @block.gpsimd
            def _(pool):
                for ring in (A, T, S, O):
                    ring.credit(pool)
                nc.gpsimd.memset(vaug, 1.0).then_inc(prepared, 1)
                if first:
                    pool.wait_ge(prepared, 81)
                    nc.gpsimd.tensor_scalar(rows_[:, 0:2 * D], rows_[:, 0:2 * D], HD ** -0.5, 1.0, ALU.mult,
                                            ALU.mult).then_inc(prepared, 1)
                    pool.wait_ge(prepared, 82)

                def step(where, what, g, b, it):
                    if what == "norm_stats":
                        norm.root(pool, b)
                    if first and what in ("q", "k"):
                        i = raw[what][3]
                        pool.wait_ge(qk_var, b * 2 + i + 1)
                        nc.gpsimd.tensor_tensor(qrs[:, i:i + 1], qve[:, i:i + 1], chip.mhalf[:, 0:1],
                                                ALU.pow).then_inc(qk_rstd, 1)
                    if first and what in ("q_norm", "k_norm"):
                        c, w, d, i = raw[what[0]]
                        pool.wait_ge(qk_z, b * 2 + i + 1)
                        nc.gpsimd.tensor_tensor(w, c, rows_[:, 2 * i * D:(2 * i + 1) * D], ALU.mult).then_inc(qk_w, 1)
                        pool.wait_ge(qk_w, b * 2 + i + 1)
                        twice = lambda ap: ap.rearrange("p (h k) -> p h k", k=HD).unsqueeze(2).to_broadcast([P, NH, 2, HD])
                        nc.gpsimd.tensor_tensor(d.rearrange("p (h s k) -> p h s k", s=2, k=HD), twice(w),
                                                twice(rows_[:, (2 * i + 1) * D:(2 * i + 2) * D]), ALU.add).then_inc(qk_ready, 1)

                schedule(nc.gpsimd, step)

            @block.tensor
            def _(pe):
                def step(where, what, g, b, it):
                    if what == "norm_turn":
                        norm.turn(pe, b, t_use(where, "norm", it))
                    if what in ("q", "k", "v"):
                        if what == "q":
                            h = t_use(where, "norm", it)
                            pe.wait_ge(h.free, h.done)
                        a = a_use(where, what, it)
                        pe.wait_ge(a.free, a.n)
                        if first:
                            w, out = columns(chip.weight(slots[what])), a.tile[:]
                        elif what == "q":
                            w, out = columns(chip.weight(slots["q"])), a.tile[:]
                        else:
                            w = columns(chip.weight(slots["k"]), 0 if what == "k" else P, P)
                            out = a.tile[:, 0:P]
                        product(nc, out, tokens(chip.hT, b), w, CH).then_inc(a.full, 1)
                    if what in ("q_turn", "k_turn"):
                        d, i = raw[what[0]][2:]
                        if first:
                            pe.wait_ge(qk_ready, b * 2 + i + 1)
                        else:
                            a = a_use(where, what[0], it)
                            pe.wait_ge(a.free, a.done)
                        for half in range(2):
                            t = t_use(where, f"{what[0]}{half}", it)
                            pe.wait_ge(t.free, t.n)
                            turn(chip, t.tile, d[:, half * 512:(half + 1) * 512]).then_inc(t.full, 1)
                    if what == "scores":
                        if g == 0:
                            pe.wait_ge(stacked, b + 1)
                        s = S.use(g, b, NG)
                        pe.wait_ge(s.free, s.n)
                        for i, (tile, rg, _) in enumerate(group[g]):
                            at = slice(32 * rg, 32 * rg + 32)
                            lhs = q_pair[at, tile * P:(tile + 1) * P]
                            nc.tensor.matmul(s.tile[:, i * P:(i + 1) * P], lhs, stackT[at, tile * P:(tile + 1) * P],
                                             start=True, stop=False)
                            last = nc.tensor.matmul(s.tile[:, i * P:(i + 1) * P], lhs,
                                                    stackS[at, tile * P:(tile + 1) * P], start=False, stop=True)
                        last.then_inc(s.full, 1)
                    if what == "probs":
                        pe.wait_ge(prob_ready, b * NG + g + 1)
                        t = t_use(where, f"p{g}", it)
                        pe.wait_ge(t.free, t.n)
                        turn(chip, t.tile, prob[:, (g % 2) * 512:(g % 2 + 1) * 512]).then_inc(t.full, 1)
                    if what == "pv":
                        t = t_use(where, f"p{g}", it)
                        pe.wait_ge(t.free, t.done)
                        if g == 0:
                            pe.wait_ge(v_ready, b + 1)
                        u = O.use(g // 4, b, 2)
                        if g % 4 == 0:
                            pe.wait_ge(u.free, u.n)
                        for i, (tile, rg, head) in enumerate(group[g]):
                            at = (i * 4 + rg) * 17
                            kv = head if first else tile
                            src = (g % 2) * 512 + i * P
                            last = nc.tensor.matmul(u.tile[:, at:at + 17], pT[:, src:src + P],
                                                    vaug[:, kv * 17:(kv + 1) * 17], start=True, stop=True)
                        if g % 4 == 3:
                            last.then_inc(u.full, 1)
                    if what == "out_turn":
                        u = O.use(1, b, 2)
                        pe.wait_ge(u.free, u.done)
                        t = t_use(where, "out", it)
                        pe.wait_ge(t.free, t.n)
                        turn(chip, t.tile, o).then_inc(t.full, 1)
                    if what == "out":
                        t = t_use(where, "out", it)
                        pe.wait_ge(t.free, t.done)
                        a = a_use(where, "out", it)
                        pe.wait_ge(a.free, a.n)
                        product(nc, a.tile[:], lambda half, c: (oh, ol)[half][:, c * P:(c + 1) * P],
                                columns(chip.weight(slots["o"])), CH).then_inc(a.full, 1)

                schedule(nc.tensor, step)

            @block.scalar
            def _(act):
                def step(where, what, g, b, it):
                    if what == "norm_turn":
                        norm.split_hi(act, b, t_use(where, "norm", it))
                    if not first and what in ("q", "k"):
                        a = a_use(where, what, it)
                        act.wait_ge(a.full, a.n)
                        if what == "q":
                            src = a.tile[:].rearrange("p (h k) -> p h k", k=HD).unsqueeze(2).to_broadcast([P, NH, 2, HD])
                            nc.scalar.activation(qd.rearrange("p (h s k) -> p h s k", s=2, k=HD), src, ACT.Copy,
                                                 scale=HD ** -0.5).then_inc(a.free, 1)
                        else:
                            src = a.tile[:, 0:P].rearrange("p (h k) -> p h k", k=HD).unsqueeze(2).to_broadcast([P, NKV, 8, HD])
                            nc.scalar.activation(kd.rearrange("p (h s k) -> p h s k", s=8, k=HD), src,
                                                 ACT.Copy).then_inc(a.free, 1)
                    if what in ("q_turn", "k_turn"):
                        for half in range(2):
                            t = t_use(where, f"{what[0]}{half}", it)
                            act.wait_ge(t.full, t.n)
                            nc.scalar.activation(hold[:, t.slot * 512:(t.slot + 1) * 512], t.tile[:],
                                                 ACT.Copy).then_inc(held, 1)
                    if what == "scores":
                        act.wait_ge(maxed, b * NG + g + 1)
                        s = S.use(g, b, NG)
                        for i in range(GH):
                            at = (g % 2) * 512 + i * P
                            src = sB[:, at:at + P] if first else s.tile[:, i * P:(i + 1) * P]
                            m = (g % 2) * GH + i
                            last = nc.scalar.activation(prob[:, at:at + P], src, ACT.Exp, bias=nmax[:, m:m + 1])
                        last.then_inc(prob_ready, 1)
                    if what == "out_turn":
                        t = t_use(where, "out", it)
                        act.wait_ge(t.full, t.n)
                        nc.scalar.activation(oh, t.tile[:], ACT.Copy).then_inc(o_hi, 1)

                schedule(nc.scalar, step)

            @block.vector
            def _(dve):
                dve.wait_ge(prepared, 82 if first else 1)

                def step(where, what, g, b, it):
                    if what == "norm_stats":
                        norm.stats(dve, b, b)
                    if what == "norm_turn":
                        norm.scale(dve, b, b)
                    if what == "norm_split":
                        norm.split_lo(dve, b, b, t_use(where, "norm", it))
                    if first and what in ("q", "k"):
                        c, _, _, i = raw[what]
                        a = a_use(where, what, it)
                        dve.wait_ge(a.full, a.n)
                        nc.vector.tensor_scalar(c, a.tile[:], CLIP, -CLIP, ALU.min, ALU.max).then_inc(a.free, 1)
                        dve.wait_ge(a.free, a.done)
                        st = qst[:, 6 * i:6 * i + 6]
                        nc.vector.bn_stats(st, c).then_inc(qk_chain, 1)
                        dve.wait_ge(qk_chain, b * 4 + 2 * i + 1)
                        dve.sem_inc(carrier, 1)
                        nc.vector.bn_aggr(qmv[:, 2 * i:2 * i + 2], st).then_inc(qk_chain, 1)
                        dve.wait_ge(qk_chain, b * 4 + 2 * i + 2)
                        nc.vector.tensor_scalar(qve[:, i:i + 1], qmv[:, 2 * i + 1:2 * i + 2], EPS, None,
                                                ALU.add).then_inc(qk_var, 1)
                    if first and what in ("q_norm", "k_norm"):
                        c, _, _, i = raw[what[0]]
                        dve.wait_ge(qk_rstd, b * 2 + i + 1)
                        nc.vector.tensor_scalar(c, c, qmv[:, 2 * i:2 * i + 1], qrs[:, i:i + 1],
                                                ALU.subtract, ALU.mult).then_inc(qk_z, 1)
                    if what == "v":
                        a = a_use(where, what, it)
                        dve.wait_ge(a.full, a.n)
                        dst = vaug[:, 0:nkv * 17].rearrange("p (h k) -> p h k", k=17)[:, :, 0:HD]
                        src = a.tile[:, 0:nkv * HD].rearrange("p (h k) -> p h k", k=HD)
                        if first:
                            nc.vector.tensor_scalar(dst, src, CLIP, -CLIP, ALU.min, ALU.max).then_inc(a.free, 1)
                        else:
                            nc.vector.tensor_copy(dst, src).then_inc(a.free, 1)
                        dve.wait_ge(a.free, a.done)
                        dve.sem_inc(v_ready, 1)
                    if what in ("q_turn", "k_turn"):
                        for half in range(2):
                            t = t_use(where, f"{what[0]}{half}", it)
                            dve.wait_ge(held, b * 4 + half + (1 if what[0] == "q" else 3))
                            h = hold[:, t.slot * 512:(t.slot + 1) * 512]
                            at = slice(half * 512, (half + 1) * 512)
                            if what[0] == "q":
                                nc.vector.scalar_tensor_tensor(out=q_pair[:, at], in0=h, scalar=chip.half[:, 0:1],
                                                               in1=t.tile[:], op0=ALU.mult, op1=ALU.add).then_inc(t.free, 1)
                            else:
                                nc.vector.scalar_tensor_tensor(out=stackT[:, at], in0=h, scalar=chip.half[:, 0:1],
                                                               in1=t.tile[:], op0=ALU.mult, op1=ALU.add)
                                nc.vector.scalar_tensor_tensor(out=stackS[:, at], in0=h, scalar=chip.half[:, 1:2],
                                                               in1=t.tile[:], op0=ALU.mult, op1=ALU.add).then_inc(t.free, 1)
                        if what[0] == "k":
                            dve.wait_ge(t.free, t.done)
                            dve.sem_inc(stacked, 1)
                    if what == "scores":
                        s = S.use(g, b, NG)
                        dve.wait_ge(s.full, s.n)
                        at = slice((g % 2) * 512, (g % 2 + 1) * 512)
                        if first:
                            if g >= 2:
                                dve.wait_ge(prob_ready, b * NG + g - 1)
                            nc.vector.tensor_tensor(sB[:, at], s.tile[:], bias[:, g * 512:(g + 1) * 512],
                                                    ALU.add).then_inc(s.free, 1)
                            dve.wait_ge(s.free, s.done)
                        src = sB[:, at] if first else s.tile[:]
                        nc.vector.tensor_reduce(nmax[:, (g % 2) * GH:(g % 2 + 1) * GH], heads(src), AX, ALU.max,
                                                negate=True).then_inc(maxed, 1)
                    if what == "probs":
                        if not first:
                            s = S.use(g, b, NG)
                            dve.wait_ge(prob_ready, b * NG + g + 1)
                            dve.sem_inc(s.free, 1)
                        t = t_use(where, f"p{g}", it)
                        dve.wait_ge(t.full, t.n)
                        nc.vector.tensor_copy(pT[:, (g % 2) * 512:(g % 2 + 1) * 512], t.tile[:]).then_inc(t.free, 1)
                    if what == "pv" and g % 4 == 3:
                        u = O.use(g // 4, b, 2)
                        dve.wait_ge(u.full, u.n)
                        n = 16
                        src = u.tile[:, 0:n * 17].rearrange("p (h k) -> p h k", k=17)
                        r = rinv[:, (g // 4) * n:(g // 4 + 1) * n]
                        nc.vector.reciprocal(r, src[:, :, HD]).then_inc(summed, 1)
                        dve.wait_ge(summed, b * 2 + g // 4 + 1)
                        dst = o[:, (g // 4) * 256:(g // 4 + 1) * 256].rearrange("p (h k) -> p h k", k=HD)
                        nc.vector.tensor_tensor(dst, src[:, :, 0:HD], spread(r, n, HD), ALU.mult).then_inc(u.free, 1)
                    if what == "out_turn":
                        t = t_use(where, "out", it)
                        dve.wait_ge(o_hi, b + 1)
                        nc.vector.tensor_tensor(ol, t.tile[:], oh, ALU.subtract).then_inc(t.free, 1)
                    if what == "out":
                        a = a_use(where, "out", it)
                        dve.wait_ge(a.full, a.n)
                        at = bass.ds(b * D, D)
                        nc.vector.tensor_tensor(chip.x[:, at], chip.x[:, at], a.tile[:], ALU.add).then_inc(a.free, 1)

                schedule(nc.vector, step)


def rms_stats(nc, dve, src, junk, ss, eps_out, chain, k):
    for i in range(GH):
        at = slice(i * P, (i + 1) * P)
        last = nc.vector.tensor_tensor_reduce(out=junk[:, at], in0=src[:, at], in1=src[:, at], scale=1.0, scalar=0.0,
                                              op0=ALU.mult, op1=ALU.add, accum_out=ss[:, i:i + 1])
    last.then_inc(chain, 1)
    dve.wait_ge(chain, k + 1)
    return nc.vector.tensor_scalar(eps_out, ss, 1.0 / P, EPS, ALU.mult, ALU.add)


def cross_views(chip):
    kT_hi, kT_lo, v_hi, v_lo = carve(chip.big, [(NKV * NB * P, F16)] * 4)
    return (kT_hi, kT_lo), (v_hi, v_lo)


def per_head(t, b):
    return t.rearrange("p (h r) -> p h r", h=NKV)[:, :, bass.ds(b * P, P)]


def cross_keys(chip, k_slots, v_slots):
    nc, io = chip.nc, chip.io
    kT, v = cross_views(chip)
    kf, junk, kn, kw, wrow, qrow, ss, ve, rk = carve(chip.small, [
        (1024, F32), (512, F32), (512, F32), (1024, F32), (P, F32), (P, F32), (4, F32), (8, F32), (8, F32)])
    with chip.begin():
        sem = chip.sem
        A = Ring("A", chip.psum[0:4], sem)
        T = Ring("T", chip.psum[4:6], sem)
        copied, squares, var, root, scaled, ready, split, rows_ready = (
            sem(n) for n in ("copied", "squares", "var", "root", "scaled", "ready", "split_hi", "rows_ready"))
        v_split = sem("v_hi")
        with nc.Block() as block:

            @block.sync
            def _(sp):
                sp.dma_start(wrow, io["vectors"][V_XKN:V_XKN + 1, 0:P].partition_broadcast(P)).then_inc(rows_ready, 16)
                sp.dma_start(qrow, io["vectors"][V_XQN:V_XQN + 1, 0:P].partition_broadcast(P)).then_inc(rows_ready, 16)

            @block.gpsimd
            def _(pool):
                A.credit(pool)
                T.credit(pool)
                pool.wait_ge(rows_ready, 32)
                nc.gpsimd.tensor_tensor(wrow, wrow, qrow, ALU.mult).then_inc(rows_ready, 1)
                pool.wait_ge(rows_ready, 33)
                nc.gpsimd.tensor_scalar(wrow, wrow, P ** -0.5, 1.0, ALU.mult, ALU.mult).then_inc(rows_ready, 1)
                pool.wait_ge(rows_ready, 34)
                with nc.gpsimd.Fori(0, NB) as b:
                    for m in range(2):
                        k = b * 2 + m
                        pool.wait_ge(var, k + 1)
                        nc.gpsimd.tensor_tensor(rk[:, m * 4:m * 4 + 4], ve[:, m * 4:m * 4 + 4], chip.mhalf[:, 0:4],
                                                ALU.pow).then_inc(root, 1)
                        pool.wait_ge(root, k + 1)
                        nc.gpsimd.tensor_tensor(heads(kn), heads(kf[:, m * 512:(m + 1) * 512]),
                                                spread(rk[:, m * 4:m * 4 + 4], GH, P), ALU.mult).then_inc(scaled, 1)
                        pool.wait_ge(scaled, k + 1)
                        nc.gpsimd.tensor_tensor(heads(kw[:, m * 512:(m + 1) * 512]), heads(kn),
                                                wrow.unsqueeze(1).to_broadcast([P, GH, P]), ALU.mult).then_inc(ready, 1)

            @block.tensor
            def _(pe):
                with nc.tensor.Fori(0, NB) as b:
                    for m, slot in enumerate((*k_slots, *v_slots)):
                        a = A.use(m, b, 4)
                        pe.wait_ge(a.free, a.n)
                        product(nc, a.tile[:], tokens(chip.cT, b), columns(chip.weight(slot)), CH).then_inc(a.full, 1)
                    for m in range(2):
                        t = T.use(m, b, 2)
                        pe.wait_ge(ready, b * 2 + m + 1)
                        pe.wait_ge(t.free, t.n)
                        turn(chip, t.tile, kw[:, m * 512:(m + 1) * 512]).then_inc(t.full, 1)

            @block.scalar
            def _(act):
                with nc.scalar.Fori(0, NB) as b:
                    for m in range(2):
                        a = A.use(m, b, 4)
                        act.wait_ge(a.full, a.n)
                        nc.scalar.activation(kf[:, m * 512:(m + 1) * 512], a.tile[:], ACT.Copy).then_inc(a.free, 1)
                    for m in range(2):
                        a = A.use(2 + m, b, 4)
                        act.wait_ge(a.full, a.n)
                        nc.scalar.activation(per_head(v[0], b)[:, m * 4:m * 4 + 4, :], heads(a.tile[:]),
                                             ACT.Copy).then_inc(v_split, 1)
                    for m in range(2):
                        t = T.use(m, b, 2)
                        act.wait_ge(t.full, t.n)
                        nc.scalar.activation(per_head(kT[0], b)[:, m * 4:m * 4 + 4, :], heads(t.tile[:]),
                                             ACT.Copy).then_inc(split, 1)

            @block.vector
            def _(dve):
                with nc.vector.Fori(0, NB) as b:
                    for m in range(2):
                        a = A.use(m, b, 4)
                        dve.wait_ge(a.free, a.done)
                        rms_stats(nc, dve, kf[:, m * 512:(m + 1) * 512], junk, ss, ve[:, m * 4:m * 4 + 4], squares,
                                  b * 2 + m).then_inc(var, 1)
                        dve.wait_ge(var, b * 2 + m + 1)
                    for m in range(2):
                        a = A.use(2 + m, b, 4)
                        dve.wait_ge(v_split, b * 2 + m + 1)
                        nc.vector.tensor_tensor(per_head(v[1], b)[:, m * 4:m * 4 + 4, :], heads(a.tile[:]),
                                                per_head(v[0], b)[:, m * 4:m * 4 + 4, :], ALU.subtract).then_inc(a.free, 1)
                    for m in range(2):
                        t = T.use(m, b, 2)
                        dve.wait_ge(split, b * 2 + m + 1)
                        nc.vector.tensor_tensor(per_head(kT[1], b)[:, m * 4:m * 4 + 4, :], heads(t.tile[:]),
                                                per_head(kT[0], b)[:, m * 4:m * 4 + 4, :], ALU.subtract).then_inc(t.free, 1)


def norm_all(chip):
    nc = chip.nc
    with chip.begin():
        sem = chip.sem
        T = Ring("T", chip.psum[0:2], sem)
        norm = Norm(chip, sem)
        with nc.Block() as block:

            @block.gpsimd
            def _(pool):
                T.credit(pool)
                with nc.gpsimd.Fori(0, NB) as b:
                    norm.root(pool, b)

            @block.vector
            def _(dve):
                with nc.vector.Fori(0, NB // 2) as h:
                    for i in range(2):
                        b = h * 2 + i
                        norm.stats(dve, b, b)
                        norm.scale(dve, b, b)
                        norm.split_lo(dve, b, b, T.use(i, h, 2))

            @block.tensor
            def _(pe):
                with nc.tensor.Fori(0, NB // 2) as h:
                    for i in range(2):
                        norm.turn(pe, h * 2 + i, T.use(i, h, 2))

            @block.scalar
            def _(act):
                with nc.scalar.Fori(0, NB // 2) as h:
                    for i in range(2):
                        norm.split_hi(act, h * 2 + i, T.use(i, h, 2))


CROSS_ORDER = [("norm", 2), ("q_turn", 1), ("q", 0), ("pv", 3), ("probs", 2), ("scores", 1), ("out", 4)]


def cross_attention(chip, even, odd):
    nc, io = chip.nc, chip.io
    kT, v = cross_views(chip)
    qf, qn, s_, prob, pn, mask, qh, ql, ph, pl, a0h, a0l, a1h, a1l, junk_, ss, ve, rq, nmax, rs, ri = carve(chip.small, [
        (512, F32), (512, F32), (512, F32), (512, F32), (512, F32), (P, F32), (512, F16), (512, F16), (512, F16),
        (512, F16), (512, F16), (512, F16), (512, F16), (512, F16), (512, F32), (4, F32), (4, F32), (4, F32),
        (4, F32), (4, F32), (4, F32)])
    ah, al = (a0h, a1h), (a0l, a1l)
    n_slots = 2 * NB
    PARTS = NB // 2
    incoming = [odd[0], odd[1], even[0], even[1]]
    base = list(chip.n_staged)

    with chip.begin():
        sem = chip.sem
        A = Ring("A", chip.psum[0:2], sem)
        T = Ring("T", chip.psum[2:4], sem)
        S = Ring("S", chip.psum[4:6], sem)
        O = Ring("O", chip.psum[6:8], sem)
        qf_ready, squares, var, root, qn_ready, q_hi, s_ready, maxed, prob_ready, sums, inv, pn_ready, p_hi, a_hi = (
            sem(n) for n in ("qf_ready", "squares", "var", "root", "qn_ready", "q_hi", "s_ready", "maxed",
                             "prob_ready", "sums", "inv", "pn_ready", "p_hi", "a_hi"))
        w_hi, w_done, got_mask = sem("w_hi"), sem("w_done"), sem("got_mask")

        def one(ring, bank, s, gg):
            return Use(bank, ring.tiles[bank], ring.full[bank], ring.free[bank], gg * n_slots + s + 1)

        def schedule(eng, step):
            with eng.Fori(0, NKV // 2) as gg:
                for slot in range(n_slots + 4):
                    for what, behind in CROSS_ORDER:
                        s = slot - behind
                        if 0 <= s < n_slots:
                            step(what, s, gg, gg * n_slots + s)
                    if slot < n_slots:
                        step("weights", slot, gg, gg * n_slots + slot)

        with nc.Block() as block:

            @block.sync
            def _(sp):
                sp.dma_start(mask, io["mask"]).then_inc(got_mask, 16)
                with nc.sync.Fori(0, NKV // 2) as gg:
                    for m in range(4):
                        sp.wait_ge(w_done, gg * n_slots + PARTS * (m + 1))
                        mat = gg * 4 + (W_XQO + 4 + m)
                        sp.dma_start(chip.stage[:, m % 2, :],
                                     io["weights"][bass.ds(mat, 1), :, :].rearrange("o p n -> p (o n)")
                                     ).then_inc(chip.staged[m % 2], 16)

            @block.gpsimd
            def _(pool):
                for ring in (A, T, S, O):
                    ring.credit(pool)

                def step(what, s, gg, k):
                    if what == "q":
                        pool.wait_ge(var, k + 1)
                        nc.gpsimd.tensor_tensor(rq, ve, chip.mhalf[:, 0:4], ALU.pow).then_inc(root, 1)
                        pool.wait_ge(root, k + 1)
                        nc.gpsimd.tensor_tensor(heads(qn), heads(qf), spread(rq, GH, P), ALU.mult).then_inc(qn_ready, 1)
                    if what == "norm":
                        pool.wait_ge(inv, k + 1)
                        nc.gpsimd.tensor_tensor(heads(pn), heads(prob), spread(ri, GH, P), ALU.mult).then_inc(pn_ready, 1)
                    if what == "weights":
                        m, part = s // PARTS, s % PARTS
                        at = slice(part * D, (part + 1) * D)
                        pool.wait_ge(w_hi, k + 1)
                        nc.gpsimd.tensor_tensor(chip.w[1][:, incoming[m], at], chip.stage[:, m % 2, at],
                                                chip.w[0][:, incoming[m], at], ALU.subtract).then_inc(w_done, 1)

                schedule(nc.gpsimd, step)

            @block.tensor
            def _(pe):
                def step(what, s, gg, k):
                    b, odd_half = s % NB, s // NB
                    if what == "q":
                        if s == NB:
                            pe.wait_ge(w_done, gg * n_slots + PARTS)
                        a = one(A, 0, s, gg)
                        pe.wait_ge(a.free, a.n)
                        product(nc, a.tile[:], tokens(chip.hT, b), columns(chip.weight((even, odd)[odd_half][0])),
                                CH).then_inc(a.full, 1)
                    if what == "q_turn":
                        t = one(T, 0, s, gg)
                        pe.wait_ge(qn_ready, k + 1)
                        pe.wait_ge(t.free, t.n)
                        turn(chip, t.tile, qn).then_inc(t.full, 1)
                    if what == "scores":
                        t = one(T, 0, s, gg)
                        pe.wait_ge(t.free, t.done)
                        u = S.use(s, gg, n_slots)
                        pe.wait_ge(u.free, u.n)
                        key = (gg * 2 + odd_half) * (NB * P) + b * P
                        for i in range(GH):
                            last = product(nc, u.tile[:, i * P:(i + 1) * P],
                                           lambda half, c, i=i: (qh, ql)[half][:, i * P:(i + 1) * P],
                                           lambda half, c: kT[half][:, bass.ds(key, P)], 1)
                        last.then_inc(u.full, 1)
                    if what == "probs":
                        t = one(T, 1, s, gg)
                        pe.wait_ge(pn_ready, k + 1)
                        pe.wait_ge(t.free, t.n)
                        turn(chip, t.tile, pn).then_inc(t.full, 1)
                    if what == "pv":
                        t = one(T, 1, s, gg)
                        pe.wait_ge(t.free, t.done)
                        u = O.use(s, gg, n_slots)
                        pe.wait_ge(u.free, u.n)
                        val = (gg * 2 + odd_half) * (NB * P) + b * P
                        product(nc, u.tile[:], lambda half, c: v[half][:, bass.ds(val, P)],
                                lambda half, c: (ph, pl)[half], 1).then_inc(u.full, 1)
                    if what == "out":
                        if s == NB:
                            pe.wait_ge(w_done, gg * n_slots + 2 * PARTS)
                        u = O.use(s, gg, n_slots)
                        pe.wait_ge(u.free, u.done)
                        a = one(A, 1, s, gg)
                        pe.wait_ge(a.free, a.n)
                        product(nc, a.tile[:], lambda half, c: (ah, al)[half][s % 2][:, c * P:(c + 1) * P],
                                columns(chip.weight((even, odd)[odd_half][1])), CH).then_inc(a.full, 1)

                schedule(nc.tensor, step)

            @block.scalar
            def _(act):
                def step(what, s, gg, k):
                    if what == "q":
                        a = one(A, 0, s, gg)
                        act.wait_ge(a.full, a.n)
                        nc.scalar.activation(qf, a.tile[:], ACT.Copy).then_inc(a.free, 1)
                    if what == "q_turn":
                        t = one(T, 0, s, gg)
                        act.wait_ge(t.full, t.n)
                        nc.scalar.activation(qh, t.tile[:], ACT.Copy).then_inc(q_hi, 1)
                    if what == "scores":
                        act.wait_ge(maxed, k + 1)
                        for i in range(GH):
                            at = slice(i * P, (i + 1) * P)
                            last = nc.scalar.activation(prob[:, at], s_[:, at], ACT.Exp, bias=nmax[:, i:i + 1],
                                                        accum_out=rs[:, i:i + 1])
                        last.then_inc(prob_ready, 1)
                    if what == "probs":
                        t = one(T, 1, s, gg)
                        act.wait_ge(t.full, t.n)
                        nc.scalar.activation(ph, t.tile[:], ACT.Copy).then_inc(p_hi, 1)
                    if what == "pv":
                        u = O.use(s, gg, n_slots)
                        act.wait_ge(u.full, u.n)
                        nc.scalar.activation(ah[s % 2], u.tile[:], ACT.Copy, scale=1 / PSCALE).then_inc(a_hi, 1)
                    if what == "weights":
                        m, part = s // PARTS, s % PARTS
                        if part == 0:
                            act.wait_ge(chip.staged[m % 2], gg * 32 + base[m % 2] + 16 * (m // 2))
                            if m == 2:
                                a = one(A, 0, NB - 1, gg)
                                act.wait_ge(a.full, a.n)
                            if m == 3:
                                a = one(A, 1, NB - 1, gg)
                                act.wait_ge(a.full, a.n)
                        at = slice(part * D, (part + 1) * D)
                        nc.scalar.activation(chip.w[0][:, incoming[m], at], chip.stage[:, m % 2, at],
                                             ACT.Copy).then_inc(w_hi, 1)

                schedule(nc.scalar, step)

            @block.vector
            def _(dve):
                dve.wait_ge(got_mask, 16)

                def step(what, s, gg, k):
                    if what == "q":
                        a = one(A, 0, s, gg)
                        dve.wait_ge(a.free, a.done)
                        rms_stats(nc, dve, qf, junk_, ss, ve, squares, k).then_inc(var, 1)
                    if what == "q_turn":
                        t = one(T, 0, s, gg)
                        dve.wait_ge(q_hi, k + 1)
                        nc.vector.tensor_tensor(ql, t.tile[:], qh, ALU.subtract).then_inc(t.free, 1)
                    if what == "scores":
                        u = S.use(s, gg, n_slots)
                        dve.wait_ge(u.full, u.n)
                        nc.vector.tensor_tensor(heads(s_), heads(u.tile[:]),
                                                mask.unsqueeze(1).to_broadcast([P, GH, P]), ALU.add).then_inc(u.free, 1)
                        dve.wait_ge(u.free, u.done)
                        nc.vector.tensor_reduce(nmax, heads(s_), AX, ALU.max, negate=True).then_inc(maxed, 1)
                    if what == "norm":
                        dve.wait_ge(prob_ready, k + 1)
                        nc.vector.tensor_scalar(rs, rs, 1 / PSCALE, None, ALU.mult).then_inc(sums, 1)
                        dve.wait_ge(sums, k + 1)
                        nc.vector.reciprocal(ri, rs).then_inc(inv, 1)
                    if what == "probs":
                        t = one(T, 1, s, gg)
                        dve.wait_ge(p_hi, k + 1)
                        nc.vector.tensor_tensor(pl, t.tile[:], ph, ALU.subtract).then_inc(t.free, 1)
                    if what == "pv":
                        u = O.use(s, gg, n_slots)
                        dve.wait_ge(a_hi, k + 1)
                        nc.vector.scalar_tensor_tensor(out=al[s % 2], in0=u.tile[:], scalar=1 / PSCALE, in1=ah[s % 2],
                                                       op0=ALU.mult, op1=ALU.subtract).then_inc(u.free, 1)
                    if what == "out":
                        a = one(A, 1, s, gg)
                        dve.wait_ge(a.full, a.n)
                        at = slice((s % NB) * D, (s % NB + 1) * D)
                        nc.vector.tensor_tensor(chip.x[:, at], chip.x[:, at], a.tile[:], ALU.add).then_inc(a.free, 1)

                schedule(nc.vector, step)
    for i in range(2):
        chip.n_staged[i] += 16 * 2 * (NKV // 2)


def experts(chip, base_slot, ag_slot):
    nc, io = chip.nc, chip.io
    n_ag = NE * RANK + NE + 1
    CHAIN = 11
    bst, bh, bl, brow, thr = carve(chip.big, [(D, F32), (D, F16), (D, BF16), (D, F32), (4, F32)])
    lay = carve(chip.small, [(n_ag + 3, F32), (P, F32), (P, F16), (P, F16), (NE, F32), (NE, F32), (NE, F32),
                             (8, F32)] * 2)
    names = ("hg", "hw", "hi", "lo", "e", "w", "w2", "c")
    bufs = [dict(zip(names, lay[8 * i:8 * i + 8], strict=True)) for i in range(2)]

    def col(i, n):
        return bufs[i]["c"][:, n:n + 1]

    with chip.begin():
        sem = chip.sem
        G = Ring("G", chip.psum[0:2], sem)
        Y = Ring("Y", chip.psum[2:4], sem)
        T = Ring("T", chip.psum[4:6], sem)
        got, b_hi, b_lo, nthr, chain, expo, hw_ready, hw_hi, x_b = (
            sem(n) for n in ("got", "b_hi", "b_lo", "nthr", "chain", "expo", "hw_ready", "hw_hi", "x_bias"))
        with nc.Block() as block:

            @block.sync
            def _(sp):
                sp.dma_start(bst, io["expert_b"]).then_inc(got, 16)
                sp.dma_start(brow, io["vectors"][V_BASE:V_BASE + 1, :].partition_broadcast(P)).then_inc(got, 16)
                sp.dma_start(thr[:, 0:2], io["vectors"][V_BTHR:V_BTHR + 1, 0:2].partition_broadcast(P)).then_inc(got, 16)

            @block.gpsimd
            def _(pool):
                for ring in (G, Y, T):
                    ring.credit(pool)
                pool.wait_ge(got, 48)
                with nc.gpsimd.Fori(0, NB) as b:
                    at = bass.ds(b * D, D)
                    nc.gpsimd.tensor_tensor(chip.x[:, at], chip.x[:, at], brow, ALU.add).then_inc(x_b, 1)

            @block.tensor
            def _(pe):
                pe.wait_ge(b_lo, 1)
                with nc.tensor.Fori(0, NB // 2) as h:
                    for i in range(2):
                        u = G.use(i, h, 2)
                        pe.wait_ge(u.free, u.n)
                        product(nc, u.tile[:, 0:n_ag], tokens(chip.hT, h * 2 + i),
                                columns(chip.weight(ag_slot), 0, n_ag), CH).then_inc(u.full, 1)
                    for i in range(2):
                        y = Y.use(i, h, 2)
                        pe.wait_ge(y.free, y.n)
                        product(nc, y.tile[:], tokens(chip.hT, h * 2 + i), columns(chip.weight(base_slot)), CH,
                                stop=False)
                    for i in range(2):
                        t = T.use(i, h, 2)
                        pe.wait_ge(hw_ready, h * 2 + i + 1)
                        pe.wait_ge(t.free, t.n)
                        turn(chip, t.tile, bufs[i]["hw"], 1).then_inc(t.full, 1)
                    for i in range(2):
                        t, y = T.use(i, h, 2), Y.use(i, h, 2)
                        pe.wait_ge(t.free, t.done)
                        product(nc, y.tile[:], lambda half, c, i=i: bufs[i][("hi", "lo")[half]],
                                lambda half, c: (bh, bl)[half], 1, start=False).then_inc(y.full, 1)

            @block.scalar
            def _(act):
                act.wait_ge(got, 48)
                nc.scalar.activation(bh, bst, ACT.Copy).then_inc(b_hi, 1)
                nc.scalar.activation(thr[:, 2:3], thr[:, 0:1], ACT.Copy, scale=-1.0).then_inc(nthr, 1)
                act.wait_ge(nthr, 1)
                with nc.scalar.Fori(0, NB // 2) as h:
                    for i in range(2):
                        hg = bufs[i]["hg"]
                        act.wait_ge(chain, (h * 2 + i) * CHAIN + 2)
                        nc.scalar.activation(bufs[i]["e"], hg[:, P:P + NE], ACT.Exp, bias=col(i, 0),
                                             accum_out=col(i, 1))
                        nc.scalar.activation(col(i, 2), hg[:, P + NE:P + NE + 1], ACT.Exp, bias=thr[:, 2:3],
                                             scale=-1.0).then_inc(expo, 1)
                    for i in range(2):
                        t = T.use(i, h, 2)
                        act.wait_ge(t.full, t.n)
                        nc.scalar.activation(bufs[i]["hi"], t.tile[:, 0:P], ACT.Copy).then_inc(hw_hi, 1)

            @block.vector
            def _(dve):
                dve.wait_ge(b_hi, 1)
                nc.vector.tensor_tensor(bl, bst, bh, ALU.subtract).then_inc(b_lo, 1)
                with nc.vector.Fori(0, NB // 2) as h:
                    for i in range(2):
                        count = [0]

                        def link(ins, k=h * 2 + i, count=count):
                            count[0] += 1
                            ins.then_inc(chain, 1)
                            dve.wait_ge(chain, k * CHAIN + count[0])

                        u, t = G.use(i, h, 2), bufs[i]
                        dve.wait_ge(u.full, u.n)
                        link(nc.vector.tensor_copy(t["hg"][:, 0:n_ag], u.tile[:, 0:n_ag]))
                        dve.sem_inc(u.free, 1)
                        link(nc.vector.tensor_reduce(col(i, 0), t["hg"][:, P:P + NE], AX, ALU.max, negate=True))
                        dve.wait_ge(expo, h * 2 + i + 1)
                        link(nc.vector.tensor_scalar(col(i, 2), col(i, 2), 8.0, 8.0, ALU.mult, ALU.add))
                        link(nc.vector.reciprocal(col(i, 2), col(i, 2)))
                        link(nc.vector.reciprocal(col(i, 3), col(i, 1)))
                        link(nc.vector.tensor_scalar(t["w"], t["e"], col(i, 3), col(i, 2), ALU.mult, ALU.subtract))
                        link(nc.vector.tensor_scalar(t["w2"], t["w"], 0.0, None, ALU.max, ALU.add,
                                                     accum_out=col(i, 4)))
                        link(nc.vector.tensor_scalar(col(i, 5), col(i, 4), 0.0, None, ALU.is_equal))
                        link(nc.vector.tensor_tensor(col(i, 4), col(i, 4), col(i, 5), ALU.add))
                        link(nc.vector.reciprocal(col(i, 4), col(i, 4)))
                        link(nc.vector.tensor_scalar(t["w2"], t["w2"], col(i, 4), 2.0, ALU.mult, ALU.mult))
                        assert count[0] == CHAIN
                        nc.vector.tensor_tensor(heads(t["hw"], NE), heads(t["hg"][:, 0:P], NE),
                                                spread(t["w2"], NE, RANK), ALU.mult).then_inc(hw_ready, 1)
                    for i in range(2):
                        t = T.use(i, h, 2)
                        dve.wait_ge(hw_hi, h * 2 + i + 1)
                        nc.vector.tensor_tensor(bufs[i]["lo"], t.tile[:, 0:P], bufs[i]["hi"],
                                                ALU.subtract).then_inc(t.free, 1)
                    for i in range(2):
                        y = Y.use(i, h, 2)
                        at = bass.ds((h * 2 + i) * D, D)
                        dve.wait_ge(x_b, h * 2 + i + 1)
                        dve.wait_ge(y.full, y.n)
                        nc.vector.tensor_tensor(chip.x[:, at], chip.x[:, at], y.tile[:], ALU.add).then_inc(y.free, 1)


def last_cross_views(chip):
    q_hi, q_lo, k_hi, k_lo, rest = carve(chip.big, [(CH * NB * P, F16)] * 4 + [(8192, F32)])
    return (q_hi, q_lo), (k_hi, k_lo), rest


def last_cross_projections(chip, q_slot, k_slot):
    nc, io = chip.nc, chip.io
    q, k, rest = last_cross_views(chip)
    bias = rest[:, 0:2 * CH]
    WIDE = NB * P
    todo = [(out, slot, src, first + tile, tile, part)
            for out, slot, src, first in ((k, k_slot, chip.cT, CH), (q, q_slot, chip.hT, 0))
            for tile in range(CH) for part in range(2)]
    with chip.begin():
        A = Ring("A", chip.psum[0:4], chip.sem)
        got, hi = chip.sem("got"), chip.sem("hi")
        with nc.Block() as block:

            @block.sync
            def _(sp):
                sp.dma_start(bias, io["cross_bias"]).then_inc(got, 16)

            @block.gpsimd
            def _(pool):
                A.credit(pool)

            @block.tensor
            def _(pe):
                for n, (_, slot, src, _, tile, part) in enumerate(todo):
                    a = A.use(n)
                    w = chip.weight(slot)
                    pe.wait_ge(a.free, a.n)

                    def batches(half, c, src=src, part=part):
                        rows = src[half][:].rearrange("p (b c t) -> p b c t", b=NB, c=CH)
                        return rows[:, part * (NB // 2):(part + 1) * (NB // 2), c, :]

                    product(nc, a.tile[:], lambda half, c, w=w, t=tile: w[half][:, c * D + t * P:c * D + (t + 1) * P],
                            batches, CH).then_inc(a.full, 1)

            @block.scalar
            def _(act):
                act.wait_ge(got, 16)
                for n, (out, _, _, b, tile, part) in enumerate(todo):
                    a = A.use(n)
                    at = slice(tile * WIDE + part * D, tile * WIDE + (part + 1) * D)
                    act.wait_ge(a.full, a.n)
                    nc.scalar.activation(out[0][:, at], a.tile[:], ACT.Identity, bias=bias[:, b:b + 1]).then_inc(hi, 1)

            @block.vector
            def _(dve):
                dve.wait_ge(got, 16)
                for n, (out, _, _, b, tile, part) in enumerate(todo):
                    a = A.use(n)
                    at = slice(tile * WIDE + part * D, tile * WIDE + (part + 1) * D)
                    dve.wait_ge(hi, n + 1)
                    nc.vector.scalar_tensor_tensor(out=out[1][:, at], in0=a.tile[:], scalar=bias[:, b:b + 1],
                                                   in1=out[0][:, at], op0=ALU.add, op1=ALU.subtract).then_inc(a.free, 1)


def last_cross_attention(chip):
    nc, io = chip.nc, chip.io
    q, k, rest = last_cross_views(chip)
    WIDE = NB * P
    cst, ch, cl = carve(rest, [(2 * D, F32), (2 * D, F16), (2 * D, F16)])
    prob, ph, pl, nmax, nm, rs, ri = carve(chip.small, [
        (2 * P, F32), (2 * P, F16), (2 * P, F16), (2, F32), (2, F32), (2, F32), (2, F32)])
    scale = float(np.float32(1.0) / np.sqrt(np.float32(D)))
    with chip.begin():
        sem = chip.sem
        S = Ring("S", chip.psum[0:2], sem)
        T = Ring("T", chip.psum[2:4], sem)
        Y = Ring("Y", chip.psum[4:6], sem)
        C = Ring("C", [cst[:, i * D:(i + 1) * D] for i in range(2)], sem)
        c_hi, c_lo, maxed, scaled, prob_ready, p_hi, inv = (
            sem(n) for n in ("ctx_hi", "ctx_lo", "maxed", "scaled", "prob_ready", "p_hi", "inv"))
        with nc.Block() as block:

            @block.sync
            def _(sp):
                with nc.sync.Fori(0, NB // 2) as h:
                    for i in range(2):
                        c = C.use(i, h, 2)
                        sp.wait_ge(c.free, c.n)
                        sp.dma_start(c.tile, io["ctx"][bass.ds(h * 2 + i, 1), :, :].rearrange("o p n -> p (o n)")
                                     ).then_inc(c.full, 16)

            @block.gpsimd
            def _(pool):
                for ring in (S, T, Y, C):
                    ring.credit(pool)
                with nc.gpsimd.Fori(0, NB // 2) as h:
                    for i in range(2):
                        c = C.use(i, h, 2)
                        at = slice(i * D, (i + 1) * D)
                        pool.wait_ge(c_hi, h * 2 + i + 1)
                        nc.gpsimd.tensor_tensor(cl[:, at], c.tile, ch[:, at], ALU.subtract).then_inc(c.free, 1)

            @block.tensor
            def _(pe):
                with nc.tensor.Fori(0, NB // 2) as h:
                    for i in range(2):
                        s = S.use(i, h, 2)
                        pe.wait_ge(s.free, s.n)
                        b = h * 2 + i
                        product(nc, s.tile[:, 0:P], lambda half, c, b=b: q[half][:, bass.ds(b * P + c * WIDE, P)],
                                lambda half, c, b=b: k[half][:, bass.ds(b * P + c * WIDE, P)], CH).then_inc(s.full, 1)
                    for i in range(2):
                        t = T.use(i, h, 2)
                        pe.wait_ge(prob_ready, h * 2 + i + 1)
                        pe.wait_ge(t.free, t.n)
                        turn(chip, t.tile, prob[:, i * P:(i + 1) * P], 1).then_inc(t.full, 1)
                    for i in range(2):
                        t, y, c = T.use(i, h, 2), Y.use(i, h, 2), C.use(i, h, 2)
                        pe.wait_ge(t.free, t.done)
                        pe.wait_ge(c.free, c.done)
                        pe.wait_ge(y.free, y.n)
                        product(nc, y.tile[:], lambda half, c, i=i: (ph, pl)[half][:, i * P:(i + 1) * P],
                                lambda half, c, i=i: (ch, cl)[half][:, i * D:(i + 1) * D], 1).then_inc(y.full, 1)

            @block.scalar
            def _(act):
                with nc.scalar.Fori(0, NB // 2) as h:
                    for i in range(2):
                        c, y = C.use(i, h, 2), Y.use(i, h, 2)
                        act.wait_ge(c.full, (c.n) * 16)
                        act.wait_ge(y.free, y.n)
                        nc.scalar.activation(ch[:, i * D:(i + 1) * D], c.tile, ACT.Copy).then_inc(c_hi, 1)
                    for i in range(2):
                        s = S.use(i, h, 2)
                        act.wait_ge(scaled, h * 2 + i + 1)
                        nc.scalar.activation(prob[:, i * P:(i + 1) * P], s.tile[:, 0:P], ACT.Exp, bias=nm[:, i:i + 1],
                                             scale=scale, accum_out=rs[:, i:i + 1]).then_inc(prob_ready, 1)
                    for i in range(2):
                        t = T.use(i, h, 2)
                        act.wait_ge(t.full, t.n)
                        nc.scalar.activation(ph[:, i * P:(i + 1) * P], t.tile[:, 0:P], ACT.Copy).then_inc(p_hi, 1)

            @block.vector
            def _(dve):
                with nc.vector.Fori(0, NB // 2) as h:
                    for i in range(2):
                        s = S.use(i, h, 2)
                        dve.wait_ge(s.full, s.n)
                        nc.vector.tensor_reduce(nmax[:, i:i + 1], s.tile[:, 0:P], AX, ALU.max,
                                                negate=True).then_inc(maxed, 1)
                        dve.wait_ge(maxed, h * 2 + i + 1)
                        nc.vector.tensor_scalar(nm[:, i:i + 1], nmax[:, i:i + 1], scale, None, ALU.mult).then_inc(scaled, 1)
                    for i in range(2):
                        s, t = S.use(i, h, 2), T.use(i, h, 2)
                        dve.wait_ge(p_hi, h * 2 + i + 1)
                        nc.vector.tensor_tensor(pl[:, i * P:(i + 1) * P], t.tile[:, 0:P], ph[:, i * P:(i + 1) * P],
                                                ALU.subtract).then_inc(t.free, 1)
                        dve.sem_inc(s.free, 1)
                        nc.vector.reciprocal(ri[:, i:i + 1], rs[:, i:i + 1]).then_inc(inv, 1)
                    for i in range(2):
                        y = Y.use(i, h, 2)
                        at = bass.ds((h * 2 + i) * D, D)
                        dve.wait_ge(inv, h * 2 + i + 1)
                        dve.wait_ge(y.full, y.n)
                        nc.vector.scalar_tensor_tensor(out=chip.x[:, at], in0=y.tile[:], scalar=ri[:, i:i + 1],
                                                       in1=chip.x[:, at], op0=ALU.mult, op1=ALU.add).then_inc(y.free, 1)


def sign_projection(chip, slot):
    nc, io = chip.nc, chip.io
    out, s, t = carve(chip.big, [(NB * D, F32), (4, F32), (4, F32)])
    with chip.begin():
        sem = chip.sem
        A = Ring("A", chip.psum[2:4], sem)
        T = Ring("T", chip.psum[0:2], sem)
        norm = Norm(chip, sem)
        got, steps, soft, written = (sem(n) for n in ("got", "steps", "softplus", "written"))
        with nc.Block() as block:

            @block.sync
            def _(sp):
                sp.dma_start(s[:, 0:2], io["vectors"][V_SCALE:V_SCALE + 1, 0:2].partition_broadcast(P)).then_inc(got, 16)
                with nc.sync.Fori(0, NB // 2) as h:
                    for i in range(2):
                        a = A.use(i, h, 2)
                        sp.wait_ge(a.free, a.done)
                        at = bass.ds((h * 2 + i) * D, D)
                        sp.dma_start(io["out"][:, at], out[:, at]).then_inc(written, 16)
                sp.wait_ge(written, 16 * NB)

            @block.gpsimd
            def _(pool):
                A.credit(pool)
                T.credit(pool)
                with nc.gpsimd.Fori(0, NB) as b:
                    norm.root(pool, b)

            @block.tensor
            def _(pe):
                def normal(h, i):
                    norm.turn(pe, h * 2 + i, T.use(i, h, 2))

                with nc.tensor.Fori(0, NB // 2) as h:
                    for i in range(2):
                        normal(h, i)
                    for i in range(2):
                        t_, a = T.use(i, h, 2), A.use(i, h, 2)
                        pe.wait_ge(t_.free, t_.done)
                        pe.wait_ge(a.free, a.n)
                        product(nc, a.tile[:], tokens(chip.hT, h * 2 + i), columns(chip.weight(slot)),
                                CH).then_inc(a.full, 1)

            @block.scalar
            def _(act):
                act.wait_ge(got, 16)
                nc.scalar.activation(t[:, 0:1], s[:, 0:1], ACT.Abs).then_inc(steps, 1)
                act.wait_ge(steps, 1)
                nc.scalar.activation(t[:, 1:2], t[:, 0:1], ACT.Exp, scale=-1.0).then_inc(steps, 1)
                act.wait_ge(steps, 2)
                nc.scalar.activation(t[:, 2:3], t[:, 1:2], ACT.Ln, bias=1.0).then_inc(steps, 1)
                with nc.scalar.Fori(0, NB // 2) as h:
                    for i in range(2):
                        norm.split_hi(act, h * 2 + i, T.use(i, h, 2))

            @block.vector
            def _(dve):
                dve.wait_ge(steps, 3)
                nc.vector.tensor_scalar(s[:, 2:3], s[:, 0:1], 0.0, t[:, 2:3], ALU.max, ALU.add).then_inc(soft, 1)
                dve.wait_ge(soft, 1)
                with nc.vector.Fori(0, NB // 2) as h:
                    for i in range(2):
                        b = h * 2 + i
                        norm.stats(dve, b, b)
                        norm.scale(dve, b, b)
                        norm.split_lo(dve, b, b, T.use(i, h, 2))
                    for i in range(2):
                        a = A.use(i, h, 2)
                        at = bass.ds((h * 2 + i) * D, D)
                        dve.wait_ge(a.full, a.n)
                        nc.vector.scalar_tensor_tensor(out=out[:, at], in0=a.tile[:], scalar=s[:, 2:3],
                                                       in1=chip.x[:, at], op0=ALU.mult, op1=ALU.add).then_inc(a.free, 1)


def decoder(nc, io):
    with ExitStack() as ctx:
        chip = Chip(nc, ctx, io)
        prepare(chip)
        split_weights(chip, [(W_QKVO + i, i) for i in range(4)], [W_XK, W_XK + 1])
        self_attention(chip, 0, {"q": 0, "k": 1, "v": 2, "o": 3})
        split_weights(chip, [(W_XK, 4), (W_XK + 1, 5), (W_XV, 0), (W_XV + 1, 1), (W_XQO, 2), (W_XQO + 1, 3)],
                      [W_XQO + 2, W_XQO + 3])
        cross_keys(chip, (4, 5), (0, 1))
        norm_all(chip)
        cross_attention(chip, (2, 3), (4, 5))
        split_weights(chip, [(W_BASE, 0), (W_AG, 1), (W_L1O, 4), (W_LXQ, 5)], [W_LXK, W_SIGN])
        norm_all(chip)
        experts(chip, 0, 1)
        self_attention(chip, 1, {"q": 2, "k": 3, "o": 4})
        split_weights(chip, [(W_LXK, 0), (W_SIGN, 1)], [])
        norm_all(chip)
        last_cross_projections(chip, 5, 0)
        last_cross_attention(chip)
        sign_projection(chip, 1)


def alibi_table():
    slopes = (1.0 / np.power(2.0, np.arange(1, NH + 1, dtype=np.float32) * (8.0 / NH))).astype(np.float32)
    pos = np.arange(P)
    rel = (pos[None, :] - pos[:, None]).astype(np.float32)
    table = np.empty((P, NG, GH, P), np.float32)
    for g in range(NG):
        for i in range(GH):
            head = ((g // 4) * 4 + i) * 4 + g % 4
            table[:, g, i, :] = np.where(rel <= 0, slopes[head] * rel, np.float32(-1e30))
    return table.reshape(P, NG * GH * P)


def kernel(x, ctx_4096, mask_1x1xSxS2_ff0, L0_attn_Wqkv, L0_attn_q_ln_w, L0_attn_q_ln_b, L0_attn_k_ln_w,
           L0_attn_k_ln_b, L0_attn_Wout, L0_xattn_q_proj_w, L0_xattn_k_proj_w, L0_xattn_v_proj_w, L0_xattn_o_proj_w,
           L0_xattn_q_norm_w, L0_xattn_k_norm_w, L0_ffn_W_base, L0_ffn_b_base, L0_ffn_W_gate, L0_ffn_W_thr,
           L0_ffn_b_thr, L0_ffn_A_w, L0_ffn_B_w, L1_attn_Wq, L1_attn_Wk, L1_attn_Wv, L1_attn_Wo, L1_xattn_Wq,
           L1_xattn_bq, L1_xattn_Wk, L1_xattn_bk, L1_ffn_sign, L1_ffn_scale):
    import concourse.bacc as bacc
    from concourse.bass_utils import run_bass_kernel_spmd

    f32 = np.float32

    def matrix(w_t):
        full = np.zeros((D, D), f32)
        full[:, :w_t.shape[1]] = w_t
        return full.reshape(CH, P, D).transpose(1, 0, 2).reshape(P, MAT)

    a = {n: np.asarray(v) for n, v in locals().items()
         if n not in ("f32", "matrix", "bacc", "run_bass_kernel_spmd")}
    weights = np.empty((N_MATS, P, MAT), f32)
    qkv = a["L0_attn_Wqkv"]
    for i in range(3):
        weights[W_QKVO + i] = matrix(qkv[i * D:(i + 1) * D].T)
    weights[W_QKVO + 3] = matrix(a["L0_attn_Wout"].T)
    for i in range(2):
        weights[W_XK + i] = matrix(a["L0_xattn_k_proj_w"][i * D:(i + 1) * D].T)
        weights[W_XV + i] = matrix(a["L0_xattn_v_proj_w"][i * D:(i + 1) * D].T)
    for g in range(NKV):
        weights[W_XQO + 2 * g] = matrix(a["L0_xattn_q_proj_w"][g * D:(g + 1) * D].T)
        weights[W_XQO + 2 * g + 1] = matrix(a["L0_xattn_o_proj_w"][:, g * D:(g + 1) * D].T)
    weights[W_L1Q] = matrix(a["L1_attn_Wq"].T)
    weights[W_L1KV] = matrix(np.concatenate([a["L1_attn_Wk"], a["L1_attn_Wv"]]).T)
    weights[W_BASE] = matrix(a["L0_ffn_W_base"].T)
    weights[W_AG] = matrix(np.concatenate([a["L0_ffn_A_w"].reshape(NE * RANK, D), a["L0_ffn_W_gate"],
                                           a["L0_ffn_W_thr"][None]]).T)
    weights[W_L1O] = matrix(a["L1_attn_Wo"].T)
    weights[W_LXQ] = matrix(a["L1_xattn_Wq"].T)
    weights[W_LXK] = matrix(a["L1_xattn_Wk"].T)
    weights[W_SIGN] = matrix(a["L1_ffn_sign"])

    vectors = np.zeros((9, D), f32)
    for row, name in ((V_QW, "L0_attn_q_ln_w"), (V_QB, "L0_attn_q_ln_b"), (V_KW, "L0_attn_k_ln_w"),
                      (V_KB, "L0_attn_k_ln_b"), (V_XQN, "L0_xattn_q_norm_w"), (V_XKN, "L0_xattn_k_norm_w"),
                      (V_BASE, "L0_ffn_b_base"), (V_BTHR, "L0_ffn_b_thr"), (V_SCALE, "L1_ffn_scale")):
        flat = a[name].reshape(-1)
        vectors[row, :flat.size] = flat

    late = np.arange(P) % 32 >= HD
    arrays = {
        "x": a["x"].transpose(1, 0, 2).reshape(P, NB * D),
        "ctxT": a["ctx_4096"].reshape(NB, P, CH, P).transpose(3, 0, 2, 1).reshape(P, NB * D),
        "ctx": a["ctx_4096"],
        "mask": a["mask_1x1xSxS2_ff0"].reshape(P, P),
        "weights": weights,
        "expert_b": a["L0_ffn_B_w"].transpose(0, 2, 1).reshape(P, D),
        "vectors": vectors,
        "cross_bias": np.concatenate([a["L1_xattn_bq"].reshape(CH, P), a["L1_xattn_bk"].reshape(CH, P)]).T,
        "ident": np.eye(P, dtype=f32),
        "half": np.stack([np.where(late, -1, 0), np.where(late, 0, -1)], 1).astype(f32),
        "alibi": alibi_table(),
    }
    nc = bacc.Bacc("TRN2", target_bir_lowering=False, num_devices=1)
    io = {}
    for name, v in arrays.items():
        arrays[name] = np.ascontiguousarray(v)
        io[name] = nc.dram_tensor(f"in_{name}", v.shape, mybir.dt.from_np(v.dtype), kind="ExternalInput").ap()
    io["out"] = nc.dram_tensor("out", (P, NB * D), F32, kind="ExternalOutput").ap()
    decoder(nc, io)
    result = run_bass_kernel_spmd(nc, [{f"in_{name}": v for name, v in arrays.items()}], core_ids=[0])
    return result.results[0]["out"].reshape(P, NB, D).transpose(1, 0, 2)
```

```python
from contextlib import ExitStack

import numpy as np

import concourse.bass as bass
from concourse import mybir

F32 = mybir.dt.float32
F16 = mybir.dt.float16
BF16 = mybir.dt.bfloat16
ALU = mybir.AluOpType
ACT = mybir.ActivationFunctionType
AX = mybir.AxisListType.X

P = 128
NB = 8
D = 512
CH = D // P
MAT = CH * D
EPS = 1e-5
NH = 32
HD = 16
NKV = 8
GH = 4
NG = NH // GH
CLIP = 8.0
PSCALE = 1024.0
NE, RANK = 8, 16
SLOTS = 6

W_QKVO = 0
W_XK, W_XV = 4, 6
W_XQO = 8
W_L1Q, W_L1KV, W_BASE, W_AG, W_L1O, W_LXQ, W_LXK, W_SIGN = range(8 + 2 * NKV, 16 + 2 * NKV)
N_MATS = 16 + 2 * NKV

V_QW, V_QB, V_KW, V_KB, V_XQN, V_XKN, V_BASE, V_BTHR, V_SCALE = range(9)


class Use:

    def __init__(self, slot, tile, full, free, n):
        self.slot, self.tile, self.full, self.free, self.n, self.done = slot, tile, full, free, n, n + 1


class Ring:

    def __init__(self, name, tiles, sem):
        self.tiles = tiles
        self.full = [sem(f"{name}{i}_full") for i in range(len(tiles))]
        self.free = [sem(f"{name}{i}_free") for i in range(len(tiles))]

    def credit(self, eng):
        for s in self.free:
            eng.sem_inc(s, 1)

    def use(self, k, it=0, per=0):
        depth = len(self.tiles)
        assert per % depth == 0
        i = k % depth
        return Use(i, self.tiles[i], self.full[i], self.free[i], it * (per // depth) + (k // depth + 1))


class Chip:

    def __init__(self, nc, ctx, io):
        self.nc, self.io, self.phase = nc, io, 0

        def sb(name, shape, dt=F32):
            return ctx.enter_context(nc.sbuf_tensor(name, shape, dt))

        self.x = sb("x", [P, NB * D])
        self.hT = [sb("hT_hi", [P, NB * D], F16), sb("hT_lo", [P, NB * D], F16)]
        self.cT = [sb("cT_hi", [P, NB * D], F16), sb("cT_lo", [P, NB * D], F16)]
        self.w = [sb("w_hi", [P, SLOTS, MAT], F16), sb("w_lo", [P, SLOTS, MAT], BF16)]
        self.stage = sb("stage", [P, 2, MAT])
        self.ident = sb("ident", [P, P])
        self.half = sb("half", [P, 2])
        self.z = sb("z", [P, 2 * D])
        self.st = sb("st", [P, 6 * NB])
        self.mv = sb("mv", [P, 2 * NB])
        self.ve = sb("ve", [P, NB])
        self.rstd = sb("rstd", [P, NB])
        self.mhalf = sb("mhalf", [P, 8])
        self.big = sb("big", [P, 16384])
        self.small = sb("small", [P, 5632])
        self.psum = [ctx.enter_context(nc.psum_tensor(f"bank{i}", [P, 512], F32)) for i in range(8)]
        self.loaded = ctx.enter_context(nc.semaphore("loaded"))
        self.staged = [ctx.enter_context(nc.semaphore(f"staged{i}")) for i in range(2)]
        self.n_staged = [0, 0]

    def sem(self, name):
        return self.nc.alloc_semaphore(f"{name}_{self.phase}")

    def begin(self):
        self.phase += 1
        return self.nc.cleanup_on_exit()

    def load_weight(self, eng, mat, buf):
        self.n_staged[buf] += 16
        eng.dma_start(self.stage[:, buf, :], self.io["weights"][mat]).then_inc(self.staged[buf], 16)

    def weight(self, slot):
        return [self.w[0][:, slot, :], self.w[1][:, slot, :]]


def carve(region, shapes):
    at, out = 0, []
    for cols, dt in shapes:
        words = cols if dt == F32 else cols // 2
        v = region[:, at:at + words]
        out.append(v if dt == F32 else v.bitcast(dt))
        at += words
    assert at <= region.shape[1], (at, region.shape)
    return out


def product(nc, out, lhs, rhs, chunks, start=True, stop=True):
    n = 0
    for c in range(chunks):
        for a, b in ((0, 0), (0, 1), (1, 0)):
            last = nc.tensor.matmul(out, lhs(a, c), rhs(b, c), start=start and n == 0,
                                    stop=stop and n == 3 * chunks - 1)
            n += 1
    return last


def tokens(pair, b):
    return lambda half, c: pair[half][:, bass.ds(b * D + c * P, P)]


def columns(pair, first=0, n=D):
    return lambda half, c: pair[half][:, c * D + first:c * D + first + n]


def turn(chip, bank, src, n=4):
    for i in range(n):
        last = chip.nc.tensor.transpose(bank[:, i * P:(i + 1) * P], src[:, i * P:(i + 1) * P], chip.ident[:])
    return last


def heads(ap, n=GH):
    return ap.rearrange("p (h k) -> p h k", h=n)


def spread(ap, n, m):
    return ap.unsqueeze(2).to_broadcast([P, n, m])


class Norm:

    def __init__(self, chip, sem, turns):
        self.chip, self.turns = chip, turns
        self.stats_done, self.var, self.rstd, self.z, self.hi = (
            sem(f"norm_{n}") for n in ("stats", "var", "rstd", "z", "hi"))

    def use(self, b, it=0, per=0):
        return self.turns.use(b, it, per)

    def stats(self, dve):
        nc, c = self.chip.nc, self.chip
        for b in range(NB):
            nc.vector.bn_stats(c.st[:, 6 * b:6 * b + 6], c.x[:, b * D:(b + 1) * D]).then_inc(self.stats_done, 1)
        for b in range(NB):
            dve.wait_ge(self.stats_done, b + 1)
            nc.vector.bn_aggr(c.mv[:, 2 * b:2 * b + 2], c.st[:, 6 * b:6 * b + 6]).then_inc(self.stats_done, 1)
        dve.wait_ge(self.stats_done, 2 * NB)
        var = c.mv[:].rearrange("p (b k) -> p b k", k=2)[:, :, 1]
        nc.vector.tensor_scalar(c.ve[:], var, EPS, None, ALU.add).then_inc(self.var, 1)

    def root(self, pool):
        c = self.chip
        pool.wait_ge(self.var, 1)
        c.nc.gpsimd.tensor_tensor(c.rstd[:], c.ve[:], c.mhalf[:], ALU.pow).then_inc(self.rstd, 1)

    def scale(self, dve, b):
        c = self.chip
        dve.wait_ge(self.rstd, 1)
        z = c.z[:, (b % 2) * D:(b % 2 + 1) * D]
        c.nc.vector.tensor_scalar(z, c.x[:, b * D:(b + 1) * D], c.mv[:, 2 * b:2 * b + 1], c.rstd[:, b:b + 1],
                                  ALU.subtract, ALU.mult).then_inc(self.z, 1)

    def turn(self, pe, b):
        t = self.use(b)
        pe.wait_ge(self.z, b + 1)
        pe.wait_ge(t.free, t.n)
        turn(self.chip, t.tile, self.chip.z[:, (b % 2) * D:(b % 2 + 1) * D]).then_inc(t.full, 1)

    def split_hi(self, act, b):
        c, t = self.chip, self.use(b)
        act.wait_ge(t.full, t.n)
        c.nc.scalar.activation(c.hT[0][:, b * D:(b + 1) * D], t.tile[:], ACT.Copy).then_inc(self.hi, 1)

    def split_lo(self, dve, b):
        c, t = self.chip, self.use(b)
        dve.wait_ge(self.hi, b + 1)
        at = slice(b * D, (b + 1) * D)
        c.nc.vector.tensor_tensor(c.hT[1][:, at], t.tile[:], c.hT[0][:, at], ALU.subtract).then_inc(t.free, 1)

    def vector_rows(self, dve):
        self.scale(dve, 0)
        for b in range(NB):
            if b + 1 < NB:
                self.scale(dve, b + 1)
            self.split_lo(dve, b)


class Splitting:

    def __init__(self, chip, sem, slot, parts=NB):
        self.chip, self.slot, self.width = chip, slot, 2 * MAT // parts
        self.hi, self.done = sem("bg_hi"), sem("bg_done")
        self.staged = list(chip.n_staged)
        self.parts = parts

    def columns(self, t, it):
        flat = t.rearrange("p s n -> p (s n)")
        return flat[:, bass.ds(it * self.width + self.slot * MAT, self.width)]

    def source(self, it):
        return self.chip.stage[:].rearrange("p s n -> p (s n)")[:, bass.ds(it * self.width, self.width)]

    def split_hi(self, act, it):
        c = self.chip
        c.nc.scalar.activation(self.columns(c.w[0], it), self.source(it), ACT.Copy).then_inc(self.hi, 1)

    def split_lo(self, pool, it):
        c = self.chip
        pool.wait_ge(self.hi, it + 1)
        c.nc.gpsimd.tensor_tensor(self.columns(c.w[1], it), self.source(it), self.columns(c.w[0], it),
                                  ALU.subtract).then_inc(self.done, 1)

    def wait_staged(self, act):
        for i in range(2):
            act.wait_ge(self.chip.staged[i], self.staged[i])

    def prefetch(self, sp, mats):
        for i, mat in enumerate(mats):
            sp.wait_ge(self.done, (i + 1) * self.parts // 2)
            self.chip.load_weight(sp, mat, i)


def begin_layer(chip, plan, prefetch, start=False):
    nc, io = chip.nc, chip.io
    cut = MAT // 2
    cstage = chip.big[:, 0:NB * D]
    with chip.begin():
        sem = chip.sem
        T = Ring("T", chip.psum[0:2], sem)
        norm = Norm(chip, sem, T)
        hi, lo_dve, lo_pool, ctx_in, ctx_hi, const = (
            sem(n) for n in ("weight_hi", "weight_lo_dve", "weight_lo_pool", "ctx_in", "ctx_hi", "const"))
        at = [n if not start else 0 for n in chip.n_staged]
        due = []
        for i in range(len(plan)):
            if i >= 2 or start:
                at[i % 2] += 16
            due.append(at[i % 2])
        with nc.Block() as block:

            @block.sync
            def _(sp):
                if start:
                    for h in range(2):
                        part = slice(h * NB // 2 * D, (h + 1) * NB // 2 * D)
                        sp.dma_start(chip.x[:, part], io["x"][:, part]).then_inc(chip.loaded, 16)
                    sp.dma_start(chip.ident[:], io["ident"]).then_inc(chip.loaded, 16)
                    sp.dma_start(chip.half[:], io["half"]).then_inc(chip.loaded, 16)
                    for i in range(2):
                        chip.load_weight(sp, plan[i][0], i)
                    sp.dma_start(cstage, io["ctxT"]).then_inc(ctx_in, 16)
                for i, mat in enumerate([m for m, _ in plan[2:]] + prefetch):
                    sp.wait_ge(lo_dve, i + 1)
                    sp.wait_ge(lo_pool, i + 1)
                    chip.load_weight(sp, mat, i % 2)

            @block.tensor
            def _(pe):
                if start:
                    pe.wait_ge(chip.loaded, 64)
                for b in range(NB):
                    norm.turn(pe, b)

            @block.scalar
            def _(act):
                def weight(i):
                    act.wait_ge(chip.staged[i % 2], due[i])
                    nc.scalar.activation(chip.w[0][:, plan[i][1], :], chip.stage[:, i % 2, :], ACT.Copy).then_inc(hi, 1)

                for i in range(min(2, len(plan))):
                    weight(i)
                for b in range(NB):
                    norm.split_hi(act, b)
                for i in range(2, len(plan)):
                    weight(i)
                if start:
                    act.wait_ge(ctx_in, 16)
                    nc.scalar.activation(chip.cT[0][:], cstage, ACT.Copy).then_inc(ctx_hi, 1)

            @block.vector
            def _(dve):
                if start:
                    dve.wait_ge(chip.loaded, 64)
                norm.stats(dve)
                norm.vector_rows(dve)
                for i, (_, slot) in enumerate(plan):
                    dve.wait_ge(hi, i + 1)
                    nc.vector.tensor_tensor(chip.w[1][:, slot, 0:cut], chip.stage[:, i % 2, 0:cut],
                                            chip.w[0][:, slot, 0:cut], ALU.subtract).then_inc(lo_dve, 1)
                if start:
                    dve.wait_ge(ctx_hi, 1)
                    nc.vector.tensor_tensor(chip.cT[1][:], cstage, chip.cT[0][:], ALU.subtract)

            @block.gpsimd
            def _(pool):
                T.credit(pool)
                if start:
                    nc.gpsimd.memset(chip.mhalf[:], -0.5).then_inc(const, 1)
                    pool.wait_ge(const, 1)
                norm.root(pool)
                for i, (_, slot) in enumerate(plan):
                    pool.wait_ge(hi, i + 1)
                    nc.gpsimd.tensor_tensor(chip.w[1][:, slot, cut:], chip.stage[:, i % 2, cut:],
                                            chip.w[0][:, slot, cut:], ALU.subtract).then_inc(lo_pool, 1)


SELF_ORDER = """
    scores_2 probs_0 exp_2 +q_0 +q_1 p_lo_0 +q_2
    scores_3 probs_1 exp_3 +q_3 pv_0 p_lo_1 +q_take_0 +k_0 +k_1
    scores_4 probs_2 exp_4 pv_1 p_lo_2 +k_2 +q_norm_0 +k_3 +k_take_0
    scores_5 probs_3 exp_5 pv_2 p_lo_3 +v_0 +k_norm_0
    scores_6 probs_4 exp_6 pv_3 p_lo_4 +q_turn_0 +v_1 +q_stack_0 +q_norm_1
    scores_7 probs_5 exp_7 pv_4 p_lo_5 o_take_0 +k_turn_0 +v_2 out_turn_0 +k_stack_0 +k_norm_1
    +scores_0 probs_6 +exp_0 pv_5 p_lo_6 out_lo_0 +q_turn_1 +v_3 +q_stack_1 out_0
    +scores_1 probs_7 +exp_1 pv_6 p_lo_7 +v_clip_0 out_1 pv_7 o_take_1 +k_turn_1 out_turn_1 +k_stack_1 +v_take_0
    out_lo_1 out_2 out_3 out_take_0
"""
SELF_FRONT = """
    q_0 q_1 q_2 q_3 q_take_0 k_0 k_1 k_2 k_3 k_take_0 q_norm_0 k_norm_0 v_0 v_1 v_2 v_3 v_clip_0 v_take_0 q_norm_1
    k_norm_1 q_turn_0 k_turn_0 q_stack_0 k_stack_0 scores_0 exp_0 q_turn_1 k_turn_1 scores_1 exp_1 q_stack_1 k_stack_1
"""


def stages(text):
    return [(w.lstrip("+").rpartition("_")[0], int(w[-1]), w[0] == "+") for w in text.split()]


def turned(what, n):
    return {"q_turn": [f"q{n}"], "k_turn": [f"k{n}"], "probs": [f"p{n}"], "out_turn": [f"out{n}"]}.get(what, [])


def self_attention(chip, layer, slots):
    nc, io = chip.nc, chip.io
    first = layer == 0
    nkv = NH if first else NKV
    tiles_t = NH // GH
    bias, qd, kd, qc, kc, qw, kw, rows_, sB, prob, hold, pT_hi, pT_lo = carve(chip.big, [
        (NG * 512, F32), (1024, F32), (1024, F32), (512, F32), (512, F32), (512, F32), (512, F32), (2048, F32),
        (2048, F32), (2048, F32), (1024, F16), (1024, F16), (1024, F16)])
    o, oh, ol, nmax, rinv, qst, qmv, qve, qrs, qS, kT_, kS_, vc, v_hi, v_lo = carve(chip.small, [
        (512, F32), (512, F16), (512, F16), (16, F32), (32, F32), (12, F32), (4, F32), (2, F32), (2, F32),
        (1024, F16), (1024, F16), (1024, F16), (512, F32), (NH * 17, F16), (NH * 17, BF16)])
    pT, v_aug = (pT_hi, pT_lo), (v_hi, v_lo)
    group = [[((g // 4) * 4 + i, g % 4, ((g // 4) * 4 + i) * 4 + g % 4) for i in range(GH)] for g in range(NG)]
    raw = {"q": (qc, qw, qd, 0), "k": (kc, kw, kd, 1)}
    q_pair, stackT, stackS = qS, kT_, kS_
    front, order = stages(SELF_FRONT), stages(SELF_ORDER)
    front_T = [u for what, n, _ in front for u in turned(what, n)]
    body_T = [u for what, n, _ in order for u in turned(what, n)]
    last_T = [u for what, n, ahead in order if not ahead for u in turned(what, n)]
    front_A, body_A, last_A = ["q", "k", "v"], ["q", "k", "v", "out"], ["out"]

    with chip.begin():
        sem = chip.sem
        A = Ring("A", chip.psum[0:2], sem)
        T = Ring("T", chip.psum[2:4], sem)
        S = Ring("S", chip.psum[4:6], sem)
        O = Ring("O", chip.psum[6:8], sem)
        qk_chain, qk_var, qk_rstd, qk_z, qk_w, qk_ready = (
            sem(n) for n in ("qk_chain", "qk_var", "qk_rstd", "qk_z", "qk_w", "qk_ready"))
        stacked, v_clipped, v_hi_ready, v_ready, carrier = (
            sem(n) for n in ("stacked", "v_clipped", "v_hi_ready", "v_ready", "carrier"))
        held, maxed, prob_ready, p_hi, summed, o_hi, prepared = (
            sem(n) for n in ("held", "maxed", "prob_ready", "p_hi", "summed", "o_hi", "prepared"))

        def place(ahead, body, last, where, name):
            if where == "ahead":
                return ahead.index(name)
            if where == "body":
                return len(ahead) + body.index(name)
            return len(ahead) + (NB - 1) * len(body) + last.index(name)

        def t_use(where, name, it):
            return T.use(place(front_T, body_T, last_T, where, name), it, len(body_T) if where == "body" else 0)

        def a_use(where, name, it):
            return A.use(place(front_A, body_A, last_A, where, name), it, len(body_A) if where == "body" else 0)

        def schedule(eng, step):
            for what, g, _ in front:
                step("ahead", what, g, 0, 0)
            with eng.Fori(0, NB - 1) as it:
                for what, g, ahead in order:
                    step("body", what, g, it + 1 if ahead else it, it)
            for what, g, ahead in order:
                if not ahead:
                    step("last", what, g, NB - 1, 0)

        def values(t):
            return t[:, 0:nkv * 17].rearrange("p (h k) -> p h k", k=17)[:, :, 0:HD]

        clipped = vc[:, 0:nkv * HD].rearrange("p (h k) -> p h k", k=HD)

        with nc.Block() as block:

            @block.sync
            def _(sp):
                if first:
                    for i, row in enumerate((V_QW, V_QB, V_KW, V_KB)):
                        sp.dma_start(rows_[:, i * D:(i + 1) * D],
                                     io["vectors"][row:row + 1, :].partition_broadcast(P)).then_inc(prepared, 16)
                    sp.dma_start(bias, io["alibi"]).then_inc(prepared, 16)

            @block.gpsimd
            def _(pool):
                for ring in (A, T, S, O):
                    ring.credit(pool)
                nc.gpsimd.memset(v_hi, 1.0).then_inc(prepared, 1)
                nc.gpsimd.memset(v_lo, 0.0).then_inc(prepared, 1)
                if first:
                    pool.wait_ge(prepared, 82)
                    nc.gpsimd.tensor_scalar(rows_[:, 0:2 * D], rows_[:, 0:2 * D], HD ** -0.5, 1.0, ALU.mult,
                                            ALU.mult).then_inc(prepared, 1)
                    pool.wait_ge(prepared, 83)

                def step(where, what, g, b, it):
                    if first and what in ("q_take", "k_take"):
                        i = raw[what[0]][3]
                        pool.wait_ge(qk_var, b * 2 + i + 1)
                        nc.gpsimd.tensor_tensor(qrs[:, i:i + 1], qve[:, i:i + 1], chip.mhalf[:, 0:1],
                                                ALU.pow).then_inc(qk_rstd, 1)
                    if first and what in ("q_norm", "k_norm"):
                        c, w, d, i = raw[what[0]]
                        half = slice(g * 256, (g + 1) * 256)
                        pool.wait_ge(qk_z, b * 2 + i + 1)
                        weight, shift = (rows_[:, (2 * i + j) * D:(2 * i + j + 1) * D][:, half] for j in range(2))
                        nc.gpsimd.tensor_tensor(w[:, half], c[:, half], weight, ALU.mult).then_inc(qk_w, 1)
                        pool.wait_ge(qk_w, b * 4 + 2 * g + i + 1)
                        twice = lambda ap: ap.rearrange("p (h k) -> p h k", k=HD).unsqueeze(2).to_broadcast([P, 16, 2, HD])
                        out = d[:, g * 512:(g + 1) * 512].rearrange("p (h s k) -> p h s k", s=2, k=HD)
                        nc.gpsimd.tensor_tensor(out, twice(w[:, half]), twice(shift), ALU.add).then_inc(qk_ready, 1)
                    if what == "v_take":
                        pool.wait_ge(v_hi_ready, b + 1)
                        nc.gpsimd.tensor_tensor(values(v_lo), clipped, values(v_hi), ALU.subtract).then_inc(v_ready, 1)

                schedule(nc.gpsimd, step)

            @block.tensor
            def _(pe):
                def step(where, what, g, b, it):
                    if what in ("q", "k", "v"):
                        a = a_use(where, what, it)
                        if g == 0:
                            pe.wait_ge(a.free, a.n)
                        first_col, width = (0, D) if first or what == "q" else (0 if what == "k" else P, P)
                        w = columns(chip.weight(slots[what]), g * D + first_col, width)
                        last = product(nc, a.tile[:, 0:width], lambda half, c: tokens(chip.hT, b)(half, g), w, 1,
                                       start=g == 0, stop=g == CH - 1)
                        if g == CH - 1:
                            last.then_inc(a.full, 1)
                    if what in ("q_turn", "k_turn"):
                        d, i = raw[what[0]][2:]
                        if first:
                            pe.wait_ge(qk_ready, b * 4 + 2 * g + i + 1)
                        else:
                            a = a_use(where, what[0], it)
                            pe.wait_ge(a.free, a.done)
                        t = t_use(where, f"{what[0]}{g}", it)
                        pe.wait_ge(t.free, t.n)
                        turn(chip, t.tile, d[:, g * 512:(g + 1) * 512]).then_inc(t.full, 1)
                    if what == "scores":
                        if g % 4 == 0:
                            pe.wait_ge(stacked, b * 2 + g // 4 + 1)
                        s = S.use(g, b, NG)
                        if first:
                            pe.wait_ge(s.free, s.n)
                        elif where != "ahead":
                            pe.wait_ge(prob_ready, b * NG + g - 1)
                        for i, (tile, rg, _) in enumerate(group[g]):
                            at = slice(32 * rg, 32 * rg + 32)
                            lhs = q_pair[at, tile * P:(tile + 1) * P]
                            nc.tensor.matmul(s.tile[:, i * P:(i + 1) * P], lhs, stackT[at, tile * P:(tile + 1) * P],
                                             start=True, stop=False)
                            last = nc.tensor.matmul(s.tile[:, i * P:(i + 1) * P], lhs,
                                                    stackS[at, tile * P:(tile + 1) * P], start=False, stop=True)
                        last.then_inc(s.full, 1)
                    if what == "probs":
                        pe.wait_ge(prob_ready, b * NG + g + 1)
                        t = t_use(where, f"p{g}", it)
                        pe.wait_ge(t.free, t.n)
                        turn(chip, t.tile, prob[:, (g % 4) * 512:(g % 4 + 1) * 512]).then_inc(t.full, 1)
                    if what == "pv":
                        t = t_use(where, f"p{g}", it)
                        pe.wait_ge(t.free, t.done)
                        if g == 0:
                            pe.wait_ge(v_ready, b + 1)
                        u = O.use(g // 4, b, 2)
                        if g % 4 == 0:
                            pe.wait_ge(u.free, u.n)
                        for i, (tile, rg, head) in enumerate(group[g]):
                            at = (i * 4 + rg) * 17
                            kv = head if first else tile
                            src = (g % 2) * 512 + i * P
                            last = product(nc, u.tile[:, at:at + 17], lambda half, c: pT[half][:, src:src + P],
                                           lambda half, c: v_aug[half][:, kv * 17:(kv + 1) * 17], 1)
                        if g % 4 == 3:
                            last.then_inc(u.full, 1)
                    if what == "out_turn":
                        u = O.use(g, b, 2)
                        pe.wait_ge(u.free, u.done)
                        t = t_use(where, f"out{g}", it)
                        pe.wait_ge(t.free, t.n)
                        turn(chip, t.tile, o[:, g * 256:(g + 1) * 256], 2).then_inc(t.full, 1)
                    if what == "out":
                        a = a_use(where, "out", it)
                        if g % 2 == 0:
                            t = t_use(where, f"out{g // 2}", it)
                            pe.wait_ge(t.free, t.done)
                        if g == 0:
                            pe.wait_ge(a.free, a.n)
                        last = product(nc, a.tile[:], lambda half, c: (oh, ol)[half][:, g * P:(g + 1) * P],
                                       columns(chip.weight(slots["o"]), g * D), 1, start=g == 0, stop=g == CH - 1)
                        if g == CH - 1:
                            last.then_inc(a.full, 1)

                schedule(nc.tensor, step)

            @block.scalar
            def _(act):
                def step(where, what, g, b, it):
                    if not first and what in ("q_take", "k_take"):
                        a = a_use(where, what[0], it)
                        act.wait_ge(a.full, a.n)
                        if what[0] == "q":
                            src = a.tile[:].rearrange("p (h k) -> p h k", k=HD).unsqueeze(2).to_broadcast([P, NH, 2, HD])
                            nc.scalar.activation(qd.rearrange("p (h s k) -> p h s k", s=2, k=HD), src, ACT.Copy,
                                                 scale=HD ** -0.5).then_inc(a.free, 1)
                        else:
                            src = a.tile[:, 0:P].rearrange("p (h k) -> p h k", k=HD).unsqueeze(2).to_broadcast([P, NKV, 8, HD])
                            nc.scalar.activation(kd.rearrange("p (h s k) -> p h s k", s=8, k=HD), src,
                                                 ACT.Copy).then_inc(a.free, 1)
                    if what in ("q_turn", "k_turn"):
                        t = t_use(where, f"{what[0]}{g}", it)
                        act.wait_ge(t.full, t.n)
                        nc.scalar.activation(hold[:, t.slot * 512:(t.slot + 1) * 512], t.tile[:],
                                             ACT.Copy).then_inc(held, 1)
                    if what == "exp":
                        act.wait_ge(maxed, b * NG + g + 1)
                        s = S.use(g, b, NG)
                        for i in range(GH):
                            at = (g % 4) * 512 + i * P
                            src = sB[:, at:at + P] if first else s.tile[:, i * P:(i + 1) * P]
                            m = (g % 4) * GH + i
                            last = nc.scalar.activation(prob[:, at:at + P], src, ACT.Exp, bias=nmax[:, m:m + 1])
                        last.then_inc(prob_ready, 1)
                    if what == "probs":
                        t = t_use(where, f"p{g}", it)
                        act.wait_ge(t.full, t.n)
                        nc.scalar.activation(pT[0][:, (g % 2) * 512:(g % 2 + 1) * 512], t.tile[:], ACT.Copy,
                                             scale=PSCALE).then_inc(p_hi, 1)
                    if what == "v_take":
                        act.wait_ge(v_clipped, b + 1)
                        if where == "body":
                            u = O.use(1, it, 2)
                            act.wait_ge(u.full, u.n)
                        nc.scalar.activation(values(v_hi), clipped, ACT.Copy).then_inc(v_hi_ready, 1)
                    if what == "out_turn":
                        t = t_use(where, f"out{g}", it)
                        act.wait_ge(t.full, t.n)
                        nc.scalar.activation(oh[:, g * 256:(g + 1) * 256], t.tile[:, 0:256], ACT.Copy).then_inc(o_hi, 1)

                schedule(nc.scalar, step)

            @block.vector
            def _(dve):
                dve.wait_ge(prepared, 83 if first else 2)

                def step(where, what, g, b, it):
                    if first and what in ("q_take", "k_take"):
                        c, _, _, i = raw[what[0]]
                        a = a_use(where, what[0], it)
                        dve.wait_ge(a.full, a.n)
                        nc.vector.tensor_scalar(c, a.tile[:], CLIP, -CLIP, ALU.min, ALU.max).then_inc(a.free, 1)
                        dve.wait_ge(a.free, a.done)
                        st = qst[:, 6 * i:6 * i + 6]
                        nc.vector.bn_stats(st, c).then_inc(qk_chain, 1)
                        dve.wait_ge(qk_chain, b * 4 + 2 * i + 1)
                        dve.sem_inc(carrier, 1)
                        nc.vector.bn_aggr(qmv[:, 2 * i:2 * i + 2], st).then_inc(qk_chain, 1)
                        dve.wait_ge(qk_chain, b * 4 + 2 * i + 2)
                        nc.vector.tensor_scalar(qve[:, i:i + 1], qmv[:, 2 * i + 1:2 * i + 2], EPS, None,
                                                ALU.add).then_inc(qk_var, 1)
                    if first and what in ("q_norm", "k_norm") and g == 0:
                        c, _, _, i = raw[what[0]]
                        dve.wait_ge(qk_rstd, b * 2 + i + 1)
                        nc.vector.tensor_scalar(c, c, qmv[:, 2 * i:2 * i + 1], qrs[:, i:i + 1],
                                                ALU.subtract, ALU.mult).then_inc(qk_z, 1)
                    if what == "v_clip":
                        a = a_use(where, "v", it)
                        dve.wait_ge(a.full, a.n)
                        src = a.tile[:, 0:nkv * HD].rearrange("p (h k) -> p h k", k=HD)
                        if first:
                            nc.vector.tensor_scalar(clipped, src, CLIP, -CLIP, ALU.min, ALU.max).then_inc(v_clipped, 1)
                        else:
                            nc.vector.tensor_copy(clipped, src).then_inc(v_clipped, 1)
                        dve.wait_ge(v_clipped, b + 1)
                        dve.sem_inc(a.free, 1)
                    if what in ("q_stack", "k_stack"):
                        t = t_use(where, f"{what[0]}{g}", it)
                        dve.wait_ge(held, b * 4 + 2 * g + (1 if what[0] == "q" else 2))
                        h = hold[:, t.slot * 512:(t.slot + 1) * 512]
                        at = slice(g * 512, (g + 1) * 512)
                        if what[0] == "q":
                            nc.vector.scalar_tensor_tensor(out=q_pair[:, at], in0=h, scalar=chip.half[:, 0:1],
                                                           in1=t.tile[:], op0=ALU.mult, op1=ALU.add).then_inc(t.free, 1)
                        else:
                            nc.vector.scalar_tensor_tensor(out=stackT[:, at], in0=h, scalar=chip.half[:, 0:1],
                                                           in1=t.tile[:], op0=ALU.mult, op1=ALU.add)
                            nc.vector.scalar_tensor_tensor(out=stackS[:, at], in0=h, scalar=chip.half[:, 1:2],
                                                           in1=t.tile[:], op0=ALU.mult, op1=ALU.add).then_inc(t.free, 1)
                        if what[0] == "k":
                            dve.wait_ge(t.free, t.done)
                            dve.sem_inc(stacked, 1)
                    if what == "scores":
                        s = S.use(g, b, NG)
                        dve.wait_ge(s.full, s.n)
                        at = slice((g % 4) * 512, (g % 4 + 1) * 512)
                        if first:
                            nc.vector.tensor_tensor(sB[:, at], s.tile[:], bias[:, g * 512:(g + 1) * 512],
                                                    ALU.add).then_inc(s.free, 1)
                            dve.wait_ge(s.free, s.done)
                        src = sB[:, at] if first else s.tile[:]
                        nc.vector.tensor_reduce(nmax[:, (g % 4) * GH:(g % 4 + 1) * GH], heads(src), AX, ALU.max,
                                                negate=True).then_inc(maxed, 1)
                    if what == "p_lo":
                        t = t_use(where, f"p{g}", it)
                        at = slice((g % 2) * 512, (g % 2 + 1) * 512)
                        dve.wait_ge(p_hi, b * NG + g + 1)
                        nc.vector.scalar_tensor_tensor(out=pT[1][:, at], in0=t.tile[:], scalar=PSCALE, in1=pT[0][:, at],
                                                       op0=ALU.mult, op1=ALU.subtract).then_inc(t.free, 1)
                    if what == "o_take":
                        u = O.use(g, b, 2)
                        dve.wait_ge(u.full, u.n)
                        n = 16
                        src = u.tile[:, 0:n * 17].rearrange("p (h k) -> p h k", k=17)
                        r = rinv[:, g * n:(g + 1) * n]
                        nc.vector.reciprocal(r, src[:, :, HD]).then_inc(summed, 1)
                        dve.wait_ge(summed, b * 2 + g + 1)
                        dst = o[:, g * 256:(g + 1) * 256].rearrange("p (h k) -> p h k", k=HD)
                        nc.vector.tensor_tensor(dst, src[:, :, 0:HD], spread(r, n, HD), ALU.mult).then_inc(u.free, 1)
                    if what == "out_lo":
                        t = t_use(where, f"out{g}", it)
                        at = slice(g * 256, (g + 1) * 256)
                        dve.wait_ge(o_hi, b * 2 + g + 1)
                        nc.vector.tensor_tensor(ol[:, at], t.tile[:, 0:256], oh[:, at], ALU.subtract).then_inc(t.free, 1)
                    if what == "out_take":
                        a = a_use(where, "out", it)
                        dve.wait_ge(a.full, a.n)
                        at = bass.ds(b * D, D)
                        nc.vector.tensor_tensor(chip.x[:, at], chip.x[:, at], a.tile[:], ALU.add).then_inc(a.free, 1)

                schedule(nc.vector, step)


def rms_stats(nc, dve, src, junk, ss, eps_out, chain, k):
    for i in range(GH):
        at = slice(i * P, (i + 1) * P)
        last = nc.vector.tensor_tensor_reduce(out=junk[:, at], in0=src[:, at], in1=src[:, at], scale=1.0, scalar=0.0,
                                              op0=ALU.mult, op1=ALU.add, accum_out=ss[:, i:i + 1])
    last.then_inc(chain, 1)
    dve.wait_ge(chain, k + 1)
    return nc.vector.tensor_scalar(eps_out, ss, 1.0 / P, EPS, ALU.mult, ALU.add)


def cross_views(chip):
    kT_hi, kT_lo, v_hi, v_lo = carve(chip.big, [(NKV * NB * P, F16)] * 4)
    return (kT_hi, kT_lo), (v_hi, v_lo)


def per_head(t, b):
    return t.rearrange("p (h r) -> p h r", h=NKV)[:, :, bass.ds(b * P, P)]


def cross_keys(chip, k_slots, v_slots):
    nc, io = chip.nc, chip.io
    kT, v = cross_views(chip)
    kf, junk, kn, kw, wrow, qrow, ss, ve, rk = carve(chip.small, [
        (1024, F32), (512, F32), (512, F32), (1024, F32), (P, F32), (P, F32), (4, F32), (8, F32), (8, F32)])
    with chip.begin():
        sem = chip.sem
        A = Ring("A", chip.psum[0:4], sem)
        T = Ring("T", chip.psum[4:6], sem)
        copied, squares, var, root, scaled, ready, split, rows_ready = (
            sem(n) for n in ("copied", "squares", "var", "root", "scaled", "ready", "split_hi", "rows_ready"))
        v_split = sem("v_hi")
        with nc.Block() as block:

            @block.sync
            def _(sp):
                sp.dma_start(wrow, io["vectors"][V_XKN:V_XKN + 1, 0:P].partition_broadcast(P)).then_inc(rows_ready, 16)
                sp.dma_start(qrow, io["vectors"][V_XQN:V_XQN + 1, 0:P].partition_broadcast(P)).then_inc(rows_ready, 16)

            @block.gpsimd
            def _(pool):
                A.credit(pool)
                T.credit(pool)
                pool.wait_ge(rows_ready, 32)
                nc.gpsimd.tensor_tensor(wrow, wrow, qrow, ALU.mult).then_inc(rows_ready, 1)
                pool.wait_ge(rows_ready, 33)
                nc.gpsimd.tensor_scalar(wrow, wrow, P ** -0.5, 1.0, ALU.mult, ALU.mult).then_inc(rows_ready, 1)
                pool.wait_ge(rows_ready, 34)
                with nc.gpsimd.Fori(0, NB) as b:
                    for m in range(2):
                        k = b * 2 + m
                        pool.wait_ge(var, k + 1)
                        nc.gpsimd.tensor_tensor(rk[:, m * 4:m * 4 + 4], ve[:, m * 4:m * 4 + 4], chip.mhalf[:, 0:4],
                                                ALU.pow).then_inc(root, 1)
                        pool.wait_ge(root, k + 1)
                        nc.gpsimd.tensor_tensor(heads(kn), heads(kf[:, m * 512:(m + 1) * 512]),
                                                spread(rk[:, m * 4:m * 4 + 4], GH, P), ALU.mult).then_inc(scaled, 1)
                        pool.wait_ge(scaled, k + 1)
                        nc.gpsimd.tensor_tensor(heads(kw[:, m * 512:(m + 1) * 512]), heads(kn),
                                                wrow.unsqueeze(1).to_broadcast([P, GH, P]), ALU.mult).then_inc(ready, 1)

            @block.tensor
            def _(pe):
                with nc.tensor.Fori(0, NB) as b:
                    for m, slot in enumerate((*k_slots, *v_slots)):
                        a = A.use(m, b, 4)
                        pe.wait_ge(a.free, a.n)
                        product(nc, a.tile[:], tokens(chip.cT, b), columns(chip.weight(slot)), CH).then_inc(a.full, 1)
                    for m in range(2):
                        t = T.use(m, b, 2)
                        pe.wait_ge(ready, b * 2 + m + 1)
                        pe.wait_ge(t.free, t.n)
                        turn(chip, t.tile, kw[:, m * 512:(m + 1) * 512]).then_inc(t.full, 1)

            @block.scalar
            def _(act):
                with nc.scalar.Fori(0, NB) as b:
                    for m in range(2):
                        a = A.use(m, b, 4)
                        act.wait_ge(a.full, a.n)
                        nc.scalar.activation(kf[:, m * 512:(m + 1) * 512], a.tile[:], ACT.Copy).then_inc(a.free, 1)
                    for m in range(2):
                        a = A.use(2 + m, b, 4)
                        act.wait_ge(a.full, a.n)
                        nc.scalar.activation(per_head(v[0], b)[:, m * 4:m * 4 + 4, :], heads(a.tile[:]),
                                             ACT.Copy).then_inc(v_split, 1)
                    for m in range(2):
                        t = T.use(m, b, 2)
                        act.wait_ge(t.full, t.n)
                        nc.scalar.activation(per_head(kT[0], b)[:, m * 4:m * 4 + 4, :], heads(t.tile[:]),
                                             ACT.Copy).then_inc(split, 1)

            @block.vector
            def _(dve):
                with nc.vector.Fori(0, NB) as b:
                    for m in range(2):
                        a = A.use(m, b, 4)
                        dve.wait_ge(a.free, a.done)
                        rms_stats(nc, dve, kf[:, m * 512:(m + 1) * 512], junk, ss, ve[:, m * 4:m * 4 + 4], squares,
                                  b * 2 + m).then_inc(var, 1)
                        dve.wait_ge(var, b * 2 + m + 1)
                    for m in range(2):
                        a = A.use(2 + m, b, 4)
                        dve.wait_ge(v_split, b * 2 + m + 1)
                        nc.vector.tensor_tensor(per_head(v[1], b)[:, m * 4:m * 4 + 4, :], heads(a.tile[:]),
                                                per_head(v[0], b)[:, m * 4:m * 4 + 4, :], ALU.subtract).then_inc(a.free, 1)
                    for m in range(2):
                        t = T.use(m, b, 2)
                        dve.wait_ge(split, b * 2 + m + 1)
                        nc.vector.tensor_tensor(per_head(kT[1], b)[:, m * 4:m * 4 + 4, :], heads(t.tile[:]),
                                                per_head(kT[0], b)[:, m * 4:m * 4 + 4, :], ALU.subtract).then_inc(t.free, 1)


CROSS_ORDER = [("norm", 2), ("weights", 0), ("q_turn", 1), ("q", 0), ("pv", 3), ("probs", 2), ("scores", 1), ("out", 4)]
LAG = 4


def cross_attention(chip, even, odd):
    nc, io = chip.nc, chip.io
    kT, v = cross_views(chip)
    qf, qn, s_, prob, pn, mask, qh, ql, ph, pl, a0h, a0l, a1h, a1l, junk_, ss, ve, rq, nmax, rs, ri = carve(chip.small, [
        (512, F32), (512, F32), (512, F32), (512, F32), (512, F32), (P, F32), (512, F16), (512, F16), (512, F16),
        (512, F16), (512, F16), (512, F16), (512, F16), (512, F16), (512, F32), (4, F32), (4, F32), (4, F32),
        (4, F32), (4, F32), (4, F32)])
    ah, al = (a0h, a1h), (a0l, a1l)
    n_slots = 2 * NB
    PARTS = NB // 2
    incoming = [odd[0], odd[1], even[0], even[1]]
    base = list(chip.n_staged)

    with chip.begin():
        sem = chip.sem
        A = Ring("A", chip.psum[0:2], sem)
        T = Ring("T", chip.psum[2:4], sem)
        S = Ring("S", chip.psum[4:6], sem)
        O = Ring("O", chip.psum[6:8], sem)
        qf_ready, squares, var, root, qn_ready, q_hi, s_ready, maxed, prob_ready, sums, inv, pn_ready, p_hi, a_hi = (
            sem(n) for n in ("qf_ready", "squares", "var", "root", "qn_ready", "q_hi", "s_ready", "maxed",
                             "prob_ready", "sums", "inv", "pn_ready", "p_hi", "a_hi"))
        w_hi, w_done, got_mask = sem("w_hi"), sem("w_done"), sem("got_mask")

        def one(ring, bank, s, gg):
            return Use(bank, ring.tiles[bank], ring.full[bank], ring.free[bank], gg * n_slots + s + 1)

        def schedule(eng, step):
            def slots(gg, first, end, limit):
                for slot in range(first, end):
                    for what, behind in CROSS_ORDER:
                        if 0 <= slot - behind < limit:
                            step(what, slot - behind, gg, gg * n_slots + (slot - behind))

            slots(0, 0, LAG, n_slots)
            with eng.Fori(0, NKV // 2 - 1) as gg:
                slots(gg, LAG, n_slots + LAG, n_slots + LAG)
            slots(NKV // 2 - 1, LAG, n_slots + LAG, n_slots)

        with nc.Block() as block:

            @block.sync
            def _(sp):
                sp.dma_start(mask, io["mask"]).then_inc(got_mask, 16)
                with nc.sync.Fori(0, NKV // 2) as gg:
                    for m in range(4):
                        sp.wait_ge(w_done, gg * n_slots + PARTS * (m + 1))
                        mat = gg * 4 + (W_XQO + 4 + m)
                        sp.dma_start(chip.stage[:, m % 2, :],
                                     io["weights"][bass.ds(mat, 1), :, :].rearrange("o p n -> p (o n)")
                                     ).then_inc(chip.staged[m % 2], 16)

            @block.gpsimd
            def _(pool):
                for ring in (A, T, S, O):
                    ring.credit(pool)

                def step(what, s, gg, k):
                    if what == "q":
                        pool.wait_ge(var, k + 1)
                        nc.gpsimd.tensor_tensor(rq, ve, chip.mhalf[:, 0:4], ALU.pow).then_inc(root, 1)
                        pool.wait_ge(root, k + 1)
                        nc.gpsimd.tensor_tensor(heads(qn), heads(qf), spread(rq, GH, P), ALU.mult).then_inc(qn_ready, 1)
                    if what == "norm":
                        pool.wait_ge(inv, k + 1)
                        nc.gpsimd.tensor_tensor(heads(pn), heads(prob), spread(ri, GH, P), ALU.mult).then_inc(pn_ready, 1)
                    if what == "weights":
                        m, part = s // PARTS % 4, s % PARTS
                        at = slice(part * D, (part + 1) * D)
                        pool.wait_ge(w_hi, k + 1)
                        nc.gpsimd.tensor_tensor(chip.w[1][:, incoming[m], at], chip.stage[:, m % 2, at],
                                                chip.w[0][:, incoming[m], at], ALU.subtract).then_inc(w_done, 1)

                schedule(nc.gpsimd, step)

            @block.tensor
            def _(pe):
                def step(what, s, gg, k):
                    b, odd_half = s % NB, s // NB % 2
                    if what == "q":
                        if s == NB:
                            pe.wait_ge(w_done, gg * n_slots + PARTS)
                        if s == n_slots:
                            pe.wait_ge(w_done, gg * n_slots + 3 * PARTS)
                        if s == n_slots + LAG - 1:
                            pe.wait_ge(w_done, gg * n_slots + 4 * PARTS)
                        a = one(A, 0, s, gg)
                        pe.wait_ge(a.free, a.n)
                        product(nc, a.tile[:], tokens(chip.hT, b), columns(chip.weight((even, odd)[odd_half][0])),
                                CH).then_inc(a.full, 1)
                    if what == "q_turn":
                        t = one(T, 0, s, gg)
                        pe.wait_ge(qn_ready, k + 1)
                        pe.wait_ge(t.free, t.n)
                        turn(chip, t.tile, qn).then_inc(t.full, 1)
                    if what == "scores":
                        t = one(T, 0, s, gg)
                        pe.wait_ge(t.free, t.done)
                        u = S.use(s, gg, n_slots)
                        pe.wait_ge(u.free, u.n)
                        key = (gg * 2 + s // NB) * (NB * P) + b * P
                        for i in range(GH):
                            last = product(nc, u.tile[:, i * P:(i + 1) * P],
                                           lambda half, c, i=i: (qh, ql)[half][:, i * P:(i + 1) * P],
                                           lambda half, c: kT[half][:, bass.ds(key, P)], 1)
                        last.then_inc(u.full, 1)
                    if what == "probs":
                        t = one(T, 1, s, gg)
                        pe.wait_ge(pn_ready, k + 1)
                        pe.wait_ge(t.free, t.n)
                        turn(chip, t.tile, pn).then_inc(t.full, 1)
                    if what == "pv":
                        t = one(T, 1, s, gg)
                        pe.wait_ge(t.free, t.done)
                        u = O.use(s, gg, n_slots)
                        pe.wait_ge(u.free, u.n)
                        val = (gg * 2 + s // NB) * (NB * P) + b * P
                        product(nc, u.tile[:], lambda half, c: v[half][:, bass.ds(val, P)],
                                lambda half, c: (ph, pl)[half], 1).then_inc(u.full, 1)
                    if what == "out":
                        if s == NB:
                            pe.wait_ge(w_done, gg * n_slots + 2 * PARTS)
                        u = O.use(s, gg, n_slots)
                        pe.wait_ge(u.free, u.done)
                        a = one(A, 1, s, gg)
                        pe.wait_ge(a.free, a.n)
                        product(nc, a.tile[:], lambda half, c: (ah, al)[half][s % 2][:, c * P:(c + 1) * P],
                                columns(chip.weight((even, odd)[odd_half][1])), CH).then_inc(a.full, 1)

                schedule(nc.tensor, step)

            @block.scalar
            def _(act):
                def step(what, s, gg, k):
                    if what == "q":
                        a = one(A, 0, s, gg)
                        act.wait_ge(a.full, a.n)
                        nc.scalar.activation(qf, a.tile[:], ACT.Copy).then_inc(a.free, 1)
                    if what == "q_turn":
                        t = one(T, 0, s, gg)
                        act.wait_ge(t.full, t.n)
                        nc.scalar.activation(qh, t.tile[:], ACT.Copy).then_inc(q_hi, 1)
                    if what == "scores":
                        act.wait_ge(maxed, k + 1)
                        for i in range(GH):
                            at = slice(i * P, (i + 1) * P)
                            last = nc.scalar.activation(prob[:, at], s_[:, at], ACT.Exp, bias=nmax[:, i:i + 1],
                                                        accum_out=rs[:, i:i + 1])
                        last.then_inc(prob_ready, 1)
                    if what == "probs":
                        t = one(T, 1, s, gg)
                        act.wait_ge(t.full, t.n)
                        nc.scalar.activation(ph, t.tile[:], ACT.Copy).then_inc(p_hi, 1)
                    if what == "pv":
                        u = O.use(s, gg, n_slots)
                        act.wait_ge(u.full, u.n)
                        nc.scalar.activation(ah[s % 2], u.tile[:], ACT.Copy, scale=1 / PSCALE).then_inc(a_hi, 1)
                    if what == "weights":
                        m, part = s // PARTS, s % PARTS
                        if part == 0:
                            act.wait_ge(chip.staged[m % 2], gg * 32 + (base[m % 2] + 16 * (m // 2)))
                            if m == 1:
                                act.wait_ge(A.free[1], gg * n_slots + 1)
                            if m == 2:
                                a = one(A, 0, NB - 1, gg)
                                act.wait_ge(a.full, a.n)
                            if m == 3:
                                a = one(A, 1, NB - 1, gg)
                                act.wait_ge(a.full, a.n)
                            if m == 4:
                                a = one(A, 0, n_slots - 1, gg)
                                act.wait_ge(a.full, a.n)
                        at = slice(part * D, (part + 1) * D)
                        nc.scalar.activation(chip.w[0][:, incoming[m % 4], at], chip.stage[:, m % 2, at],
                                             ACT.Copy).then_inc(w_hi, 1)

                schedule(nc.scalar, step)

            @block.vector
            def _(dve):
                dve.wait_ge(got_mask, 16)

                def step(what, s, gg, k):
                    if what == "q":
                        a = one(A, 0, s, gg)
                        dve.wait_ge(a.free, a.done)
                        rms_stats(nc, dve, qf, junk_, ss, ve, squares, k).then_inc(var, 1)
                    if what == "q_turn":
                        t = one(T, 0, s, gg)
                        dve.wait_ge(q_hi, k + 1)
                        nc.vector.tensor_tensor(ql, t.tile[:], qh, ALU.subtract).then_inc(t.free, 1)
                    if what == "scores":
                        u = S.use(s, gg, n_slots)
                        dve.wait_ge(u.full, u.n)
                        nc.vector.tensor_tensor(heads(s_), heads(u.tile[:]),
                                                mask.unsqueeze(1).to_broadcast([P, GH, P]), ALU.add).then_inc(u.free, 1)
                        dve.wait_ge(u.free, u.done)
                        nc.vector.tensor_reduce(nmax, heads(s_), AX, ALU.max, negate=True).then_inc(maxed, 1)
                    if what == "norm":
                        dve.wait_ge(prob_ready, k + 1)
                        nc.vector.tensor_scalar(rs, rs, 1 / PSCALE, None, ALU.mult).then_inc(sums, 1)
                        dve.wait_ge(sums, k + 1)
                        nc.vector.reciprocal(ri, rs).then_inc(inv, 1)
                    if what == "probs":
                        t = one(T, 1, s, gg)
                        dve.wait_ge(p_hi, k + 1)
                        nc.vector.tensor_tensor(pl, t.tile[:], ph, ALU.subtract).then_inc(t.free, 1)
                    if what == "pv":
                        u = O.use(s, gg, n_slots)
                        dve.wait_ge(a_hi, k + 1)
                        nc.vector.scalar_tensor_tensor(out=al[s % 2], in0=u.tile[:], scalar=1 / PSCALE, in1=ah[s % 2],
                                                       op0=ALU.mult, op1=ALU.subtract).then_inc(u.free, 1)
                    if what == "out":
                        a = one(A, 1, s, gg)
                        dve.wait_ge(a.full, a.n)
                        at = slice((s % NB) * D, (s % NB + 1) * D)
                        nc.vector.tensor_tensor(chip.x[:, at], chip.x[:, at], a.tile[:], ALU.add).then_inc(a.free, 1)

                schedule(nc.vector, step)
    for i in range(2):
        chip.n_staged[i] += 16 * 2 * (NKV // 2)


def experts(chip, base_slot, ag_slot):
    nc, io = chip.nc, chip.io
    n_ag = NE * RANK + NE + 1
    CHAIN = 11
    bst, bh, bl, brow, thr = carve(chip.big, [(D, F32), (D, F16), (D, BF16), (D, F32), (4, F32)])
    lay = carve(chip.small, [(n_ag + 3, F32), (P, F32), (P, F16), (P, F16), (NE, F32), (NE, F32), (NE, F32),
                             (8, F32)] * 2)
    names = ("hg", "hw", "hi", "lo", "e", "w", "w2", "c")
    bufs = [dict(zip(names, lay[8 * i:8 * i + 8], strict=True)) for i in range(2)]

    def col(i, n):
        return bufs[i]["c"][:, n:n + 1]

    with chip.begin():
        sem = chip.sem
        G = Ring("G", chip.psum[0:2], sem)
        Y = Ring("Y", chip.psum[2:4], sem)
        T = Ring("T", chip.psum[4:6], sem)
        got, b_hi, b_lo, nthr, chain, expo, hw_ready, hw_hi, x_b = (
            sem(n) for n in ("got", "b_hi", "b_lo", "nthr", "chain", "expo", "hw_ready", "hw_hi", "x_bias"))
        with nc.Block() as block:

            @block.sync
            def _(sp):
                sp.dma_start(bst, io["expert_b"]).then_inc(got, 16)
                sp.dma_start(brow, io["vectors"][V_BASE:V_BASE + 1, :].partition_broadcast(P)).then_inc(got, 16)
                sp.dma_start(thr[:, 0:2], io["vectors"][V_BTHR:V_BTHR + 1, 0:2].partition_broadcast(P)).then_inc(got, 16)

            @block.gpsimd
            def _(pool):
                for ring in (G, Y, T):
                    ring.credit(pool)
                pool.wait_ge(got, 48)
                with nc.gpsimd.Fori(0, NB) as b:
                    at = bass.ds(b * D, D)
                    nc.gpsimd.tensor_tensor(chip.x[:, at], chip.x[:, at], brow, ALU.add).then_inc(x_b, 1)

            @block.tensor
            def _(pe):
                pe.wait_ge(b_lo, 1)
                with nc.tensor.Fori(0, NB // 2) as h:
                    for i in range(2):
                        u = G.use(i, h, 2)
                        pe.wait_ge(u.free, u.n)
                        product(nc, u.tile[:, 0:n_ag], tokens(chip.hT, h * 2 + i),
                                columns(chip.weight(ag_slot), 0, n_ag), CH).then_inc(u.full, 1)
                    for i in range(2):
                        y = Y.use(i, h, 2)
                        pe.wait_ge(y.free, y.n)
                        product(nc, y.tile[:], tokens(chip.hT, h * 2 + i), columns(chip.weight(base_slot)), CH,
                                stop=False)
                    for i in range(2):
                        t = T.use(i, h, 2)
                        pe.wait_ge(hw_ready, h * 2 + i + 1)
                        pe.wait_ge(t.free, t.n)
                        turn(chip, t.tile, bufs[i]["hw"], 1).then_inc(t.full, 1)
                    for i in range(2):
                        t, y = T.use(i, h, 2), Y.use(i, h, 2)
                        pe.wait_ge(t.free, t.done)
                        product(nc, y.tile[:], lambda half, c, i=i: bufs[i][("hi", "lo")[half]],
                                lambda half, c: (bh, bl)[half], 1, start=False).then_inc(y.full, 1)

            @block.scalar
            def _(act):
                act.wait_ge(got, 48)
                nc.scalar.activation(bh, bst, ACT.Copy).then_inc(b_hi, 1)
                nc.scalar.activation(thr[:, 2:3], thr[:, 0:1], ACT.Copy, scale=-1.0).then_inc(nthr, 1)
                act.wait_ge(nthr, 1)
                with nc.scalar.Fori(0, NB // 2) as h:
                    for i in range(2):
                        hg = bufs[i]["hg"]
                        act.wait_ge(chain, (h * 2 + i) * CHAIN + 2)
                        nc.scalar.activation(bufs[i]["e"], hg[:, P:P + NE], ACT.Exp, bias=col(i, 0),
                                             accum_out=col(i, 1))
                        nc.scalar.activation(col(i, 2), hg[:, P + NE:P + NE + 1], ACT.Exp, bias=thr[:, 2:3],
                                             scale=-1.0).then_inc(expo, 1)
                    for i in range(2):
                        t = T.use(i, h, 2)
                        act.wait_ge(t.full, t.n)
                        nc.scalar.activation(bufs[i]["hi"], t.tile[:, 0:P], ACT.Copy).then_inc(hw_hi, 1)

            @block.vector
            def _(dve):
                dve.wait_ge(b_hi, 1)
                nc.vector.tensor_tensor(bl, bst, bh, ALU.subtract).then_inc(b_lo, 1)
                with nc.vector.Fori(0, NB // 2) as h:
                    for i in range(2):
                        count = [0]

                        def link(ins, k=h * 2 + i, count=count):
                            count[0] += 1
                            ins.then_inc(chain, 1)
                            dve.wait_ge(chain, k * CHAIN + count[0])

                        u, t = G.use(i, h, 2), bufs[i]
                        dve.wait_ge(u.full, u.n)
                        link(nc.vector.tensor_copy(t["hg"][:, 0:n_ag], u.tile[:, 0:n_ag]))
                        dve.sem_inc(u.free, 1)
                        link(nc.vector.tensor_reduce(col(i, 0), t["hg"][:, P:P + NE], AX, ALU.max, negate=True))
                        dve.wait_ge(expo, h * 2 + i + 1)
                        link(nc.vector.tensor_scalar(col(i, 2), col(i, 2), 8.0, 8.0, ALU.mult, ALU.add))
                        link(nc.vector.reciprocal(col(i, 2), col(i, 2)))
                        link(nc.vector.reciprocal(col(i, 3), col(i, 1)))
                        link(nc.vector.tensor_scalar(t["w"], t["e"], col(i, 3), col(i, 2), ALU.mult, ALU.subtract))
                        link(nc.vector.tensor_scalar(t["w2"], t["w"], 0.0, None, ALU.max, ALU.add,
                                                     accum_out=col(i, 4)))
                        link(nc.vector.tensor_scalar(col(i, 5), col(i, 4), 0.0, None, ALU.is_equal))
                        link(nc.vector.tensor_tensor(col(i, 4), col(i, 4), col(i, 5), ALU.add))
                        link(nc.vector.reciprocal(col(i, 4), col(i, 4)))
                        link(nc.vector.tensor_scalar(t["w2"], t["w2"], col(i, 4), 2.0, ALU.mult, ALU.mult))
                        assert count[0] == CHAIN
                        nc.vector.tensor_tensor(heads(t["hw"], NE), heads(t["hg"][:, 0:P], NE),
                                                spread(t["w2"], NE, RANK), ALU.mult).then_inc(hw_ready, 1)
                    for i in range(2):
                        t = T.use(i, h, 2)
                        dve.wait_ge(hw_hi, h * 2 + i + 1)
                        nc.vector.tensor_tensor(bufs[i]["lo"], t.tile[:, 0:P], bufs[i]["hi"],
                                                ALU.subtract).then_inc(t.free, 1)
                    for i in range(2):
                        y = Y.use(i, h, 2)
                        at = bass.ds((h * 2 + i) * D, D)
                        dve.wait_ge(x_b, h * 2 + i + 1)
                        dve.wait_ge(y.full, y.n)
                        nc.vector.tensor_tensor(chip.x[:, at], chip.x[:, at], y.tile[:], ALU.add).then_inc(y.free, 1)


def last_cross_views(chip):
    q_hi, q_lo, k_hi, k_lo, rest = carve(chip.big, [(CH * NB * P, F16)] * 4 + [(8192, F32)])
    return (q_hi, q_lo), (k_hi, k_lo), rest


def last_cross_projections(chip, q_slot, k_slot):
    nc, io = chip.nc, chip.io
    q, k, rest = last_cross_views(chip)
    bias = rest[:, 0:2 * CH]
    WIDE = NB * P
    todo = [(out, slot, src, first + tile, tile, part)
            for out, slot, src, first in ((k, k_slot, chip.cT, CH), (q, q_slot, chip.hT, 0))
            for tile in range(CH) for part in range(2)]
    with chip.begin():
        A = Ring("A", chip.psum[0:4], chip.sem)
        got, hi = chip.sem("got"), chip.sem("hi")
        with nc.Block() as block:

            @block.sync
            def _(sp):
                sp.dma_start(bias, io["cross_bias"]).then_inc(got, 16)

            @block.gpsimd
            def _(pool):
                A.credit(pool)

            @block.tensor
            def _(pe):
                for n, (_, slot, src, _, tile, part) in enumerate(todo):
                    a = A.use(n)
                    w = chip.weight(slot)
                    pe.wait_ge(a.free, a.n)

                    def batches(half, c, src=src, part=part):
                        rows = src[half][:].rearrange("p (b c t) -> p b c t", b=NB, c=CH)
                        return rows[:, part * (NB // 2):(part + 1) * (NB // 2), c, :]

                    product(nc, a.tile[:], lambda half, c, w=w, t=tile: w[half][:, c * D + t * P:c * D + (t + 1) * P],
                            batches, CH).then_inc(a.full, 1)

            @block.scalar
            def _(act):
                act.wait_ge(got, 16)
                for n, (out, _, _, b, tile, part) in enumerate(todo):
                    a = A.use(n)
                    at = slice(tile * WIDE + part * D, tile * WIDE + (part + 1) * D)
                    act.wait_ge(a.full, a.n)
                    nc.scalar.activation(out[0][:, at], a.tile[:], ACT.Identity, bias=bias[:, b:b + 1]).then_inc(hi, 1)

            @block.vector
            def _(dve):
                dve.wait_ge(got, 16)
                for n, (out, _, _, b, tile, part) in enumerate(todo):
                    a = A.use(n)
                    at = slice(tile * WIDE + part * D, tile * WIDE + (part + 1) * D)
                    dve.wait_ge(hi, n + 1)
                    nc.vector.scalar_tensor_tensor(out=out[1][:, at], in0=a.tile[:], scalar=bias[:, b:b + 1],
                                                   in1=out[0][:, at], op0=ALU.add, op1=ALU.subtract).then_inc(a.free, 1)


def last_cross_attention(chip):
    nc, io = chip.nc, chip.io
    q, k, rest = last_cross_views(chip)
    WIDE = NB * P
    cst, ch, cl = carve(rest, [(2 * D, F32), (2 * D, F16), (2 * D, F16)])
    prob, ph, pl, nmax, nm, rs, ri = carve(chip.small, [
        (2 * P, F32), (2 * P, F16), (2 * P, F16), (2, F32), (2, F32), (2, F32), (2, F32)])
    scale = float(np.float32(1.0) / np.sqrt(np.float32(D)))
    with chip.begin():
        sem = chip.sem
        S = Ring("S", chip.psum[0:2], sem)
        T = Ring("T", chip.psum[2:4], sem)
        Y = Ring("Y", chip.psum[4:6], sem)
        C = Ring("C", [cst[:, i * D:(i + 1) * D] for i in range(2)], sem)
        c_hi, c_lo, maxed, scaled, prob_ready, p_hi, inv = (
            sem(n) for n in ("ctx_hi", "ctx_lo", "maxed", "scaled", "prob_ready", "p_hi", "inv"))
        with nc.Block() as block:

            @block.sync
            def _(sp):
                with nc.sync.Fori(0, NB // 2) as h:
                    for i in range(2):
                        c = C.use(i, h, 2)
                        sp.wait_ge(c.free, c.n)
                        sp.dma_start(c.tile, io["ctx"][bass.ds(h * 2 + i, 1), :, :].rearrange("o p n -> p (o n)")
                                     ).then_inc(c.full, 16)

            @block.gpsimd
            def _(pool):
                for ring in (S, T, Y, C):
                    ring.credit(pool)
                with nc.gpsimd.Fori(0, NB // 2) as h:
                    for i in range(2):
                        c = C.use(i, h, 2)
                        at = slice(i * D, (i + 1) * D)
                        pool.wait_ge(c_hi, h * 2 + i + 1)
                        nc.gpsimd.tensor_tensor(cl[:, at], c.tile, ch[:, at], ALU.subtract).then_inc(c.free, 1)

            @block.tensor
            def _(pe):
                with nc.tensor.Fori(0, NB // 2) as h:
                    for i in range(2):
                        s = S.use(i, h, 2)
                        pe.wait_ge(s.free, s.n)
                        b = h * 2 + i
                        product(nc, s.tile[:, 0:P], lambda half, c, b=b: q[half][:, bass.ds(b * P + c * WIDE, P)],
                                lambda half, c, b=b: k[half][:, bass.ds(b * P + c * WIDE, P)], CH).then_inc(s.full, 1)
                    for i in range(2):
                        t = T.use(i, h, 2)
                        pe.wait_ge(prob_ready, h * 2 + i + 1)
                        pe.wait_ge(t.free, t.n)
                        turn(chip, t.tile, prob[:, i * P:(i + 1) * P], 1).then_inc(t.full, 1)
                    for i in range(2):
                        t, y, c = T.use(i, h, 2), Y.use(i, h, 2), C.use(i, h, 2)
                        pe.wait_ge(t.free, t.done)
                        pe.wait_ge(c.free, c.done)
                        pe.wait_ge(y.free, y.n)
                        product(nc, y.tile[:], lambda half, c, i=i: (ph, pl)[half][:, i * P:(i + 1) * P],
                                lambda half, c, i=i: (ch, cl)[half][:, i * D:(i + 1) * D], 1).then_inc(y.full, 1)

            @block.scalar
            def _(act):
                with nc.scalar.Fori(0, NB // 2) as h:
                    for i in range(2):
                        c, y = C.use(i, h, 2), Y.use(i, h, 2)
                        act.wait_ge(c.full, (c.n) * 16)
                        act.wait_ge(y.free, y.n)
                        nc.scalar.activation(ch[:, i * D:(i + 1) * D], c.tile, ACT.Copy).then_inc(c_hi, 1)
                    for i in range(2):
                        s = S.use(i, h, 2)
                        act.wait_ge(scaled, h * 2 + i + 1)
                        nc.scalar.activation(prob[:, i * P:(i + 1) * P], s.tile[:, 0:P], ACT.Exp, bias=nm[:, i:i + 1],
                                             scale=scale, accum_out=rs[:, i:i + 1]).then_inc(prob_ready, 1)
                    for i in range(2):
                        t = T.use(i, h, 2)
                        act.wait_ge(t.full, t.n)
                        nc.scalar.activation(ph[:, i * P:(i + 1) * P], t.tile[:, 0:P], ACT.Copy).then_inc(p_hi, 1)

            @block.vector
            def _(dve):
                with nc.vector.Fori(0, NB // 2) as h:
                    for i in range(2):
                        s = S.use(i, h, 2)
                        dve.wait_ge(s.full, s.n)
                        nc.vector.tensor_reduce(nmax[:, i:i + 1], s.tile[:, 0:P], AX, ALU.max,
                                                negate=True).then_inc(maxed, 1)
                        dve.wait_ge(maxed, h * 2 + i + 1)
                        nc.vector.tensor_scalar(nm[:, i:i + 1], nmax[:, i:i + 1], scale, None, ALU.mult).then_inc(scaled, 1)
                    for i in range(2):
                        s, t = S.use(i, h, 2), T.use(i, h, 2)
                        dve.wait_ge(p_hi, h * 2 + i + 1)
                        nc.vector.tensor_tensor(pl[:, i * P:(i + 1) * P], t.tile[:, 0:P], ph[:, i * P:(i + 1) * P],
                                                ALU.subtract).then_inc(t.free, 1)
                        dve.sem_inc(s.free, 1)
                        nc.vector.reciprocal(ri[:, i:i + 1], rs[:, i:i + 1]).then_inc(inv, 1)
                    for i in range(2):
                        y = Y.use(i, h, 2)
                        at = bass.ds((h * 2 + i) * D, D)
                        dve.wait_ge(inv, h * 2 + i + 1)
                        dve.wait_ge(y.full, y.n)
                        nc.vector.scalar_tensor_tensor(out=chip.x[:, at], in0=y.tile[:], scalar=ri[:, i:i + 1],
                                                       in1=chip.x[:, at], op0=ALU.mult, op1=ALU.add).then_inc(y.free, 1)


def sign_projection(chip, slot):
    nc, io = chip.nc, chip.io
    out, s, t = carve(chip.big, [(NB * D, F32), (4, F32), (4, F32)])
    with chip.begin():
        sem = chip.sem
        A = Ring("A", chip.psum[2:4], sem)
        T = Ring("T", chip.psum[0:2], sem)
        norm = Norm(chip, sem, T)
        got, steps, soft, written = (sem(n) for n in ("got", "steps", "softplus", "written"))
        with nc.Block() as block:

            @block.sync
            def _(sp):
                sp.dma_start(s[:, 0:2], io["vectors"][V_SCALE:V_SCALE + 1, 0:2].partition_broadcast(P)).then_inc(got, 16)
                for b in range(NB):
                    a = A.use(b)
                    sp.wait_ge(a.free, a.done)
                    at = slice(b * D, (b + 1) * D)
                    sp.dma_start(io["out"][:, at], out[:, at]).then_inc(written, 16)
                sp.wait_ge(written, 16 * NB)

            @block.gpsimd
            def _(pool):
                A.credit(pool)
                T.credit(pool)
                norm.root(pool)

            @block.tensor
            def _(pe):
                norm.turn(pe, 0)
                for b in range(NB):
                    if b + 1 < NB:
                        norm.turn(pe, b + 1)
                    t_, a = norm.use(b), A.use(b)
                    pe.wait_ge(t_.free, t_.done)
                    pe.wait_ge(a.free, a.n)
                    product(nc, a.tile[:], tokens(chip.hT, b), columns(chip.weight(slot)), CH).then_inc(a.full, 1)

            @block.scalar
            def _(act):
                act.wait_ge(got, 16)
                nc.scalar.activation(t[:, 0:1], s[:, 0:1], ACT.Abs).then_inc(steps, 1)
                act.wait_ge(steps, 1)
                nc.scalar.activation(t[:, 1:2], t[:, 0:1], ACT.Exp, scale=-1.0).then_inc(steps, 1)
                act.wait_ge(steps, 2)
                nc.scalar.activation(t[:, 2:3], t[:, 1:2], ACT.Ln, bias=1.0).then_inc(steps, 1)
                for b in range(NB):
                    norm.split_hi(act, b)

            @block.vector
            def _(dve):
                norm.stats(dve)
                dve.wait_ge(steps, 3)
                nc.vector.tensor_scalar(s[:, 2:3], s[:, 0:1], 0.0, t[:, 2:3], ALU.max, ALU.add).then_inc(soft, 1)
                dve.wait_ge(soft, 1)
                norm.scale(dve, 0)
                for b in range(NB + 1):
                    if b + 1 < NB:
                        norm.scale(dve, b + 1)
                    if b < NB:
                        norm.split_lo(dve, b)
                    if b > 0:
                        a = A.use(b - 1)
                        at = slice((b - 1) * D, b * D)
                        dve.wait_ge(a.full, a.n)
                        nc.vector.scalar_tensor_tensor(out=out[:, at], in0=a.tile[:], scalar=s[:, 2:3],
                                                       in1=chip.x[:, at], op0=ALU.mult, op1=ALU.add).then_inc(a.free, 1)


def decoder(nc, io):
    with ExitStack() as ctx:
        chip = Chip(nc, ctx, io)
        begin_layer(chip, [(W_QKVO + i, i) for i in range(4)], [W_XK, W_XK + 1], start=True)
        self_attention(chip, 0, {"q": 0, "k": 1, "v": 2, "o": 3})
        begin_layer(chip, [(W_XK, 4), (W_XK + 1, 5), (W_XV, 0), (W_XV + 1, 1), (W_XQO, 2), (W_XQO + 1, 3)],
                    [W_XQO + 2, W_XQO + 3])
        cross_keys(chip, (4, 5), (0, 1))
        cross_attention(chip, (2, 3), (4, 5))
        begin_layer(chip, [(W_BASE, 0), (W_AG, 1), (W_L1O, 4), (W_LXQ, 5)], [W_LXK, W_SIGN])
        experts(chip, 0, 1)
        begin_layer(chip, [], [])
        self_attention(chip, 1, {"q": 2, "k": 3, "v": 3, "o": 4})
        begin_layer(chip, [(W_LXK, 0), (W_SIGN, 1)], [])
        last_cross_projections(chip, 5, 0)
        last_cross_attention(chip)
        sign_projection(chip, 1)


def alibi_table():
    slopes = (1.0 / np.power(2.0, np.arange(1, NH + 1, dtype=np.float32) * (8.0 / NH))).astype(np.float32)
    pos = np.arange(P)
    rel = (pos[None, :] - pos[:, None]).astype(np.float32)
    table = np.empty((P, NG, GH, P), np.float32)
    for g in range(NG):
        for i in range(GH):
            head = ((g // 4) * 4 + i) * 4 + g % 4
            table[:, g, i, :] = np.where(rel <= 0, slopes[head] * rel, np.float32(-1e30))
    return table.reshape(P, NG * GH * P)


def kernel(x, ctx_4096, mask_1x1xSxS2_ff0, L0_attn_Wqkv, L0_attn_q_ln_w, L0_attn_q_ln_b, L0_attn_k_ln_w,
           L0_attn_k_ln_b, L0_attn_Wout, L0_xattn_q_proj_w, L0_xattn_k_proj_w, L0_xattn_v_proj_w, L0_xattn_o_proj_w,
           L0_xattn_q_norm_w, L0_xattn_k_norm_w, L0_ffn_W_base, L0_ffn_b_base, L0_ffn_W_gate, L0_ffn_W_thr,
           L0_ffn_b_thr, L0_ffn_A_w, L0_ffn_B_w, L1_attn_Wq, L1_attn_Wk, L1_attn_Wv, L1_attn_Wo, L1_xattn_Wq,
           L1_xattn_bq, L1_xattn_Wk, L1_xattn_bk, L1_ffn_sign, L1_ffn_scale):
    import concourse.bacc as bacc
    from concourse.bass_utils import run_bass_kernel_spmd

    f32 = np.float32

    def matrix(w_t):
        full = np.zeros((D, D), f32)
        full[:, :w_t.shape[1]] = w_t
        return full.reshape(CH, P, D).transpose(1, 0, 2).reshape(P, MAT)

    a = {n: np.asarray(v) for n, v in locals().items()
         if n not in ("f32", "matrix", "bacc", "run_bass_kernel_spmd")}
    weights = np.empty((N_MATS, P, MAT), f32)
    qkv = a["L0_attn_Wqkv"]
    for i in range(3):
        weights[W_QKVO + i] = matrix(qkv[i * D:(i + 1) * D].T)
    weights[W_QKVO + 3] = matrix(a["L0_attn_Wout"].T)
    for i in range(2):
        weights[W_XK + i] = matrix(a["L0_xattn_k_proj_w"][i * D:(i + 1) * D].T)
        weights[W_XV + i] = matrix(a["L0_xattn_v_proj_w"][i * D:(i + 1) * D].T)
    for g in range(NKV):
        weights[W_XQO + 2 * g] = matrix(a["L0_xattn_q_proj_w"][g * D:(g + 1) * D].T)
        weights[W_XQO + 2 * g + 1] = matrix(a["L0_xattn_o_proj_w"][:, g * D:(g + 1) * D].T)
    weights[W_L1Q] = matrix(a["L1_attn_Wq"].T)
    weights[W_L1KV] = matrix(np.concatenate([a["L1_attn_Wk"], a["L1_attn_Wv"]]).T)
    weights[W_BASE] = matrix(a["L0_ffn_W_base"].T)
    weights[W_AG] = matrix(np.concatenate([a["L0_ffn_A_w"].reshape(NE * RANK, D), a["L0_ffn_W_gate"],
                                           a["L0_ffn_W_thr"][None]]).T)
    weights[W_L1O] = matrix(a["L1_attn_Wo"].T)
    weights[W_LXQ] = matrix(a["L1_xattn_Wq"].T)
    weights[W_LXK] = matrix(a["L1_xattn_Wk"].T)
    weights[W_SIGN] = matrix(a["L1_ffn_sign"])

    vectors = np.zeros((9, D), f32)
    for row, name in ((V_QW, "L0_attn_q_ln_w"), (V_QB, "L0_attn_q_ln_b"), (V_KW, "L0_attn_k_ln_w"),
                      (V_KB, "L0_attn_k_ln_b"), (V_XQN, "L0_xattn_q_norm_w"), (V_XKN, "L0_xattn_k_norm_w"),
                      (V_BASE, "L0_ffn_b_base"), (V_BTHR, "L0_ffn_b_thr"), (V_SCALE, "L1_ffn_scale")):
        flat = a[name].reshape(-1)
        vectors[row, :flat.size] = flat

    late = np.arange(P) % 32 >= HD
    arrays = {
        "x": a["x"].transpose(1, 0, 2).reshape(P, NB * D),
        "ctxT": a["ctx_4096"].reshape(NB, P, CH, P).transpose(3, 0, 2, 1).reshape(P, NB * D),
        "ctx": a["ctx_4096"],
        "mask": a["mask_1x1xSxS2_ff0"].reshape(P, P),
        "weights": weights,
        "expert_b": a["L0_ffn_B_w"].transpose(0, 2, 1).reshape(P, D),
        "vectors": vectors,
        "cross_bias": np.concatenate([a["L1_xattn_bq"].reshape(CH, P), a["L1_xattn_bk"].reshape(CH, P)]).T,
        "ident": np.eye(P, dtype=f32),
        "half": np.stack([np.where(late, -1, 0), np.where(late, 0, -1)], 1).astype(f32),
        "alibi": alibi_table(),
    }
    nc = bacc.Bacc("TRN2", target_bir_lowering=False, num_devices=1)
    io = {}
    for name, v in arrays.items():
        arrays[name] = np.ascontiguousarray(v)
        io[name] = nc.dram_tensor(f"in_{name}", v.shape, mybir.dt.from_np(v.dtype), kind="ExternalInput").ap()
    io["out"] = nc.dram_tensor("out", (P, NB * D), F32, kind="ExternalOutput").ap()
    decoder(nc, io)
    result = run_bass_kernel_spmd(nc, [{f"in_{name}": v for name, v in arrays.items()}], core_ids=[0])
    return result.results[0]["out"].reshape(P, NB, D).transpose(1, 0, 2)
```

```python
from contextlib import ExitStack

import numpy as np

import concourse.bass as bass
from concourse import mybir

F32 = mybir.dt.float32
F16 = mybir.dt.float16
BF16 = mybir.dt.bfloat16
ALU = mybir.AluOpType
ACT = mybir.ActivationFunctionType
AX = mybir.AxisListType.X

P = 128
NB = 8
D = 512
CH = D // P
MAT = CH * D
EPS = 1e-5
NH = 32
HD = 16
NKV = 8
GH = 4
NG = NH // GH
CLIP = 8.0
PSCALE = 1024.0
NE, RANK = 8, 16
SLOTS = 6

W_QKVO = 0
W_XK, W_XV = 4, 6
W_XQO = 8
W_BASE, W_AG, W_L1Q, W_L1KV, W_L1O, W_LXQ, W_LXK, W_SIGN = range(8 + 2 * NKV, 16 + 2 * NKV)
N_MATS = 16 + 2 * NKV

V_QW, V_QB, V_KW, V_KB, V_XQN, V_XKN, V_BASE, V_BTHR, V_SCALE = range(9)

BIAS = slice(0, NG * 512)
ROWS = slice(2 * NB * D, 2 * NB * D + 4 * D)


class Use:

    def __init__(self, slot, tile, full, free, n):
        self.slot, self.tile, self.full, self.free, self.n, self.done = slot, tile, full, free, n, n + 1


class Ring:

    def __init__(self, name, tiles, sem):
        self.tiles = tiles
        self.full = [sem(f"{name}{i}_full") for i in range(len(tiles))]
        self.free = [sem(f"{name}{i}_free") for i in range(len(tiles))]

    def credit(self, eng):
        for s in self.free:
            eng.sem_inc(s, 1)

    def use(self, k, it=0, per=0):
        depth = len(self.tiles)
        assert per % depth == 0
        i = k % depth
        return Use(i, self.tiles[i], self.full[i], self.free[i], it * (per // depth) + (k // depth + 1))


class Chip:

    def __init__(self, nc, ctx, io):
        self.nc, self.io, self.phase = nc, io, 0

        def sb(name, shape, dt=F32):
            return ctx.enter_context(nc.sbuf_tensor(name, shape, dt))

        self.x = sb("x", [P, NB * D])
        self.hT = [sb("hT_hi", [P, NB * D], F16), sb("hT_lo", [P, NB * D], F16)]
        self.cT = [sb("cT_hi", [P, NB * D], F16), sb("cT_lo", [P, NB * D], F16)]
        self.w = [sb("w_hi", [P, SLOTS, MAT], F16), sb("w_lo", [P, SLOTS, MAT], BF16)]
        self.stage = sb("stage", [P, 2, MAT])
        self.ident = sb("ident", [P, P])
        self.half = sb("half", [P, 2])
        self.z = sb("z", [P, 2 * D])
        self.st = sb("st", [P, 6 * NB])
        self.mv = sb("mv", [P, 2 * NB])
        self.ve = sb("ve", [P, NB])
        self.rstd = sb("rstd", [P, NB])
        self.mhalf = sb("mhalf", [P, 8])
        self.big = sb("big", [P, 16384])
        self.small = sb("small", [P, 5632])
        self.psum = [ctx.enter_context(nc.psum_tensor(f"bank{i}", [P, 512], F32)) for i in range(8)]
        self.loaded = ctx.enter_context(nc.semaphore("loaded"))
        self.tabled = ctx.enter_context(nc.semaphore("tabled"))
        self.staged = [ctx.enter_context(nc.semaphore(f"staged{i}")) for i in range(2)]
        self.n_staged = [0, 0]

    def sem(self, name):
        return self.nc.alloc_semaphore(f"{name}_{self.phase}")

    def begin(self):
        self.phase += 1
        return self.nc.cleanup_on_exit()

    def load_weight(self, eng, mat, buf):
        self.n_staged[buf] += 16
        eng.dma_start(self.stage[:, buf, :], self.io["weights"][mat]).then_inc(self.staged[buf], 16)

    def weight(self, slot):
        return [self.w[0][:, slot, :], self.w[1][:, slot, :]]


def carve(region, shapes):
    at, out = 0, []
    for cols, dt in shapes:
        words = cols if dt == F32 else cols // 2
        v = region[:, at:at + words]
        out.append(v if dt == F32 else v.bitcast(dt))
        at += words
    assert at <= region.shape[1], (at, region.shape)
    return out


def product(nc, out, lhs, rhs, chunks, start=True, stop=True):
    n = 0
    for c in range(chunks):
        for a, b in ((0, 0), (0, 1), (1, 0)):
            last = nc.tensor.matmul(out, lhs(a, c), rhs(b, c), start=start and n == 0,
                                    stop=stop and n == 3 * chunks - 1)
            n += 1
    return last


def tokens(pair, b):
    return lambda half, c: pair[half][:, bass.ds(b * D + c * P, P)]


def columns(pair, first=0, n=D):
    return lambda half, c: pair[half][:, c * D + first:c * D + first + n]


def turn(chip, bank, src, n=4):
    for i in range(n):
        last = chip.nc.tensor.transpose(bank[:, i * P:(i + 1) * P], src[:, i * P:(i + 1) * P], chip.ident[:])
    return last


def heads(ap, n=GH):
    return ap.rearrange("p (h k) -> p h k", h=n)


def spread(ap, n, m):
    return ap.unsqueeze(2).to_broadcast([P, n, m])


class Norm:

    def __init__(self, chip, sem, turns, z=None, name="norm"):
        self.chip, self.turns, self.only_z = chip, turns, z
        self.stats_done, self.var, self.rstd, self.z, self.hi = (
            sem(f"{name}_{n}") for n in ("stats", "var", "rstd", "z", "hi"))

    def place(self, b):
        if len(self.turns.tiles) == 1:
            z = self.only_z or 0
            return self.turns.use(0, b, 1), self.chip.z[:, z * D:(z + 1) * D]
        return self.turns.use(b), self.chip.z[:, (b % 2) * D:(b % 2 + 1) * D]

    def scalars(self, dve, b):
        dve.wait_ge(self.rstd, 1 if isinstance(b, int) and b in self.batches(0) else 2)
        return self.chip.mv[:, bass.ds(2 * b, 1)], self.chip.rstd[:, bass.ds(b, 1)]

    def batches(self, part):
        return range(0, 2) if part == 0 else range(2, NB)

    def stats(self, dve, part):
        nc, c, group = self.chip.nc, self.chip, self.batches(part)
        done = 2 * group.start
        for b in group:
            nc.vector.bn_stats(c.st[:, 6 * b:6 * b + 6], c.x[:, b * D:(b + 1) * D]).then_inc(self.stats_done, 1)
        for n, b in enumerate(group):
            dve.wait_ge(self.stats_done, done + n + 1)
            nc.vector.bn_aggr(c.mv[:, 2 * b:2 * b + 2], c.st[:, 6 * b:6 * b + 6]).then_inc(self.stats_done, 1)
        dve.wait_ge(self.stats_done, done + 2 * len(group))
        var = c.mv[:].rearrange("p (b k) -> p b k", k=2)[:, group.start:group.stop, 1]
        nc.vector.tensor_scalar(c.ve[:, group.start:group.stop], var, EPS, None, ALU.add).then_inc(self.var, 1)

    def root(self, pool):
        c = self.chip
        for part in range(2):
            at = slice(self.batches(part).start, self.batches(part).stop)
            pool.wait_ge(self.var, part + 1)
            c.nc.gpsimd.tensor_tensor(c.rstd[:, at], c.ve[:, at], c.mhalf[:, at], ALU.pow).then_inc(self.rstd, 1)

    def scale(self, dve, b):
        c = self.chip
        mean, rstd = self.scalars(dve, b)
        c.nc.vector.tensor_scalar(self.place(b)[1], c.x[:, bass.ds(b * D, D)], mean, rstd,
                                  ALU.subtract, ALU.mult).then_inc(self.z, 1)

    def turn(self, pe, b):
        t, z = self.place(b)
        pe.wait_ge(self.z, b + 1)
        pe.wait_ge(t.free, t.n)
        turn(self.chip, t.tile, z).then_inc(t.full, 1)

    def split_hi(self, act, b):
        c, t = self.chip, self.place(b)[0]
        act.wait_ge(t.full, t.n)
        c.nc.scalar.activation(c.hT[0][:, bass.ds(b * D, D)], t.tile[:], ACT.Copy).then_inc(self.hi, 1)

    def split_lo(self, dve, b):
        c, t = self.chip, self.place(b)[0]
        dve.wait_ge(self.hi, b + 1)
        at = bass.ds(b * D, D)
        c.nc.vector.tensor_tensor(c.hT[1][:, at], t.tile[:], c.hT[0][:, at], ALU.subtract).then_inc(t.free, 1)

    def vector_rows(self, dve):
        self.scale(dve, 0)
        for b in range(NB):
            if b + 1 < NB:
                self.scale(dve, b + 1)
            self.split_lo(dve, b)


class PairNorm(Norm):

    def __init__(self, chip, sem, turns, z, name, scratch):
        super().__init__(chip, sem, turns, z, name)
        self.st, self.mv, self.ve, self.rs = carve(scratch, [(12, F32), (4, F32), (2, F32), (2, F32)])
        self.carrier = sem(f"{name}_carrier")
        self.i = 0

    def pair_stats(self, dve, h, i):
        nc, b = self.chip.nc, h * 2 + i
        st, mv = self.st[:, 6 * i:6 * i + 6], self.mv[:, 2 * i:2 * i + 2]
        nc.vector.bn_stats(st, self.chip.x[:, bass.ds(b * D, D)]).then_inc(self.stats_done, 1)
        dve.wait_ge(self.stats_done, b * 2 + 1)
        dve.sem_inc(self.carrier, 1)
        nc.vector.bn_aggr(mv, st).then_inc(self.stats_done, 1)
        dve.wait_ge(self.stats_done, b * 2 + 2)
        nc.vector.tensor_scalar(self.ve[:, i:i + 1], mv[:, 1:2], EPS, None, ALU.add).then_inc(self.var, 1)

    def pair_root(self, pool, h, i):
        pool.wait_ge(self.var, h * 2 + i + 1)
        self.chip.nc.gpsimd.tensor_tensor(self.rs[:, i:i + 1], self.ve[:, i:i + 1], self.chip.mhalf[:, 0:1],
                                          ALU.pow).then_inc(self.rstd, 1)

    def pair_scale(self, dve, h, i):
        self.i = i
        self.scale(dve, h * 2 + i)

    def scalars(self, dve, b):
        dve.wait_ge(self.rstd, b + 1)
        return self.mv[:, 2 * self.i:2 * self.i + 1], self.rs[:, self.i:self.i + 1]


class Splitting:

    def __init__(self, chip, sem, slot, staged, steps):
        self.chip, self.slot, self.staged, self.steps, self.width = chip, slot, staged, steps, 2 * MAT // steps
        self.hi, self.done = sem("background_hi"), sem("background_done")

    def columns(self, t, step):
        return t[:].rearrange("p s n -> p (s n)")[:, bass.ds(step * self.width + self.slot * MAT, self.width)]

    def source(self, step):
        return self.chip.stage[:].rearrange("p s n -> p (s n)")[:, bass.ds(step * self.width, self.width)]

    def split_hi(self, act, step):
        c = self.chip
        c.nc.scalar.activation(self.columns(c.w[0], step), self.source(step), ACT.Copy).then_inc(self.hi, 1)

    def split_lo(self, pool, step):
        c = self.chip
        pool.wait_ge(self.hi, step + 1)
        c.nc.gpsimd.tensor_tensor(self.columns(c.w[1], step), self.source(step), self.columns(c.w[0], step),
                                  ALU.subtract).then_inc(self.done, 1)

    def wait_staged(self, act, buf):
        act.wait_ge(self.chip.staged[buf], self.staged[buf])

    def prefetch(self, sp, mats):
        for i, mat in enumerate(mats):
            sp.wait_ge(self.done, (i + 1) * self.steps // 2)
            self.chip.load_weight(sp, mat, i)


def begin_layer(chip, plan, prefetch, start=False):
    nc, io = chip.nc, chip.io
    cut = MAT // 2
    cstage = chip.big[:, NB * D:2 * NB * D]
    assert BIAS.stop <= NB * D and ROWS.start >= 2 * NB * D
    with chip.begin():
        sem = chip.sem
        T = Ring("T", chip.psum[0:2], sem)
        norm = Norm(chip, sem, T)
        hi, lo_dve, lo_pool, ctx_in, ctx_hi, const = (
            sem(n) for n in ("weight_hi", "weight_lo_dve", "weight_lo_pool", "ctx_in", "ctx_hi", "const"))
        at = [n if not start else 0 for n in chip.n_staged]
        due = []
        for i in range(len(plan)):
            if i >= 2 or start:
                at[i % 2] += 16
            due.append(at[i % 2])
        def quarter(n):
            return slice(n * (NB // 4) * D, (n + 1) * (NB // 4) * D)

        with nc.Block() as block:

            @block.sync
            def _(sp):
                if start:
                    for h in range(2):
                        part = slice(h * NB // 2 * D, (h + 1) * NB // 2 * D)
                        sp.dma_start(chip.x[:, part], io["x"][:, part]).then_inc(chip.loaded, 16)
                    sp.dma_start(chip.ident[:], io["ident"]).then_inc(chip.loaded, 16)
                    sp.dma_start(chip.half[:], io["half"]).then_inc(chip.loaded, 16)
                    for i in range(2):
                        chip.load_weight(sp, plan[i][0], i)
                    for i, row in enumerate((V_QW, V_QB, V_KW, V_KB)):
                        sp.dma_start(chip.big[:, ROWS][:, i * D:(i + 1) * D],
                                     io["vectors"][row:row + 1, :].partition_broadcast(P)).then_inc(chip.tabled, 16)
                    sp.dma_start(cstage, io["ctxT"]).then_inc(ctx_in, 16)
                    sp.dma_start(chip.big[:, BIAS], io["alibi"]).then_inc(chip.tabled, 16)
                for i, mat in enumerate([m for m, _ in plan[2:]] + prefetch):
                    sp.wait_ge(lo_dve, i + 1)
                    sp.wait_ge(lo_pool, i + 1)
                    chip.load_weight(sp, mat, i % 2)

            @block.tensor
            def _(pe):
                if start:
                    pe.wait_ge(chip.loaded, 64)
                for b in range(NB):
                    norm.turn(pe, b)

            @block.scalar
            def _(act):
                def weight(i):
                    act.wait_ge(chip.staged[i % 2], due[i])
                    nc.scalar.activation(chip.w[0][:, plan[i][1], :], chip.stage[:, i % 2, :], ACT.Copy).then_inc(hi, 1)

                for i in range(min(2, len(plan))):
                    weight(i)
                for b in range(NB):
                    norm.split_hi(act, b)
                    if start and b >= NB // 2:
                        act.wait_ge(ctx_in, 16)
                        at = quarter(b - NB // 2)
                        nc.scalar.activation(chip.cT[0][:, at], cstage[:, at], ACT.Copy).then_inc(ctx_hi, 1)
                for i in range(2, len(plan)):
                    weight(i)

            @block.vector
            def _(dve):
                if start:
                    dve.wait_ge(chip.loaded, 64)
                def weight(i):
                    slot = plan[i][1]
                    dve.wait_ge(hi, i + 1)
                    nc.vector.tensor_tensor(chip.w[1][:, slot, 0:cut], chip.stage[:, i % 2, 0:cut],
                                            chip.w[0][:, slot, 0:cut], ALU.subtract).then_inc(lo_dve, 1)

                norm.stats(dve, 0)
                norm.stats(dve, 1)
                early = 2 if start else 0
                for i in range(early):
                    weight(i)
                norm.vector_rows(dve)
                for i in range(early, len(plan)):
                    weight(i)

            @block.gpsimd
            def _(pool):
                T.credit(pool)
                if start:
                    nc.gpsimd.memset(chip.mhalf[:], -0.5).then_inc(const, 1)
                    pool.wait_ge(const, 1)
                norm.root(pool)
                for i, (_, slot) in enumerate(plan):
                    if start and i == 2:
                        for n in range(4):
                            at = quarter(n)
                            pool.wait_ge(ctx_hi, n + 1)
                            nc.gpsimd.tensor_tensor(chip.cT[1][:, at], cstage[:, at], chip.cT[0][:, at], ALU.subtract)
                    pool.wait_ge(hi, i + 1)
                    nc.gpsimd.tensor_tensor(chip.w[1][:, slot, cut:], chip.stage[:, i % 2, cut:],
                                            chip.w[0][:, slot, cut:], ALU.subtract).then_inc(lo_pool, 1)


SELF_ORDER = ["""
    +q_0 scores_2 probs_0 exp_2 +q_1 +q_2 p_lo_0 probs_1 scores_3 pv_0 +q_3 probs_2 exp_3 p_lo_1 +q_take_0
    scores_4 +k_0 +k_1 exp_4 pv_1 +k_2 +k_3 p_lo_2 +q_norm_0 scores_5 +k_take_0 pv_2 probs_3 +v_0 exp_5
    p_lo_3 scores_6 probs_4 split_0 pv_3 exp_6 +v_1 +q_turn_0 +k_norm_0 p_lo_4 scores_7 +q_stack_0 probs_5
    exp_7 pv_4 o_take_0 +k_turn_0 p_lo_5 +v_2 out_turn_0 +k_stack_0 out_lo_0 +v_3 pv_5 +scores_0 probs_6
    +q_norm_1 +exp_0 +q_turn_1 p_lo_6 +scores_1 probs_7 out_0 +k_norm_1 +q_stack_1 +exp_1 pv_6 out_1 p_lo_7
    +v_clip_0 pv_7 +k_turn_1 o_take_1 out_turn_1 +v_take_0 out_lo_1 +k_stack_1 out_2 out_3 out_take_0
""", """
    scores_2 probs_0 exp_2 +q_0 +q_1 p_lo_0 scores_3 +q_2 probs_1 pv_0 +q_3 exp_3 +k_0 p_lo_1 +k_1 +q_take_0
    +q_norm_0 scores_4 probs_2 p_lo_2 exp_4 pv_1 +k_2 +k_3 scores_5 +k_take_0 +k_norm_0 +q_norm_1 probs_3
    exp_5 pv_2 +v_0 p_lo_3 scores_6 probs_4 pv_3 p_lo_4 +q_turn_0 scores_7 +v_1 +q_stack_0 probs_5 o_take_0
    +v_2 p_lo_5 +k_turn_0 split_0 pv_4 +k_norm_1 exp_6 out_turn_0 +k_stack_0 out_lo_0 +scores_0 exp_7 pv_5
    probs_6 +exp_0 +v_3 +q_turn_1 out_0 p_lo_6 probs_7 +q_stack_1 p_lo_7 +scores_1 +k_turn_1 pv_6 pv_7
    +v_clip_0 o_take_1 out_1 out_turn_1 out_lo_1 out_2 +k_stack_1 out_3 out_take_0 +exp_1 +v_take_0
"""]
SELF_FRONT = """
    q_0 q_1 q_2 q_3 q_take_0 k_0 k_1 k_2 k_3 k_take_0 q_norm_0 k_norm_0 v_0 v_1 v_2 v_3 v_clip_0 v_take_0 q_norm_1
    k_norm_1 q_turn_0 k_turn_0 q_stack_0 k_stack_0 scores_0 exp_0 q_turn_1 k_turn_1 scores_1 exp_1 q_stack_1 k_stack_1
"""


def stages(text):
    return [(w.lstrip("+").rpartition("_")[0], int(w[-1]), w[0] == "+") for w in text.split()]


def turned(what, n):
    return {"q_turn": [f"q{n}"], "k_turn": [f"k{n}"], "probs": [f"p{n}"], "out_turn": [f"out{n}"]}.get(what, [])


def self_attention(chip, layer, slots, coming, prefetch, late=None):
    nc, io = chip.nc, chip.io
    first = layer == 0
    nkv = NH if first else NKV
    _, qd, kd, qc, kc, qw, kw, _, sB, prob, hold, pT_hi, pT_lo = carve(chip.big, [
        (NG * 512, F32), (1024, F32), (1024, F32), (512, F32), (512, F32), (512, F32), (512, F32), (2048, F32),
        (2048, F32), (2048, F32), (1024, F16), (1024, F16), (1024, F16)])
    o, oh, ol, nmax, rinv, qst, qmv, qve, qrs, qS, kT_, kS_, vc, v_hi, v_lo = carve(chip.small, [
        (512, F32), (512, F16), (512, F16), (16, F32), (32, F32), (12, F32), (4, F32), (2, F32), (2, F32),
        (1024, F16), (1024, F16), (1024, F16), (512, F32), (NH * 17, F16), (NH * 17, BF16)])
    bias, rows_ = chip.big[:, BIAS], chip.big[:, ROWS]
    pT, v_aug = (pT_hi, pT_lo), (v_hi, v_lo)
    group = [[((g // 4) * 4 + i, g % 4, ((g // 4) * 4 + i) * 4 + g % 4) for i in range(GH)] for g in range(NG)]
    raw = {"q": (qc, qw, qd, 0), "k": (kc, kw, kd, 1)}
    q_pair, stackT, stackS = qS, kT_, kS_
    front, order = stages(SELF_FRONT), stages(SELF_ORDER[layer])
    front_T = [u for what, n, _ in front for u in turned(what, n)]
    body_T = [u for what, n, _ in order for u in turned(what, n)]
    last_T = [u for what, n, ahead in order if not ahead for u in turned(what, n)]
    front_A, body_A, last_A = ["q", "k", "v"], ["q", "k", "v", "out"], ["out"]

    with chip.begin():
        sem = chip.sem
        A = Ring("A", chip.psum[0:2], sem)
        T = Ring("T", chip.psum[2:4], sem)
        S = Ring("S", chip.psum[4:6], sem)
        O = Ring("O", chip.psum[6:8], sem)
        qk_chain, qk_var, qk_rstd, qk_z, qk_w, qk_ready = (
            sem(n) for n in ("qk_chain", "qk_var", "qk_rstd", "qk_z", "qk_w", "qk_ready"))
        stacked, v_clipped, v_hi_ready, v_ready, carrier = (
            sem(n) for n in ("stacked", "v_clipped", "v_hi_ready", "v_ready", "carrier"))
        held, maxed, prob_ready, p_hi, summed, o_hi, prepared = (
            sem(n) for n in ("held", "maxed", "prob_ready", "p_hi", "summed", "o_hi", "prepared"))

        staged = list(chip.n_staged)
        background = Splitting(chip, sem, coming, [staged[0] + (0 if late is None else 16), staged[1]], NB)
        o_weight_hi, o_weight = sem("output_weight_hi"), sem("output_weight")

        def place(ahead, body, last, where, name):
            if where == "ahead":
                return ahead.index(name)
            if where == "body":
                return len(ahead) + body.index(name)
            return len(ahead) + (NB - 1) * len(body) + last.index(name)

        def t_use(where, name, it):
            return T.use(place(front_T, body_T, last_T, where, name), it, len(body_T) if where == "body" else 0)

        def a_use(where, name, it):
            return A.use(place(front_A, body_A, last_A, where, name), it, len(body_A) if where == "body" else 0)

        def schedule(eng, step):
            for what, g, _ in front:
                step("ahead", what, g, 0, 0)
            with eng.Fori(0, NB - 1) as it:
                for what, g, ahead in order:
                    step("body", what, g, it + 1 if ahead else it, it)
            for what, g, ahead in order:
                if not ahead:
                    step("last", what, g, NB - 1, 0)

        def values(t):
            return t[:, 0:nkv * 17].rearrange("p (h k) -> p h k", k=17)[:, :, 0:HD]

        clipped = vc[:, 0:nkv * HD].rearrange("p (h k) -> p h k", k=HD)

        with nc.Block() as block:

            @block.sync
            def _(sp):
                if late is not None:
                    sp.wait_ge(o_weight, 1)
                    chip.load_weight(sp, late, 0)
                background.prefetch(sp, prefetch)

            @block.gpsimd
            def _(pool):
                for ring in (A, T, S, O):
                    ring.credit(pool)
                nc.gpsimd.memset(v_hi, 1.0).then_inc(prepared, 1)
                nc.gpsimd.memset(v_lo, 0.0).then_inc(prepared, 1)
                if first:
                    pool.wait_ge(chip.tabled, 80)
                    nc.gpsimd.tensor_scalar(rows_[:, 0:2 * D], rows_[:, 0:2 * D], HD ** -0.5, 1.0, ALU.mult,
                                            ALU.mult).then_inc(prepared, 1)
                    pool.wait_ge(prepared, 3)

                if late is not None:
                    pool.wait_ge(o_weight_hi, 1)
                    hi, lo = chip.weight(slots["o"])
                    nc.gpsimd.tensor_tensor(lo, chip.stage[:, 0, :], hi, ALU.subtract).then_inc(o_weight, 1)

                def step(where, what, g, b, it):
                    if first and what in ("q_take", "k_take"):
                        i = raw[what[0]][3]
                        pool.wait_ge(qk_var, b * 2 + i + 1)
                        nc.gpsimd.tensor_tensor(qrs[:, i:i + 1], qve[:, i:i + 1], chip.mhalf[:, 0:1],
                                                ALU.pow).then_inc(qk_rstd, 1)
                    if first and what in ("q_norm", "k_norm"):
                        c, w, d, i = raw[what[0]]
                        half = slice(g * 256, (g + 1) * 256)
                        pool.wait_ge(qk_z, b * 2 + i + 1)
                        weight, shift = (rows_[:, (2 * i + j) * D:(2 * i + j + 1) * D][:, half] for j in range(2))
                        nc.gpsimd.tensor_tensor(w[:, half], c[:, half], weight, ALU.mult).then_inc(qk_w, 1)
                        pool.wait_ge(qk_w, b * 4 + 2 * g + i + 1)
                        def twice(ap):
                            return ap.rearrange("p (h k) -> p h k", k=HD).unsqueeze(2).to_broadcast([P, 16, 2, HD])

                        out = d[:, g * 512:(g + 1) * 512].rearrange("p (h s k) -> p h s k", s=2, k=HD)
                        nc.gpsimd.tensor_tensor(out, twice(w[:, half]), twice(shift), ALU.add).then_inc(qk_ready, 1)
                    if not first and what in ("q_norm", "k_norm"):
                        a = a_use(where, what[0], it)
                        c, _, d, _ = raw[what[0]]
                        n, times = (16, 2) if what[0] == "q" else (NKV // 2, 8)
                        pool.wait_ge(a.free, a.done)
                        pool.sem_inc(carrier, 1)
                        src = c[:, g * n * HD:(g + 1) * n * HD].rearrange("p (h k) -> p h k", k=HD)
                        nc.gpsimd.tensor_copy(d[:, g * 512:(g + 1) * 512].rearrange("p (h s k) -> p h s k", s=times, k=HD),
                                              src.unsqueeze(2).to_broadcast([P, n, times, HD])).then_inc(qk_ready, 1)
                    if what == "split":
                        background.split_lo(pool, b)
                    if what == "v_take":
                        pool.wait_ge(v_hi_ready, b + 1)
                        nc.gpsimd.tensor_tensor(values(v_lo), clipped, values(v_hi), ALU.subtract).then_inc(v_ready, 1)

                schedule(nc.gpsimd, step)

            @block.tensor
            def _(pe):
                def step(where, what, g, b, it):
                    if what in ("q", "k", "v"):
                        a = a_use(where, what, it)
                        if g == 0:
                            pe.wait_ge(a.free, a.n)
                        first_col, width = (0, D) if first or what == "q" else (0 if what == "k" else P, P)
                        w = columns(chip.weight(slots[what]), g * D + first_col, width)
                        last = product(nc, a.tile[:, 0:width], lambda half, c: tokens(chip.hT, b)(half, g), w, 1,
                                       start=g == 0, stop=g == CH - 1)
                        if g == CH - 1:
                            last.then_inc(a.full, 1)
                    if what in ("q_turn", "k_turn"):
                        d, i = raw[what[0]][2:]
                        pe.wait_ge(qk_ready, b * 4 + 2 * g + i + 1)
                        t = t_use(where, f"{what[0]}{g}", it)
                        pe.wait_ge(t.free, t.n)
                        turn(chip, t.tile, d[:, g * 512:(g + 1) * 512]).then_inc(t.full, 1)
                    if what == "scores":
                        if g % 4 == 0:
                            pe.wait_ge(stacked, b * 2 + g // 4 + 1)
                        s = S.use(g, b, NG)
                        if first:
                            pe.wait_ge(s.free, s.n)
                        elif where != "ahead":
                            pe.wait_ge(prob_ready, b * NG + g - 1)
                        for i, (tile, rg, _) in enumerate(group[g]):
                            at = slice(32 * rg, 32 * rg + 32)
                            lhs = q_pair[at, tile * P:(tile + 1) * P]
                            nc.tensor.matmul(s.tile[:, i * P:(i + 1) * P], lhs, stackT[at, tile * P:(tile + 1) * P],
                                             start=True, stop=False)
                            last = nc.tensor.matmul(s.tile[:, i * P:(i + 1) * P], lhs,
                                                    stackS[at, tile * P:(tile + 1) * P], start=False, stop=True)
                        last.then_inc(s.full, 1)
                    if what == "probs":
                        pe.wait_ge(prob_ready, b * NG + g + 1)
                        t = t_use(where, f"p{g}", it)
                        pe.wait_ge(t.free, t.n)
                        turn(chip, t.tile, prob[:, (g % 4) * 512:(g % 4 + 1) * 512]).then_inc(t.full, 1)
                    if what == "pv":
                        t = t_use(where, f"p{g}", it)
                        pe.wait_ge(t.free, t.done)
                        if g == 0:
                            pe.wait_ge(v_ready, b + 1)
                        u = O.use(g // 4, b, 2)
                        if g % 4 == 0:
                            pe.wait_ge(u.free, u.n)
                        for i, (tile, rg, head) in enumerate(group[g]):
                            at = (i * 4 + rg) * 17
                            kv = head if first else tile
                            src = (g % 2) * 512 + i * P
                            last = product(nc, u.tile[:, at:at + 17], lambda half, c: pT[half][:, src:src + P],
                                           lambda half, c: v_aug[half][:, kv * 17:(kv + 1) * 17], 1)
                        if g % 4 == 3:
                            last.then_inc(u.full, 1)
                    if what == "out_turn":
                        u = O.use(g, b, 2)
                        pe.wait_ge(u.free, u.done)
                        t = t_use(where, f"out{g}", it)
                        pe.wait_ge(t.free, t.n)
                        turn(chip, t.tile, o[:, g * 256:(g + 1) * 256], 2).then_inc(t.full, 1)
                    if what == "out":
                        a = a_use(where, "out", it)
                        if g % 2 == 0:
                            t = t_use(where, f"out{g // 2}", it)
                            pe.wait_ge(t.free, t.done)
                        if g == 0:
                            pe.wait_ge(a.free, a.n)
                            if late is not None:
                                pe.wait_ge(o_weight, 1)
                        last = product(nc, a.tile[:], lambda half, c: (oh, ol)[half][:, g * P:(g + 1) * P],
                                       columns(chip.weight(slots["o"]), g * D), 1, start=g == 0, stop=g == CH - 1)
                        if g == CH - 1:
                            last.then_inc(a.full, 1)

                schedule(nc.tensor, step)

            @block.scalar
            def _(act):
                if late is not None:
                    act.wait_ge(chip.staged[0], staged[0])
                    nc.scalar.activation(chip.weight(slots["o"])[0], chip.stage[:, 0, :], ACT.Copy).then_inc(o_weight_hi, 1)

                def step(where, what, g, b, it):
                    if not first and what in ("q_take", "k_take"):
                        a = a_use(where, what[0], it)
                        act.wait_ge(a.full, a.n)
                        if what[0] == "q":
                            nc.scalar.activation(qc, a.tile[:], ACT.Copy, scale=HD ** -0.5).then_inc(a.free, 1)
                        else:
                            nc.scalar.activation(kc[:, 0:P], a.tile[:, 0:P], ACT.Copy).then_inc(a.free, 1)
                    if what in ("q_turn", "k_turn"):
                        t = t_use(where, f"{what[0]}{g}", it)
                        act.wait_ge(t.full, t.n)
                        nc.scalar.activation(hold[:, t.slot * 512:(t.slot + 1) * 512], t.tile[:],
                                             ACT.Copy).then_inc(held, 1)
                    if what == "split":
                        background.wait_staged(act, 0)
                        background.wait_staged(act, 1)
                        background.split_hi(act, b)
                    if what == "exp":
                        s = S.use(g, b, NG)
                        if first:
                            act.wait_ge(s.free, s.done)
                        else:
                            act.wait_ge(maxed, b * NG + g + 1)
                        for i in range(GH):
                            at = (g % 4) * 512 + i * P
                            src = sB[:, at:at + P] if first else s.tile[:, i * P:(i + 1) * P]
                            m = (g % 4) * GH + i
                            last = nc.scalar.activation(prob[:, at:at + P], src, ACT.Exp, bias=nmax[:, m:m + 1],
                                                        scale=-1.0 if first else 1.0)
                        last.then_inc(prob_ready, 1)
                    if what == "probs":
                        t = t_use(where, f"p{g}", it)
                        act.wait_ge(t.full, t.n)
                        nc.scalar.activation(pT[0][:, (g % 2) * 512:(g % 2 + 1) * 512], t.tile[:], ACT.Copy,
                                             scale=PSCALE).then_inc(p_hi, 1)
                    if what == "v_take":
                        act.wait_ge(v_clipped, b + 1)
                        if where == "body":
                            u = O.use(1, it, 2)
                            act.wait_ge(u.full, u.n)
                        nc.scalar.activation(values(v_hi), clipped, ACT.Copy).then_inc(v_hi_ready, 1)
                    if what == "out_turn":
                        t = t_use(where, f"out{g}", it)
                        act.wait_ge(t.full, t.n)
                        nc.scalar.activation(oh[:, g * 256:(g + 1) * 256], t.tile[:, 0:256], ACT.Copy).then_inc(o_hi, 1)

                schedule(nc.scalar, step)

            @block.vector
            def _(dve):
                dve.wait_ge(prepared, 3 if first else 2)
                if first:
                    dve.wait_ge(chip.tabled, 80)

                def step(where, what, g, b, it):
                    if first and what in ("q_take", "k_take"):
                        c, _, _, i = raw[what[0]]
                        a = a_use(where, what[0], it)
                        dve.wait_ge(a.full, a.n)
                        nc.vector.tensor_scalar(c, a.tile[:], CLIP, -CLIP, ALU.min, ALU.max).then_inc(a.free, 1)
                        dve.wait_ge(a.free, a.done)
                        st = qst[:, 6 * i:6 * i + 6]
                        nc.vector.bn_stats(st, c).then_inc(qk_chain, 1)
                        dve.wait_ge(qk_chain, b * 4 + 2 * i + 1)
                        dve.sem_inc(carrier, 1)
                        nc.vector.bn_aggr(qmv[:, 2 * i:2 * i + 2], st).then_inc(qk_chain, 1)
                        dve.wait_ge(qk_chain, b * 4 + 2 * i + 2)
                        nc.vector.tensor_scalar(qve[:, i:i + 1], qmv[:, 2 * i + 1:2 * i + 2], EPS, None,
                                                ALU.add).then_inc(qk_var, 1)
                    if first and what in ("q_norm", "k_norm") and g == 0:
                        c, _, _, i = raw[what[0]]
                        dve.wait_ge(qk_rstd, b * 2 + i + 1)
                        nc.vector.tensor_scalar(c, c, qmv[:, 2 * i:2 * i + 1], qrs[:, i:i + 1],
                                                ALU.subtract, ALU.mult).then_inc(qk_z, 1)
                    if what == "v_clip":
                        a = a_use(where, "v", it)
                        dve.wait_ge(a.full, a.n)
                        src = a.tile[:, 0:nkv * HD].rearrange("p (h k) -> p h k", k=HD)
                        if first:
                            nc.vector.tensor_scalar(clipped, src, CLIP, -CLIP, ALU.min, ALU.max).then_inc(v_clipped, 1)
                        else:
                            nc.vector.tensor_copy(clipped, src).then_inc(v_clipped, 1)
                        dve.wait_ge(v_clipped, b + 1)
                        dve.sem_inc(a.free, 1)
                    if what in ("q_stack", "k_stack"):
                        t = t_use(where, f"{what[0]}{g}", it)
                        dve.wait_ge(held, b * 4 + 2 * g + (1 if what[0] == "q" else 2))
                        h = hold[:, t.slot * 512:(t.slot + 1) * 512]
                        at = slice(g * 512, (g + 1) * 512)
                        if what[0] == "q":
                            nc.vector.scalar_tensor_tensor(out=q_pair[:, at], in0=h, scalar=chip.half[:, 0:1],
                                                           in1=t.tile[:], op0=ALU.mult, op1=ALU.add).then_inc(t.free, 1)
                        else:
                            nc.vector.scalar_tensor_tensor(out=stackT[:, at], in0=h, scalar=chip.half[:, 0:1],
                                                           in1=t.tile[:], op0=ALU.mult, op1=ALU.add)
                            nc.vector.scalar_tensor_tensor(out=stackS[:, at], in0=h, scalar=chip.half[:, 1:2],
                                                           in1=t.tile[:], op0=ALU.mult, op1=ALU.add).then_inc(t.free, 1)
                        if what[0] == "k":
                            dve.wait_ge(t.free, t.done)
                            dve.sem_inc(stacked, 1)
                    if what == "scores":
                        s = S.use(g, b, NG)
                        if first:
                            dve.wait_ge(s.full, s.n)
                            dve.sem_inc(carrier, 1)
                            for i in range(GH):
                                at, m = (g % 4) * 512 + i * P, (g % 4) * GH + i
                                last = nc.vector.tensor_tensor_reduce(
                                    out=sB[:, at:at + P], in0=s.tile[:, i * P:(i + 1) * P],
                                    in1=bias[:, (g * GH + i) * P:(g * GH + i + 1) * P], scale=-1.0, scalar=0.0,
                                    op0=ALU.add, op1=ALU.min, accum_out=nmax[:, m:m + 1])
                            last.then_inc(s.free, 1)
                        else:
                            dve.wait_ge(s.full, s.n)
                            nc.vector.tensor_reduce(nmax[:, (g % 4) * GH:(g % 4 + 1) * GH], heads(s.tile[:]), AX, ALU.max,
                                                    negate=True).then_inc(maxed, 1)
                    if what == "p_lo":
                        t = t_use(where, f"p{g}", it)
                        at = slice((g % 2) * 512, (g % 2 + 1) * 512)
                        dve.wait_ge(p_hi, b * NG + g + 1)
                        nc.vector.scalar_tensor_tensor(out=pT[1][:, at], in0=t.tile[:], scalar=PSCALE, in1=pT[0][:, at],
                                                       op0=ALU.mult, op1=ALU.subtract).then_inc(t.free, 1)
                    if what == "o_take":
                        u = O.use(g, b, 2)
                        dve.wait_ge(u.full, u.n)
                        n = 16
                        src = u.tile[:, 0:n * 17].rearrange("p (h k) -> p h k", k=17)
                        r = rinv[:, g * n:(g + 1) * n]
                        nc.vector.reciprocal(r, src[:, :, HD]).then_inc(summed, 1)
                        dve.wait_ge(summed, b * 2 + g + 1)
                        dst = o[:, g * 256:(g + 1) * 256].rearrange("p (h k) -> p h k", k=HD)
                        nc.vector.tensor_tensor(dst, src[:, :, 0:HD], spread(r, n, HD), ALU.mult).then_inc(u.free, 1)
                    if what == "out_lo":
                        t = t_use(where, f"out{g}", it)
                        at = slice(g * 256, (g + 1) * 256)
                        dve.wait_ge(o_hi, b * 2 + g + 1)
                        nc.vector.tensor_tensor(ol[:, at], t.tile[:, 0:256], oh[:, at], ALU.subtract).then_inc(t.free, 1)
                    if what == "out_take":
                        a = a_use(where, "out", it)
                        dve.wait_ge(a.full, a.n)
                        at = bass.ds(b * D, D)
                        nc.vector.tensor_tensor(chip.x[:, at], chip.x[:, at], a.tile[:], ALU.add).then_inc(a.free, 1)

                schedule(nc.vector, step)


def rms_stats(nc, dve, src, junk, ss, eps_out, chain, k):
    for i in range(GH):
        at = slice(i * P, (i + 1) * P)
        last = nc.vector.tensor_tensor_reduce(out=junk[:, at], in0=src[:, at], in1=src[:, at], scale=1.0, scalar=0.0,
                                              op0=ALU.mult, op1=ALU.add, accum_out=ss[:, i:i + 1])
    last.then_inc(chain, 1)
    dve.wait_ge(chain, k + 1)
    return nc.vector.tensor_scalar(eps_out, ss, 1.0 / P, EPS, ALU.mult, ALU.add)


def cross_views(chip):
    kT_hi, kT_lo, v_hi, v_lo = carve(chip.big, [(NKV * NB * P, F16)] * 4)
    return (kT_hi, kT_lo), (v_hi, v_lo)


def per_head(t, b):
    return t.rearrange("p (h r) -> p h r", h=NKV)[:, :, bass.ds(b * P, P)]


def cross_keys(chip, k_slots, v_slots, coming, mats, prefetch):
    nc, io = chip.nc, chip.io
    kT, v = cross_views(chip)
    kf, junk, kn, kw, wrow, qrow, ss, ve, rk = carve(chip.small, [
        (1024, F32), (512, F32), (512, F32), (1024, F32), (P, F32), (P, F32), (4, F32), (8, F32), (8, F32)])
    with chip.begin():
        sem = chip.sem
        A = Ring("A", chip.psum[0:4], sem)
        T = Ring("T", chip.psum[4:6], sem)
        copied, squares, var, root, scaled, ready, split, rows_ready = (
            sem(n) for n in ("copied", "squares", "var", "root", "scaled", "ready", "split_hi", "rows_ready"))
        v_split, w_hi, w_lo_dve, w_lo_pool = (sem(n) for n in ("v_hi", "weight_hi", "weight_lo_dve", "weight_lo_pool"))
        norm = Norm(chip, sem, Ring("N", chip.psum[6:7], sem))
        staged = list(chip.n_staged)
        background = Splitting(chip, sem, coming, [n + 16 for n in staged], NB)
        cut = MAT // 2

        def batches(eng, do):
            for half in range(2):
                with eng.Fori(half * NB // 2, (half + 1) * NB // 2) as b:
                    do(b, half)

        def value_lo(eng, i, at):
            return eng.tensor_tensor(chip.w[1][:, v_slots[i], at], chip.stage[:, i, at], chip.w[0][:, v_slots[i], at],
                                     ALU.subtract)

        with nc.Block() as block:

            @block.sync
            def _(sp):
                sp.dma_start(wrow, io["vectors"][V_XKN:V_XKN + 1, 0:P].partition_broadcast(P)).then_inc(rows_ready, 16)
                sp.dma_start(qrow, io["vectors"][V_XQN:V_XQN + 1, 0:P].partition_broadcast(P)).then_inc(rows_ready, 16)
                for i, mat in enumerate(mats):
                    sp.wait_ge(w_lo_dve, i + 1)
                    sp.wait_ge(w_lo_pool, i + 1)
                    chip.load_weight(sp, mat, i)
                background.prefetch(sp, prefetch)

            @block.gpsimd
            def _(pool):
                A.credit(pool)
                T.credit(pool)
                norm.turns.credit(pool)
                for i in range(2):
                    pool.wait_ge(w_hi, i + 1)
                    value_lo(nc.gpsimd, i, slice(cut, MAT)).then_inc(w_lo_pool, 1)
                norm.root(pool)
                pool.wait_ge(rows_ready, 32)
                nc.gpsimd.tensor_tensor(wrow, wrow, qrow, ALU.mult).then_inc(rows_ready, 1)
                pool.wait_ge(rows_ready, 33)
                nc.gpsimd.tensor_scalar(wrow, wrow, P ** -0.5, 1.0, ALU.mult, ALU.mult).then_inc(rows_ready, 1)
                pool.wait_ge(rows_ready, 34)

                def step(b, half):
                    for m in range(2):
                        k = b * 2 + m
                        pool.wait_ge(var, k + 1)
                        nc.gpsimd.tensor_tensor(rk[:, m * 4:m * 4 + 4], ve[:, m * 4:m * 4 + 4], chip.mhalf[:, 0:4],
                                                ALU.pow).then_inc(root, 1)
                        pool.wait_ge(root, k + 1)
                        nc.gpsimd.tensor_tensor(heads(kn), heads(kf[:, m * 512:(m + 1) * 512]),
                                                spread(rk[:, m * 4:m * 4 + 4], GH, P), ALU.mult).then_inc(scaled, 1)
                        pool.wait_ge(scaled, k + 1)
                        nc.gpsimd.tensor_tensor(heads(kw[:, m * 512:(m + 1) * 512]), heads(kn),
                                                wrow.unsqueeze(1).to_broadcast([P, GH, P]), ALU.mult).then_inc(ready, 1)
                    background.split_lo(pool, b)

                batches(nc.gpsimd, step)

            @block.tensor
            def _(pe):
                def step(b, half):
                    for m, slot in enumerate((*k_slots, *v_slots)):
                        if m >= 2:
                            pe.wait_ge(w_lo_dve, m - 1)
                            pe.wait_ge(w_lo_pool, m - 1)
                        a = A.use(m, b, 4)
                        pe.wait_ge(a.free, a.n)
                        product(nc, a.tile[:], tokens(chip.cT, b), columns(chip.weight(slot)), CH).then_inc(a.full, 1)
                    for m in range(2):
                        t = T.use(m, b, 2)
                        pe.wait_ge(ready, b * 2 + m + 1)
                        pe.wait_ge(t.free, t.n)
                        turn(chip, t.tile, kw[:, m * 512:(m + 1) * 512]).then_inc(t.full, 1)
                    norm.turn(pe, b)

                batches(nc.tensor, step)

            @block.scalar
            def _(act):
                for i in range(2):
                    act.wait_ge(chip.staged[i], staged[i])
                    nc.scalar.activation(chip.w[0][:, v_slots[i], :], chip.stage[:, i, :], ACT.Copy).then_inc(w_hi, 1)

                def step(b, half):
                    for m in range(2):
                        a = A.use(m, b, 4)
                        act.wait_ge(a.full, a.n)
                        nc.scalar.activation(kf[:, m * 512:(m + 1) * 512], a.tile[:], ACT.Copy).then_inc(a.free, 1)
                    for m in range(2):
                        a = A.use(2 + m, b, 4)
                        act.wait_ge(a.full, a.n)
                        nc.scalar.activation(per_head(v[0], b)[:, m * 4:m * 4 + 4, :], heads(a.tile[:]),
                                             ACT.Copy).then_inc(v_split, 1)
                    for m in range(2):
                        t = T.use(m, b, 2)
                        act.wait_ge(t.full, t.n)
                        nc.scalar.activation(per_head(kT[0], b)[:, m * 4:m * 4 + 4, :], heads(t.tile[:]),
                                             ACT.Copy).then_inc(split, 1)
                    norm.split_hi(act, b)
                    background.wait_staged(act, half)
                    background.split_hi(act, b)

                batches(nc.scalar, step)

            @block.vector
            def _(dve):
                for i in range(2):
                    dve.wait_ge(w_hi, i + 1)
                    value_lo(nc.vector, i, slice(0, cut)).then_inc(w_lo_dve, 1)
                norm.stats(dve, 0)
                norm.stats(dve, 1)

                def step(b, half):
                    for m in range(2):
                        a = A.use(m, b, 4)
                        dve.wait_ge(a.free, a.done)
                        rms_stats(nc, dve, kf[:, m * 512:(m + 1) * 512], junk, ss, ve[:, m * 4:m * 4 + 4], squares,
                                  b * 2 + m).then_inc(var, 1)
                        dve.wait_ge(var, b * 2 + m + 1)
                    norm.scale(dve, b)
                    for m in range(2):
                        a = A.use(2 + m, b, 4)
                        dve.wait_ge(v_split, b * 2 + m + 1)
                        nc.vector.tensor_tensor(per_head(v[1], b)[:, m * 4:m * 4 + 4, :], heads(a.tile[:]),
                                                per_head(v[0], b)[:, m * 4:m * 4 + 4, :], ALU.subtract).then_inc(a.free, 1)
                    for m in range(2):
                        t = T.use(m, b, 2)
                        dve.wait_ge(split, b * 2 + m + 1)
                        nc.vector.tensor_tensor(per_head(kT[1], b)[:, m * 4:m * 4 + 4, :], heads(t.tile[:]),
                                                per_head(kT[0], b)[:, m * 4:m * 4 + 4, :], ALU.subtract).then_inc(t.free, 1)
                    norm.split_lo(dve, b)

                batches(nc.vector, step)


CROSS_ORDER = [("norm", 2), ("weights", 0), ("q_turn", 1), ("q", 0), ("pv", 3), ("probs", 2), ("scores", 1), ("out", 4)]
LAG = 4


def cross_attention(chip, even, odd):
    nc, io = chip.nc, chip.io
    kT, v = cross_views(chip)
    qf, qn, s_, prob, pn, mask, qh, ql, ph, pl, a0h, a0l, a1h, a1l, junk_, ss, ve, rq, nmax, rs, ri = carve(chip.small, [
        (512, F32), (512, F32), (512, F32), (512, F32), (512, F32), (P, F32), (512, F16), (512, F16), (512, F16),
        (512, F16), (512, F16), (512, F16), (512, F16), (512, F16), (512, F32), (4, F32), (4, F32), (4, F32),
        (4, F32), (4, F32), (4, F32)])
    ah, al = (a0h, a1h), (a0l, a1l)
    n_slots = 2 * NB
    PARTS = NB // 2
    incoming = [odd[0], odd[1], even[0], even[1]]
    base = list(chip.n_staged)

    with chip.begin():
        sem = chip.sem
        A = Ring("A", chip.psum[0:2], sem)
        T = Ring("T", chip.psum[2:4], sem)
        S = Ring("S", chip.psum[4:6], sem)
        O = Ring("O", chip.psum[6:8], sem)
        qf_ready, squares, var, root, qn_ready, q_hi, s_ready, maxed, prob_ready, sums, inv, pn_ready, p_hi, a_hi = (
            sem(n) for n in ("qf_ready", "squares", "var", "root", "qn_ready", "q_hi", "s_ready", "maxed",
                             "prob_ready", "sums", "inv", "pn_ready", "p_hi", "a_hi"))
        w_hi, w_done, got_mask = sem("w_hi"), sem("w_done"), sem("got_mask")

        def one(ring, bank, s, gg):
            return Use(bank, ring.tiles[bank], ring.full[bank], ring.free[bank], gg * n_slots + s + 1)

        def schedule(eng, step):
            def slots(gg, first, end, limit):
                for slot in range(first, end):
                    for what, behind in CROSS_ORDER:
                        if 0 <= slot - behind < limit:
                            step(what, slot - behind, gg, gg * n_slots + (slot - behind))

            slots(0, 0, LAG, n_slots)
            with eng.Fori(0, NKV // 2 - 1) as gg:
                slots(gg, LAG, n_slots + LAG, n_slots + LAG)
            slots(NKV // 2 - 1, LAG, n_slots + LAG, n_slots)

        with nc.Block() as block:

            @block.sync
            def _(sp):
                sp.dma_start(mask, io["mask"]).then_inc(got_mask, 16)
                with nc.sync.Fori(0, NKV // 2) as gg:
                    for m in range(4):
                        sp.wait_ge(w_done, gg * n_slots + PARTS * (m + 1))
                        mat = gg * 4 + (W_XQO + 4 + m)
                        sp.dma_start(chip.stage[:, m % 2, :],
                                     io["weights"][bass.ds(mat, 1), :, :].rearrange("o p n -> p (o n)")
                                     ).then_inc(chip.staged[m % 2], 16)

            @block.gpsimd
            def _(pool):
                for ring in (A, T, S, O):
                    ring.credit(pool)

                def step(what, s, gg, k):
                    if what == "q":
                        pool.wait_ge(var, k + 1)
                        nc.gpsimd.tensor_tensor(rq, ve, chip.mhalf[:, 0:4], ALU.pow).then_inc(root, 1)
                        pool.wait_ge(root, k + 1)
                        nc.gpsimd.tensor_tensor(heads(qn), heads(qf), spread(rq, GH, P), ALU.mult).then_inc(qn_ready, 1)
                    if what == "norm":
                        pool.wait_ge(inv, k + 1)
                        nc.gpsimd.tensor_tensor(heads(pn), heads(prob), spread(ri, GH, P), ALU.mult).then_inc(pn_ready, 1)
                    if what == "weights":
                        m, part = s // PARTS % 4, s % PARTS
                        at = slice(part * D, (part + 1) * D)
                        pool.wait_ge(w_hi, k + 1)
                        nc.gpsimd.tensor_tensor(chip.w[1][:, incoming[m], at], chip.stage[:, m % 2, at],
                                                chip.w[0][:, incoming[m], at], ALU.subtract).then_inc(w_done, 1)

                schedule(nc.gpsimd, step)

            @block.tensor
            def _(pe):
                def step(what, s, gg, k):
                    b, odd_half = s % NB, s // NB % 2
                    if what == "q":
                        if s == NB:
                            pe.wait_ge(w_done, gg * n_slots + PARTS)
                        if s == n_slots:
                            pe.wait_ge(w_done, gg * n_slots + 3 * PARTS)
                        if s == n_slots + LAG - 1:
                            pe.wait_ge(w_done, gg * n_slots + 4 * PARTS)
                        a = one(A, 0, s, gg)
                        pe.wait_ge(a.free, a.n)
                        product(nc, a.tile[:], tokens(chip.hT, b), columns(chip.weight((even, odd)[odd_half][0])),
                                CH).then_inc(a.full, 1)
                    if what == "q_turn":
                        t = one(T, 0, s, gg)
                        pe.wait_ge(qn_ready, k + 1)
                        pe.wait_ge(t.free, t.n)
                        turn(chip, t.tile, qn).then_inc(t.full, 1)
                    if what == "scores":
                        t = one(T, 0, s, gg)
                        pe.wait_ge(t.free, t.done)
                        u = S.use(s, gg, n_slots)
                        pe.wait_ge(u.free, u.n)
                        key = (gg * 2 + s // NB) * (NB * P) + b * P
                        for i in range(GH):
                            last = product(nc, u.tile[:, i * P:(i + 1) * P],
                                           lambda half, c, i=i: (qh, ql)[half][:, i * P:(i + 1) * P],
                                           lambda half, c: kT[half][:, bass.ds(key, P)], 1)
                        last.then_inc(u.full, 1)
                    if what == "probs":
                        t = one(T, 1, s, gg)
                        pe.wait_ge(pn_ready, k + 1)
                        pe.wait_ge(t.free, t.n)
                        turn(chip, t.tile, pn).then_inc(t.full, 1)
                    if what == "pv":
                        t = one(T, 1, s, gg)
                        pe.wait_ge(t.free, t.done)
                        u = O.use(s, gg, n_slots)
                        pe.wait_ge(u.free, u.n)
                        val = (gg * 2 + s // NB) * (NB * P) + b * P
                        product(nc, u.tile[:], lambda half, c: v[half][:, bass.ds(val, P)],
                                lambda half, c: (ph, pl)[half], 1).then_inc(u.full, 1)
                    if what == "out":
                        if s == NB:
                            pe.wait_ge(w_done, gg * n_slots + 2 * PARTS)
                        u = O.use(s, gg, n_slots)
                        pe.wait_ge(u.free, u.done)
                        a = one(A, 1, s, gg)
                        pe.wait_ge(a.free, a.n)
                        product(nc, a.tile[:], lambda half, c: (ah, al)[half][s % 2][:, c * P:(c + 1) * P],
                                columns(chip.weight((even, odd)[odd_half][1])), CH).then_inc(a.full, 1)

                schedule(nc.tensor, step)

            @block.scalar
            def _(act):
                def step(what, s, gg, k):
                    if what == "q":
                        a = one(A, 0, s, gg)
                        act.wait_ge(a.full, a.n)
                        nc.scalar.activation(qf, a.tile[:], ACT.Copy).then_inc(a.free, 1)
                    if what == "q_turn":
                        t = one(T, 0, s, gg)
                        act.wait_ge(t.full, t.n)
                        nc.scalar.activation(qh, t.tile[:], ACT.Copy).then_inc(q_hi, 1)
                    if what == "scores":
                        act.wait_ge(maxed, k + 1)
                        for i in range(GH):
                            at = slice(i * P, (i + 1) * P)
                            last = nc.scalar.activation(prob[:, at], s_[:, at], ACT.Exp, bias=nmax[:, i:i + 1],
                                                        accum_out=rs[:, i:i + 1])
                        last.then_inc(prob_ready, 1)
                    if what == "probs":
                        t = one(T, 1, s, gg)
                        act.wait_ge(t.full, t.n)
                        nc.scalar.activation(ph, t.tile[:], ACT.Copy).then_inc(p_hi, 1)
                    if what == "pv":
                        u = O.use(s, gg, n_slots)
                        act.wait_ge(u.full, u.n)
                        nc.scalar.activation(ah[s % 2], u.tile[:], ACT.Copy, scale=1 / PSCALE).then_inc(a_hi, 1)
                    if what == "weights":
                        m, part = s // PARTS, s % PARTS
                        if part == 0:
                            act.wait_ge(chip.staged[m % 2], gg * 32 + (base[m % 2] + 16 * (m // 2)))
                            if m == 1:
                                act.wait_ge(A.free[1], gg * n_slots + 1)
                            if m == 2:
                                a = one(A, 0, NB - 1, gg)
                                act.wait_ge(a.full, a.n)
                            if m == 3:
                                a = one(A, 1, NB - 1, gg)
                                act.wait_ge(a.full, a.n)
                            if m == 4:
                                a = one(A, 0, n_slots - 1, gg)
                                act.wait_ge(a.full, a.n)
                        at = slice(part * D, (part + 1) * D)
                        nc.scalar.activation(chip.w[0][:, incoming[m % 4], at], chip.stage[:, m % 2, at],
                                             ACT.Copy).then_inc(w_hi, 1)

                schedule(nc.scalar, step)

            @block.vector
            def _(dve):
                dve.wait_ge(got_mask, 16)

                def step(what, s, gg, k):
                    if what == "q":
                        a = one(A, 0, s, gg)
                        dve.wait_ge(a.free, a.done)
                        rms_stats(nc, dve, qf, junk_, ss, ve, squares, k).then_inc(var, 1)
                    if what == "q_turn":
                        t = one(T, 0, s, gg)
                        dve.wait_ge(q_hi, k + 1)
                        nc.vector.tensor_tensor(ql, t.tile[:], qh, ALU.subtract).then_inc(t.free, 1)
                    if what == "scores":
                        u = S.use(s, gg, n_slots)
                        dve.wait_ge(u.full, u.n)
                        nc.vector.tensor_tensor(heads(s_), heads(u.tile[:]),
                                                mask.unsqueeze(1).to_broadcast([P, GH, P]), ALU.add).then_inc(u.free, 1)
                        dve.wait_ge(u.free, u.done)
                        nc.vector.tensor_reduce(nmax, heads(s_), AX, ALU.max, negate=True).then_inc(maxed, 1)
                    if what == "norm":
                        dve.wait_ge(prob_ready, k + 1)
                        nc.vector.tensor_scalar(rs, rs, 1 / PSCALE, None, ALU.mult).then_inc(sums, 1)
                        dve.wait_ge(sums, k + 1)
                        nc.vector.reciprocal(ri, rs).then_inc(inv, 1)
                    if what == "probs":
                        t = one(T, 1, s, gg)
                        dve.wait_ge(p_hi, k + 1)
                        nc.vector.tensor_tensor(pl, t.tile[:], ph, ALU.subtract).then_inc(t.free, 1)
                    if what == "pv":
                        u = O.use(s, gg, n_slots)
                        dve.wait_ge(a_hi, k + 1)
                        nc.vector.scalar_tensor_tensor(out=al[s % 2], in0=u.tile[:], scalar=1 / PSCALE, in1=ah[s % 2],
                                                       op0=ALU.mult, op1=ALU.subtract).then_inc(u.free, 1)
                    if what == "out":
                        a = one(A, 1, s, gg)
                        dve.wait_ge(a.full, a.n)
                        at = slice((s % NB) * D, (s % NB + 1) * D)
                        nc.vector.tensor_tensor(chip.x[:, at], chip.x[:, at], a.tile[:], ALU.add).then_inc(a.free, 1)

                schedule(nc.vector, step)
    for i in range(2):
        chip.n_staged[i] += 16 * 2 * (NKV // 2)


def experts(chip, base_slot, ag_slot, coming, prefetch):
    nc, io = chip.nc, chip.io
    n_ag = NE * RANK + NE + 1
    CHAIN = 10
    bst, bh, bl, brow, thr = carve(chip.big, [(D, F32), (D, F16), (D, BF16), (D, F32), (4, F32)])
    lay = carve(chip.small, [(n_ag + 3, F32), (P, F32), (P, F16), (P, F16), (NE, F32), (NE, F32), (NE, F32),
                             (8, F32)] * 2 + [(20, F32)])
    names = ("hg", "hw", "hi", "lo", "e", "w", "w2", "c")
    bufs = [dict(zip(names, lay[8 * i:8 * i + 8], strict=True)) for i in range(2)]

    def col(i, n):
        return bufs[i]["c"][:, n:n + 1]

    with chip.begin():
        sem = chip.sem
        G = Ring("G", chip.psum[0:2], sem)
        Y = Ring("Y", chip.psum[2:4], sem)
        T = Ring("T", chip.psum[4:6], sem)
        got, b_hi, b_lo, nthr, chain, expo, hw_ready, hw_hi, x_b = (
            sem(n) for n in ("got", "b_hi", "b_lo", "nthr", "chain", "expo", "hw_ready", "hw_hi", "x_bias"))
        coming_in = Norm(chip, sem, Ring("I", chip.psum[6:7], sem), 0, "in")
        going_out = PairNorm(chip, sem, Ring("Z", chip.psum[7:8], sem), 1, "out", lay[-1])
        background = Splitting(chip, sem, coming, list(chip.n_staged), NB // 2)

        def pairs(eng, body):
            body(0, False, True)
            with eng.Fori(1, NB // 2 - 1) as h:
                body(h, True, True)
            body(NB // 2 - 1, True, False)

        with nc.Block() as block:

            @block.sync
            def _(sp):
                sp.dma_start(bst, io["expert_b"]).then_inc(got, 16)
                sp.dma_start(brow, io["vectors"][V_BASE:V_BASE + 1, :].partition_broadcast(P)).then_inc(got, 16)
                sp.dma_start(thr[:, 0:2], io["vectors"][V_BTHR:V_BTHR + 1, 0:2].partition_broadcast(P)).then_inc(got, 16)
                background.prefetch(sp, prefetch)

            @block.gpsimd
            def _(pool):
                for ring in (G, Y, T, coming_in.turns, going_out.turns):
                    ring.credit(pool)
                coming_in.root(pool)
                pool.wait_ge(got, 48)

                def body(h, before, after):
                    for i in range(2):
                        pool.wait_ge(coming_in.z, h * 2 + i + 1)
                        at = bass.ds((h * 2 + i) * D, D)
                        nc.gpsimd.tensor_tensor(chip.x[:, at], chip.x[:, at], brow, ALU.add).then_inc(x_b, 1)
                    if before:
                        for i in range(2):
                            going_out.pair_root(pool, h - 1, i)
                    background.split_lo(pool, h)

                pairs(nc.gpsimd, body)
                for i in range(2):
                    going_out.pair_root(pool, NB // 2 - 1, i)

            @block.tensor
            def _(pe):
                for b in range(2):
                    coming_in.turn(pe, b)

                def base(h, i):
                    y = Y.use(i, h, 2)
                    pe.wait_ge(y.free, y.n)
                    product(nc, y.tile[:], tokens(chip.hT, h * 2 + i), columns(chip.weight(base_slot)), CH, stop=False)

                def weighted(h, i):
                    t = T.use(i, h, 2)
                    pe.wait_ge(hw_ready, h * 2 + i + 1)
                    pe.wait_ge(t.free, t.n)
                    turn(chip, t.tile, bufs[i]["hw"], 1).then_inc(t.full, 1)

                def body(h, before, after):
                    for i in range(2):
                        u, rows = G.use(i, h, 2), coming_in.place(h * 2 + i)[0]
                        pe.wait_ge(rows.free, rows.done)
                        pe.wait_ge(u.free, u.n)
                        product(nc, u.tile[:, 0:n_ag], tokens(chip.hT, h * 2 + i),
                                columns(chip.weight(ag_slot), 0, n_ag), CH).then_inc(u.full, 1)
                    base(h, 0)
                    if after:
                        coming_in.turn(pe, h * 2 + 2)
                    base(h, 1)
                    for i in range(2):
                        weighted(h, i)
                    if after:
                        coming_in.turn(pe, h * 2 + 3)
                    pe.wait_ge(b_lo, 1)
                    for i in range(2):
                        t, y = T.use(i, h, 2), Y.use(i, h, 2)
                        pe.wait_ge(t.free, t.done)
                        product(nc, y.tile[:], lambda half, c, i=i: bufs[i][("hi", "lo")[half]],
                                lambda half, c: (bh, bl)[half], 1, start=False).then_inc(y.full, 1)
                        if before:
                            going_out.turn(pe, h * 2 - 2 + i)

                pairs(nc.tensor, body)
                for i in range(2):
                    going_out.turn(pe, NB - 2 + i)

            @block.scalar
            def _(act):
                act.wait_ge(got, 48)
                nc.scalar.activation(bh, bst, ACT.Copy).then_inc(b_hi, 1)
                nc.scalar.activation(thr[:, 2:3], thr[:, 0:1], ACT.Copy, scale=-1.0).then_inc(nthr, 1)
                act.wait_ge(nthr, 1)
                for b in range(2):
                    coming_in.split_hi(act, b)

                def body(h, before, after):
                    for i in range(2):
                        hg = bufs[i]["hg"]
                        act.wait_ge(chain, h * (2 * CHAIN) + (i + 1))
                        nc.scalar.activation(bufs[i]["e"], hg[:, P:P + NE], ACT.Exp, bias=col(i, 0),
                                             accum_out=col(i, 1))
                        nc.scalar.activation(col(i, 2), hg[:, P + NE:P + NE + 1], ACT.Exp, bias=thr[:, 2:3],
                                             scale=-1.0).then_inc(expo, 1)
                    if after:
                        coming_in.split_hi(act, h * 2 + 2)
                    for i in range(2):
                        t = T.use(i, h, 2)
                        act.wait_ge(t.full, t.n)
                        nc.scalar.activation(bufs[i]["hi"], t.tile[:, 0:P], ACT.Copy).then_inc(hw_hi, 1)
                    if after:
                        coming_in.split_hi(act, h * 2 + 3)
                    if before:
                        going_out.split_hi(act, h * 2 - 2)
                        going_out.split_hi(act, h * 2 - 1)
                    background.wait_staged(act, 0)
                    background.wait_staged(act, 1)
                    background.split_hi(act, h)

                pairs(nc.scalar, body)
                for i in range(2):
                    going_out.split_hi(act, NB - 2 + i)

            @block.vector
            def _(dve):
                coming_in.stats(dve, 0)
                for b in range(2):
                    coming_in.scale(dve, b)
                    coming_in.split_lo(dve, b)
                coming_in.stats(dve, 1)
                dve.wait_ge(b_hi, 1)
                nc.vector.tensor_tensor(bl, bst, bh, ALU.subtract).then_inc(b_lo, 1)

                def gate(h):
                    step = [0]

                    def link(do):
                        for i in range(2):
                            if step[0]:
                                dve.wait_ge(chain, h * (2 * CHAIN) + (2 * (step[0] - 1) + i + 1))
                            do(i, bufs[i]).then_inc(chain, 1)
                        step[0] += 1

                    vec = nc.vector
                    for i in range(2):
                        u = G.use(i, h, 2)
                        dve.wait_ge(u.full, u.n)
                        vec.tensor_copy(bufs[i]["hg"][:, 0:n_ag], u.tile[:, 0:n_ag]).then_inc(u.free, 1)
                    for i in range(2):
                        u = G.use(i, h, 2)
                        dve.wait_ge(u.free, u.done)
                    link(lambda i, t: vec.tensor_reduce(col(i, 0), t["hg"][:, P:P + NE], AX, ALU.max, negate=True))
                    dve.wait_ge(expo, h * 2 + 2)
                    link(lambda i, t: vec.tensor_scalar(col(i, 2), col(i, 2), 8.0, 8.0, ALU.mult, ALU.add))
                    link(lambda i, t: vec.reciprocal(col(i, 2), col(i, 2)))
                    link(lambda i, t: vec.reciprocal(col(i, 3), col(i, 1)))
                    link(lambda i, t: vec.tensor_scalar(t["w"], t["e"], col(i, 3), col(i, 2), ALU.mult, ALU.subtract))
                    link(lambda i, t: vec.tensor_scalar(t["w2"], t["w"], 0.0, None, ALU.max, ALU.add,
                                                        accum_out=col(i, 4)))
                    link(lambda i, t: vec.tensor_scalar(col(i, 5), col(i, 4), 0.0, None, ALU.is_equal))
                    link(lambda i, t: vec.tensor_tensor(col(i, 4), col(i, 4), col(i, 5), ALU.add))
                    link(lambda i, t: vec.reciprocal(col(i, 4), col(i, 4)))
                    link(lambda i, t: vec.tensor_scalar(t["w2"], t["w2"], col(i, 4), 2.0, ALU.mult, ALU.mult))
                    assert step[0] == CHAIN
                    for i in range(2):
                        t = bufs[i]
                        dve.wait_ge(chain, h * (2 * CHAIN) + (2 * (CHAIN - 1) + i + 1))
                        vec.tensor_tensor(heads(t["hw"], NE), heads(t["hg"][:, 0:P], NE), spread(t["w2"], NE, RANK),
                                          ALU.mult).then_inc(hw_ready, 1)

                def body(h, before, after):
                    if after:
                        coming_in.scale(dve, h * 2 + 2)
                    gate(h)
                    if after:
                        coming_in.split_lo(dve, h * 2 + 2)
                        coming_in.scale(dve, h * 2 + 3)
                    if before:
                        for i in range(2):
                            y = Y.use(i, h - 1, 2)
                            dve.wait_ge(y.free, y.done)
                            going_out.pair_stats(dve, h - 1, i)
                    for i in range(2):
                        t = T.use(i, h, 2)
                        dve.wait_ge(hw_hi, h * 2 + i + 1)
                        nc.vector.tensor_tensor(bufs[i]["lo"], t.tile[:, 0:P], bufs[i]["hi"],
                                                ALU.subtract).then_inc(t.free, 1)
                    if before:
                        going_out.pair_scale(dve, h - 1, 0)
                    if after:
                        coming_in.split_lo(dve, h * 2 + 3)
                    for i in range(2):
                        y = Y.use(i, h, 2)
                        at = bass.ds((h * 2 + i) * D, D)
                        dve.wait_ge(x_b, h * 2 + i + 1)
                        dve.wait_ge(y.full, y.n)
                        nc.vector.tensor_tensor(chip.x[:, at], chip.x[:, at], y.tile[:], ALU.add).then_inc(y.free, 1)
                        if before:
                            going_out.split_lo(dve, h * 2 - 2 + i)
                            if i == 0:
                                going_out.pair_scale(dve, h - 1, 1)

                pairs(nc.vector, body)
                for i in range(2):
                    y = Y.use(NB - 2 + i)
                    dve.wait_ge(y.free, y.done)
                    going_out.pair_stats(dve, NB // 2 - 1, i)
                for i in range(2):
                    going_out.pair_scale(dve, NB // 2 - 1, i)
                    going_out.split_lo(dve, NB - 2 + i)


def last_cross_views(chip):
    q_hi, q_lo, k_hi, k_lo, rest = carve(chip.big, [(CH * NB * P, F16)] * 4 + [(8192, F32)])
    return (q_hi, q_lo), (k_hi, k_lo), rest


def last_cross_projections(chip, q_slot, k_slot, coming):
    nc, io = chip.nc, chip.io
    q, k, rest = last_cross_views(chip)
    bias = rest[:, 0:2 * CH]
    WIDE = NB * P
    todo = [(out, slot, src, first + tile, tile, part)
            for out, slot, src, first in ((k, k_slot, chip.cT, CH), (q, q_slot, chip.hT, 0))
            for tile in range(CH) for part in range(2)]
    with chip.begin():
        A = Ring("A", chip.psum[0:4], chip.sem)
        norm = Norm(chip, chip.sem, Ring("T", chip.psum[4:6], chip.sem))
        got, hi, w_hi = chip.sem("got"), chip.sem("hi"), chip.sem("weight_hi")
        keys = len(todo) // 2
        part_width = MAT // (len(todo) - keys)

        def rows(n):
            if n < keys - 1:
                return [n - 1] if n >= 1 else []
            return range(keys - 2, NB) if n == keys - 1 else []

        with nc.Block() as block:

            @block.sync
            def _(sp):
                sp.dma_start(bias, io["cross_bias"]).then_inc(got, 16)

            @block.gpsimd
            def _(pool):
                A.credit(pool)
                norm.turns.credit(pool)
                norm.root(pool)
                for n in range(len(todo) - keys):
                    at = slice(n * part_width, (n + 1) * part_width)
                    pool.wait_ge(w_hi, n + 1)
                    nc.gpsimd.tensor_tensor(chip.w[1][:, coming, at], chip.stage[:, 0, at], chip.w[0][:, coming, at],
                                            ALU.subtract)

            @block.tensor
            def _(pe):
                for n, (_, slot, src, _, tile, part) in enumerate(todo):
                    a = A.use(n)
                    w = chip.weight(slot)
                    if 2 <= n < keys:
                        norm.turn(pe, n - 2)
                    if n == keys:
                        for b in range(keys - 2, NB):
                            norm.turn(pe, b)
                        for b in range(NB - 2, NB):
                            t = norm.place(b)[0]
                            pe.wait_ge(t.free, t.done)
                    pe.wait_ge(a.free, a.n)

                    def batches(half, c, src=src, part=part):
                        rows = src[half][:].rearrange("p (b c t) -> p b c t", b=NB, c=CH)
                        return rows[:, part * (NB // 2):(part + 1) * (NB // 2), c, :]

                    product(nc, a.tile[:], lambda half, c, w=w, t=tile: w[half][:, c * D + t * P:c * D + (t + 1) * P],
                            batches, CH).then_inc(a.full, 1)

            @block.scalar
            def _(act):
                act.wait_ge(got, 16)
                for n, (out, _, _, b, tile, part) in enumerate(todo):
                    a = A.use(n)
                    at = slice(tile * WIDE + part * D, tile * WIDE + (part + 1) * D)
                    act.wait_ge(a.full, a.n)
                    nc.scalar.activation(out[0][:, at], a.tile[:], ACT.Identity, bias=bias[:, b:b + 1]).then_inc(hi, 1)
                    for row in rows(n):
                        norm.split_hi(act, row)
                    if n >= keys:
                        at = slice((n - keys) * part_width, (n - keys + 1) * part_width)
                        act.wait_ge(chip.staged[0], chip.n_staged[0])
                        nc.scalar.activation(chip.w[0][:, coming, at], chip.stage[:, 0, at], ACT.Copy).then_inc(w_hi, 1)

            @block.vector
            def _(dve):
                norm.stats(dve, 0)
                norm.stats(dve, 1)
                dve.wait_ge(got, 16)
                norm.scale(dve, 0)
                norm.scale(dve, 1)
                for n, (out, _, _, b, tile, part) in enumerate(todo):
                    a = A.use(n)
                    at = slice(tile * WIDE + part * D, tile * WIDE + (part + 1) * D)
                    dve.wait_ge(hi, n + 1)
                    nc.vector.scalar_tensor_tensor(out=out[1][:, at], in0=a.tile[:], scalar=bias[:, b:b + 1],
                                                   in1=out[0][:, at], op0=ALU.add, op1=ALU.subtract).then_inc(a.free, 1)
                    for row in rows(n):
                        norm.split_lo(dve, row)
                        if row + 2 < NB:
                            norm.scale(dve, row + 2)


def last_cross_attention(chip):
    nc, io = chip.nc, chip.io
    q, k, rest = last_cross_views(chip)
    WIDE = NB * P
    cst, ch, cl = carve(rest, [(2 * D, F32), (2 * D, F16), (2 * D, F16)])
    prob, ph, pl, nmax, nm, rs, ri = carve(chip.small, [
        (2 * P, F32), (2 * P, F16), (2 * P, F16), (2, F32), (2, F32), (2, F32), (2, F32)])
    scale = float(np.float32(1.0) / np.sqrt(np.float32(D)))
    with chip.begin():
        sem = chip.sem
        S = Ring("S", chip.psum[0:2], sem)
        T = Ring("T", chip.psum[2:4], sem)
        Y = Ring("Y", chip.psum[4:6], sem)
        C = Ring("C", [cst[:, i * D:(i + 1) * D] for i in range(2)], sem)
        c_hi, c_lo, maxed, scaled, prob_ready, p_hi, inv = (
            sem(n) for n in ("ctx_hi", "ctx_lo", "maxed", "scaled", "prob_ready", "p_hi", "inv"))
        with nc.Block() as block:

            @block.sync
            def _(sp):
                with nc.sync.Fori(0, NB // 2) as h:
                    for i in range(2):
                        c = C.use(i, h, 2)
                        sp.wait_ge(c.free, c.n)
                        sp.dma_start(c.tile, io["ctx"][bass.ds(h * 2 + i, 1), :, :].rearrange("o p n -> p (o n)")
                                     ).then_inc(c.full, 16)

            @block.gpsimd
            def _(pool):
                for ring in (S, T, Y, C):
                    ring.credit(pool)
                with nc.gpsimd.Fori(0, NB // 2) as h:
                    for i in range(2):
                        c = C.use(i, h, 2)
                        at = slice(i * D, (i + 1) * D)
                        pool.wait_ge(c_hi, h * 2 + i + 1)
                        nc.gpsimd.tensor_tensor(cl[:, at], c.tile, ch[:, at], ALU.subtract).then_inc(c.free, 1)

            @block.tensor
            def _(pe):
                with nc.tensor.Fori(0, NB // 2) as h:
                    for i in range(2):
                        s = S.use(i, h, 2)
                        pe.wait_ge(s.free, s.n)
                        b = h * 2 + i
                        product(nc, s.tile[:, 0:P], lambda half, c, b=b: q[half][:, bass.ds(b * P + c * WIDE, P)],
                                lambda half, c, b=b: k[half][:, bass.ds(b * P + c * WIDE, P)], CH).then_inc(s.full, 1)
                    for i in range(2):
                        t = T.use(i, h, 2)
                        pe.wait_ge(prob_ready, h * 2 + i + 1)
                        pe.wait_ge(t.free, t.n)
                        turn(chip, t.tile, prob[:, i * P:(i + 1) * P], 1).then_inc(t.full, 1)
                    for i in range(2):
                        t, y, c = T.use(i, h, 2), Y.use(i, h, 2), C.use(i, h, 2)
                        pe.wait_ge(t.free, t.done)
                        pe.wait_ge(c.free, c.done)
                        pe.wait_ge(y.free, y.n)
                        product(nc, y.tile[:], lambda half, c, i=i: (ph, pl)[half][:, i * P:(i + 1) * P],
                                lambda half, c, i=i: (ch, cl)[half][:, i * D:(i + 1) * D], 1).then_inc(y.full, 1)

            @block.scalar
            def _(act):
                with nc.scalar.Fori(0, NB // 2) as h:
                    for i in range(2):
                        c, y = C.use(i, h, 2), Y.use(i, h, 2)
                        act.wait_ge(c.full, (c.n) * 16)
                        act.wait_ge(y.free, y.n)
                        nc.scalar.activation(ch[:, i * D:(i + 1) * D], c.tile, ACT.Copy).then_inc(c_hi, 1)
                    for i in range(2):
                        s = S.use(i, h, 2)
                        act.wait_ge(scaled, h * 2 + i + 1)
                        nc.scalar.activation(prob[:, i * P:(i + 1) * P], s.tile[:, 0:P], ACT.Exp, bias=nm[:, i:i + 1],
                                             scale=scale, accum_out=rs[:, i:i + 1]).then_inc(prob_ready, 1)
                    for i in range(2):
                        t = T.use(i, h, 2)
                        act.wait_ge(t.full, t.n)
                        nc.scalar.activation(ph[:, i * P:(i + 1) * P], t.tile[:, 0:P], ACT.Copy).then_inc(p_hi, 1)

            @block.vector
            def _(dve):
                with nc.vector.Fori(0, NB // 2) as h:
                    for i in range(2):
                        s = S.use(i, h, 2)
                        dve.wait_ge(s.full, s.n)
                        nc.vector.tensor_reduce(nmax[:, i:i + 1], s.tile[:, 0:P], AX, ALU.max,
                                                negate=True).then_inc(maxed, 1)
                        dve.wait_ge(maxed, h * 2 + i + 1)
                        nc.vector.tensor_scalar(nm[:, i:i + 1], nmax[:, i:i + 1], scale, None, ALU.mult).then_inc(scaled, 1)
                    for i in range(2):
                        s, t = S.use(i, h, 2), T.use(i, h, 2)
                        dve.wait_ge(p_hi, h * 2 + i + 1)
                        nc.vector.tensor_tensor(pl[:, i * P:(i + 1) * P], t.tile[:, 0:P], ph[:, i * P:(i + 1) * P],
                                                ALU.subtract).then_inc(t.free, 1)
                        dve.sem_inc(s.free, 1)
                        nc.vector.reciprocal(ri[:, i:i + 1], rs[:, i:i + 1]).then_inc(inv, 1)
                    for i in range(2):
                        y = Y.use(i, h, 2)
                        at = bass.ds((h * 2 + i) * D, D)
                        dve.wait_ge(inv, h * 2 + i + 1)
                        dve.wait_ge(y.full, y.n)
                        nc.vector.scalar_tensor_tensor(out=chip.x[:, at], in0=y.tile[:], scalar=ri[:, i:i + 1],
                                                       in1=chip.x[:, at], op0=ALU.mult, op1=ALU.add).then_inc(y.free, 1)


def sign_projection(chip, slot):
    nc, io = chip.nc, chip.io
    out, s, t = carve(chip.big, [(NB * D, F32), (4, F32), (4, F32)])
    with chip.begin():
        sem = chip.sem
        A = Ring("A", chip.psum[2:4], sem)
        T = Ring("T", chip.psum[0:2], sem)
        norm = Norm(chip, sem, T)
        got, steps, soft, written = (sem(n) for n in ("got", "steps", "softplus", "written"))
        with nc.Block() as block:

            @block.sync
            def _(sp):
                sp.dma_start(s[:, 0:2], io["vectors"][V_SCALE:V_SCALE + 1, 0:2].partition_broadcast(P)).then_inc(got, 16)
                for b in range(NB):
                    a = A.use(b)
                    sp.wait_ge(a.free, a.done)
                    at = slice(b * D, (b + 1) * D)
                    sp.dma_start(io["out"][:, at], out[:, at]).then_inc(written, 16)
                sp.wait_ge(written, 16 * NB)

            @block.gpsimd
            def _(pool):
                A.credit(pool)
                T.credit(pool)
                norm.root(pool)

            @block.tensor
            def _(pe):
                norm.turn(pe, 0)
                for b in range(NB):
                    if b + 1 < NB:
                        norm.turn(pe, b + 1)
                    t_, a = norm.place(b)[0], A.use(b)
                    pe.wait_ge(t_.free, t_.done)
                    pe.wait_ge(a.free, a.n)
                    product(nc, a.tile[:], tokens(chip.hT, b), columns(chip.weight(slot)), CH).then_inc(a.full, 1)

            @block.scalar
            def _(act):
                act.wait_ge(got, 16)
                nc.scalar.activation(t[:, 0:1], s[:, 0:1], ACT.Abs).then_inc(steps, 1)
                act.wait_ge(steps, 1)
                nc.scalar.activation(t[:, 1:2], t[:, 0:1], ACT.Exp, scale=-1.0).then_inc(steps, 1)
                act.wait_ge(steps, 2)
                nc.scalar.activation(t[:, 2:3], t[:, 1:2], ACT.Ln, bias=1.0).then_inc(steps, 1)
                for b in range(NB):
                    norm.split_hi(act, b)

            @block.vector
            def _(dve):
                norm.stats(dve, 0)
                dve.wait_ge(steps, 3)
                nc.vector.tensor_scalar(s[:, 2:3], s[:, 0:1], 0.0, t[:, 2:3], ALU.max, ALU.add).then_inc(soft, 1)
                dve.wait_ge(soft, 1)
                norm.scale(dve, 0)
                for b in range(NB + 1):
                    if b + 1 < NB:
                        norm.scale(dve, b + 1)
                    if b < NB:
                        norm.split_lo(dve, b)
                    if b == 0:
                        norm.stats(dve, 1)
                    if b > 0:
                        a = A.use(b - 1)
                        at = slice((b - 1) * D, b * D)
                        dve.wait_ge(a.full, a.n)
                        nc.vector.scalar_tensor_tensor(out=out[:, at], in0=a.tile[:], scalar=s[:, 2:3],
                                                       in1=chip.x[:, at], op0=ALU.mult, op1=ALU.add).then_inc(a.free, 1)


def decoder(nc, io):
    with ExitStack() as ctx:
        chip = Chip(nc, ctx, io)
        begin_layer(chip, [(W_QKVO + i, i) for i in range(4)], [W_XK, W_XK + 1], start=True)
        self_attention(chip, 0, {"q": 0, "k": 1, "v": 2, "o": 3}, 4, [W_XV, W_XV + 1])
        cross_keys(chip, (4, 5), (0, 1), 2, [W_XQO, W_XQO + 1], [W_XQO + 2, W_XQO + 3])
        cross_attention(chip, (2, 3), (4, 5))
        experts(chip, 2, 3, 0, [W_L1O, W_LXQ])
        self_attention(chip, 1, {"q": 0, "k": 1, "v": 1, "o": 4}, 2, [W_SIGN], late=W_LXK)
        last_cross_projections(chip, 3, 2, 5)
        last_cross_attention(chip)
        sign_projection(chip, 5)


def alibi_table():
    slopes = (1.0 / np.power(2.0, np.arange(1, NH + 1, dtype=np.float32) * (8.0 / NH))).astype(np.float32)
    pos = np.arange(P)
    rel = (pos[None, :] - pos[:, None]).astype(np.float32)
    table = np.empty((P, NG, GH, P), np.float32)
    for g in range(NG):
        for i in range(GH):
            head = ((g // 4) * 4 + i) * 4 + g % 4
            table[:, g, i, :] = np.where(rel <= 0, slopes[head] * rel, np.float32(-1e30))
    return table.reshape(P, NG * GH * P)


def kernel(x, ctx_4096, mask_1x1xSxS2_ff0, L0_attn_Wqkv, L0_attn_q_ln_w, L0_attn_q_ln_b, L0_attn_k_ln_w,
           L0_attn_k_ln_b, L0_attn_Wout, L0_xattn_q_proj_w, L0_xattn_k_proj_w, L0_xattn_v_proj_w, L0_xattn_o_proj_w,
           L0_xattn_q_norm_w, L0_xattn_k_norm_w, L0_ffn_W_base, L0_ffn_b_base, L0_ffn_W_gate, L0_ffn_W_thr,
           L0_ffn_b_thr, L0_ffn_A_w, L0_ffn_B_w, L1_attn_Wq, L1_attn_Wk, L1_attn_Wv, L1_attn_Wo, L1_xattn_Wq,
           L1_xattn_bq, L1_xattn_Wk, L1_xattn_bk, L1_ffn_sign, L1_ffn_scale):
    import concourse.bacc as bacc
    from concourse.bass_utils import run_bass_kernel_spmd

    f32 = np.float32

    def matrix(w_t):
        full = np.zeros((D, D), f32)
        full[:, :w_t.shape[1]] = w_t
        return full.reshape(CH, P, D).transpose(1, 0, 2).reshape(P, MAT)

    a = {n: np.asarray(v) for n, v in locals().items()
         if n not in ("f32", "matrix", "bacc", "run_bass_kernel_spmd")}
    weights = np.empty((N_MATS, P, MAT), f32)
    qkv = a["L0_attn_Wqkv"]
    for i in range(3):
        weights[W_QKVO + i] = matrix(qkv[i * D:(i + 1) * D].T)
    weights[W_QKVO + 3] = matrix(a["L0_attn_Wout"].T)
    for i in range(2):
        weights[W_XK + i] = matrix(a["L0_xattn_k_proj_w"][i * D:(i + 1) * D].T)
        weights[W_XV + i] = matrix(a["L0_xattn_v_proj_w"][i * D:(i + 1) * D].T)
    for g in range(NKV):
        weights[W_XQO + 2 * g] = matrix(a["L0_xattn_q_proj_w"][g * D:(g + 1) * D].T)
        weights[W_XQO + 2 * g + 1] = matrix(a["L0_xattn_o_proj_w"][:, g * D:(g + 1) * D].T)
    weights[W_L1Q] = matrix(a["L1_attn_Wq"].T)
    weights[W_L1KV] = matrix(np.concatenate([a["L1_attn_Wk"], a["L1_attn_Wv"]]).T)
    weights[W_BASE] = matrix(a["L0_ffn_W_base"].T)
    weights[W_AG] = matrix(np.concatenate([a["L0_ffn_A_w"].reshape(NE * RANK, D), a["L0_ffn_W_gate"],
                                           a["L0_ffn_W_thr"][None]]).T)
    weights[W_L1O] = matrix(a["L1_attn_Wo"].T)
    weights[W_LXQ] = matrix(a["L1_xattn_Wq"].T)
    weights[W_LXK] = matrix(a["L1_xattn_Wk"].T)
    weights[W_SIGN] = matrix(a["L1_ffn_sign"])

    vectors = np.zeros((9, D), f32)
    for row, name in ((V_QW, "L0_attn_q_ln_w"), (V_QB, "L0_attn_q_ln_b"), (V_KW, "L0_attn_k_ln_w"),
                      (V_KB, "L0_attn_k_ln_b"), (V_XQN, "L0_xattn_q_norm_w"), (V_XKN, "L0_xattn_k_norm_w"),
                      (V_BASE, "L0_ffn_b_base"), (V_BTHR, "L0_ffn_b_thr"), (V_SCALE, "L1_ffn_scale")):
        flat = a[name].reshape(-1)
        vectors[row, :flat.size] = flat

    late = np.arange(P) % 32 >= HD
    arrays = {
        "x": a["x"].transpose(1, 0, 2).reshape(P, NB * D),
        "ctxT": a["ctx_4096"].reshape(NB, P, CH, P).transpose(3, 0, 2, 1).reshape(P, NB * D),
        "ctx": a["ctx_4096"],
        "mask": a["mask_1x1xSxS2_ff0"].reshape(P, P),
        "weights": weights,
        "expert_b": a["L0_ffn_B_w"].transpose(0, 2, 1).reshape(P, D),
        "vectors": vectors,
        "cross_bias": np.concatenate([a["L1_xattn_bq"].reshape(CH, P), a["L1_xattn_bk"].reshape(CH, P)]).T,
        "ident": np.eye(P, dtype=f32),
        "half": np.stack([np.where(late, -1, 0), np.where(late, 0, -1)], 1).astype(f32),
        "alibi": alibi_table(),
    }
    nc = bacc.Bacc("TRN2", target_bir_lowering=False, num_devices=1)
    io = {}
    for name, v in arrays.items():
        arrays[name] = np.ascontiguousarray(v)
        io[name] = nc.dram_tensor(f"in_{name}", v.shape, mybir.dt.from_np(v.dtype), kind="ExternalInput").ap()
    io["out"] = nc.dram_tensor("out", (P, NB * D), F32, kind="ExternalOutput").ap()
    decoder(nc, io)
    result = run_bass_kernel_spmd(nc, [{f"in_{name}": v for name, v in arrays.items()}], core_ids=[0])
    return result.results[0]["out"].reshape(P, NB, D).transpose(1, 0, 2)
```
